# Optimizing a Trainium2 kernel written in Bass

```python
import numpy as np
import jax
import jax.numpy as jnp

def _softmax(x, axis=-1):
    return jax.nn.softmax(x, axis=axis)

def _gelu(x):
    return jax.nn.gelu(x, approximate=True)

def _silu(x):
    return jax.nn.silu(x)

def _sigmoid(x):
    return jax.nn.sigmoid(x)

def _layernorm(x, axis=-1, eps=1e-05):
    m = jnp.mean(x, axis=axis, keepdims=True)
    v = jnp.var(x, axis=axis, keepdims=True)
    return (x - m) / jnp.sqrt(v + eps)

def _scatter_add(tgt, idx, src, axis=0):
    return tgt.at[idx].add(src)

def _segment_sum(src, seg, n):
    return jax.ops.segment_sum(src, seg, n)
kernel_name = 'mk_seq_postln_d2_jaxref_r8_4c3368'

def setup_inputs(seed: int=0):
    np.random.seed(seed)
    _w = jnp.asarray

    def _L0_attn_setup():
        import jax, jax.numpy as jnp
        import numpy as np
        DIM = 128
        NUM_HEADS = 16
        NUM_GROUPS = 8

        def grouped_linear(x, w, b):
            B, N, Cin = x.shape
            G = w.shape[0]
            xg = x.reshape(B, N, G, Cin // G)
            out = jnp.einsum('bngi,gio->bngo', xg, w)
            out = out.reshape(B, N, -1)
            if b is not None:
                out = out + b
            return out
        key = jax.random.key(seed)
        k1, k2, k3, k4 = jax.random.split(key, 4)
        G = NUM_GROUPS
        x = jax.random.normal(k1, (2, 256, DIM), dtype=jnp.float32)
        w_qkv = jax.random.normal(k2, (G, DIM // G, 3 * DIM // G), dtype=jnp.float32) * (DIM // G) ** (-0.5)
        w_proj = jax.random.normal(k3, (G, DIM // G, DIM // G), dtype=jnp.float32) * (DIM // G) ** (-0.5)
        b_proj = jax.random.normal(k4, (DIM,), dtype=jnp.float32) * 0.02
        return {'x': x, 'w_qkv': w_qkv, 'w_proj': w_proj, 'b_proj': b_proj}
    _L0_attn_in = _L0_attn_setup()

    def _L0_ffn_setup():
        import jax, jax.numpy as jnp
        import numpy as np
        N_EMBD = 128
        NUM_EXPERTS = 8
        TOP_K = 2
        D_FF = 4 * N_EMBD
        B, S = (4, 256)
        key = jax.random.key(seed)
        ks = jax.random.split(key, 7)
        scale = lambda fan_in: 1.0 / np.sqrt(fan_in)
        x = jax.random.normal(ks[0], (B, S, N_EMBD), dtype=jnp.float32)
        W_router = jax.random.normal(ks[1], (N_EMBD, NUM_EXPERTS), dtype=jnp.float32) * scale(N_EMBD)
        b_router = jnp.zeros((NUM_EXPERTS,), dtype=jnp.float32)
        W1 = jax.random.normal(ks[2], (NUM_EXPERTS, N_EMBD, D_FF), dtype=jnp.float32) * scale(N_EMBD)
        b1 = jnp.zeros((NUM_EXPERTS, D_FF), dtype=jnp.float32)
        W2 = jax.random.normal(ks[3], (NUM_EXPERTS, D_FF, N_EMBD), dtype=jnp.float32) * scale(D_FF)
        b2 = jnpp = jnp.zeros((NUM_EXPERTS, N_EMBD), dtype=jnp.float32)
        return {'x': x, 'W_router': W_router, 'b_router': b_router, 'W1': W1, 'b1': b1, 'W2': W2, 'b2': b2}
    _L0_ffn_in = _L0_ffn_setup()

    def _L1_attn_setup():
        import jax, jax.numpy as jnp
        import numpy as np
        EPS = 1e-05
        B, T, D, H = (4, 512, 128, 512)

        def rmsnorm(x, w):
            rms = jnp.sqrt(jnp.mean(x * x, axis=-1, keepdims=True) + EPS)
            return x / rms * w

        def diag_ssm(x, a, b, out_w, out_b):
            at = jnp.tanh(a)
            bx = x * b

            def step(prev, xt):
                nxt = at * prev + xt
                return (nxt, nxt)
            prev0 = jnp.zeros((x.shape[0], x.shape[-1]), x.dtype)
            _, y = jax.lax.scan(step, prev0, jnp.swapaxes(bx, 0, 1))
            y = jnp.swapaxes(y, 0, 1)
            return jnp.einsum('btd,ed->bte', y, out_w) + out_b

        def gated_mlp(x, w1_w, w1_b, w2_w, w2_b, w3_w, w3_b):
            g = jax.nn.silu(jnp.einsum('btd,hd->bth', x, w2_w) + w2_b)
            u = jnp.einsum('btd,hd->bth', x, w1_w) + w1_b
            return jnp.einsum('bth,dh->btd', g * u, w3_w) + w3_b
        key = jax.random.key(seed)
        ks = jax.random.split(key, 12)
        s = lambda k, shape, scale: jax.random.normal(k, shape, dtype=jnp.float32) * scale
        return {'x': s(ks[0], (B, T, D), 1.0), 'a': s(ks[1], (D,), 1.0), 'b': jnp.ones((D,), jnp.float32), 'out_w': s(ks[2], (D, D), 1.0 / np.sqrt(D)), 'out_b': jnp.zeros((D,), jnp.float32), 'n1_w': jnp.ones((D,), jnp.float32), 'n2_w': jnp.ones((D,), jnp.float32), 'w1_w': s(ks[3], (H, D), 1.0 / np.sqrt(D)), 'w1_b': jnp.zeros((H,), jnp.float32), 'w2_w': s(ks[4], (H, D), 1.0 / np.sqrt(D)), 'w2_b': jnp.zeros((H,), jnp.float32), 'w3_w': s(ks[5], (D, H), 1.0 / np.sqrt(H)), 'w3_b': jnp.zeros((D,), jnp.float32)}
    _L1_attn_in = _L1_attn_setup()

    def _L1_ffn_setup():
        import jax, jax.numpy as jnp
        import numpy as np
        DIM = 128
        DEPTH = 2
        HEADS = 8
        DIM_HEAD = 64
        WINDOW = 64
        INNER = HEADS * DIM_HEAD
        HID = int(DIM * 4 * 2 / 3)
        B, N = (2, 1024)
        QK_SCALE = 8.0

        def shift_token(t):
            t1, t2 = jnp.split(t, 2, axis=-1)
            t2 = jnp.pad(t2, ((0, 0), (1, 0), (0, 0)))[:, :-1]
            return jnp.concatenate([t1, t2], axis=-1)

        def l2norm(t):
            return t / jnp.clip(jnp.linalg.norm(t, axis=-1, keepdims=True), 1e-12)

        def rotate_half(x):
            x1, x2 = jnp.split(x, 2, axis=-1)
            return jnp.concatenate([-x2, x1], axis=-1)

        def rotary_xpos(q, k):
            n = q.shape[-2]
            half_idx = jnp.arange(0, DIM_HEAD, 2, dtype=jnp.float32)
            inv_freq = 1.0 / 10000.0 ** (half_idx / DIM_HEAD)
            t = jnp.arange(n, dtype=jnp.float32)
            freqs = t[:, None] * inv_freq[None, :]
            freqs = jnp.concatenate([freqs, freqs], axis=-1)
            base = (half_idx + 0.4 * DIM_HEAD) / (1.4 * DIM_HEAD)
            power = (t - n // 2) / float(WINDOW // 2)
            scale = base[None, :] ** power[:, None]
            scale = jnp.concatenate([scale, scale], axis=-1)
            cos, sin = (jnp.cos(freqs), jnp.sin(freqs))
            q = q * cos * scale + rotate_half(q) * sin * scale
            k = k * cos / scale + rotate_half(k) * sin / scale
            return (q, k)

        def local_attention(q, k, v):
            b, h, n, d = q.shape
            w = n // WINDOW
            bq = q.reshape(b, h, w, WINDOW, d) * QK_SCALE
            bk = k.reshape(b, h, w, WINDOW, d)
            bv = v.reshape(b, h, w, WINDOW, d)

            def look_around(t):
                p = jnp.pad(t, ((0, 0), (0, 0), (1, 0), (0, 0), (0, 0)))
                return jnp.concatenate([p[:, :, :w], p[:, :, 1:]], axis=3)
            bk, bv = (look_around(bk), look_around(bv))
            bt = jnp.arange(n).reshape(w, WINDOW)
            btp = jnp.pad(bt, ((1, 0), (0, 0)), constant_values=-1)
            btk = jnp.concatenate([btp[:w], btp[1:]], axis=1)
            sim = jnp.einsum('bhwid,bhwjd->bhwij', bq, bk)
            i = bt[:, :, None]
            j = btk[:, None, :]
            mask = (i < j) | (i > j + WINDOW) | (j == -1)
            sim = jnp.where(mask, -jnp.finfo(sim.dtype).max, sim)
            attn = jax.nn.softmax(sim, axis=-1)
            out = jnp.einsum('bhwij,bhwjd->bhwid', attn, bv)
            return out.reshape(b, h, n, d)

        def _layer(x, wqkv, qs, ksc, wo, lg, lb, w1, b1, w2, b2):
            b, n, _ = x.shape
            h = shift_token(x)
            qkv = h @ wqkv
            q, k, v = jnp.split(qkv, 3, axis=-1)
            to_heads = lambda t: t.reshape(b, n, HEADS, DIM_HEAD).transpose(0, 2, 1, 3)
            q, k, v = (to_heads(q), to_heads(k), to_heads(v))
            q = l2norm(q) * qs
            k = l2norm(k) * ksc
            q, k = rotary_xpos(q, k)
            o = local_attention(q, k, v)
            o = o.transpose(0, 2, 1, 3).reshape(b, n, INNER)
            x = x + o @ wo
            h = shift_token(x)
            mu = h.mean(-1, keepdims=True)
            var = h.var(-1, keepdims=True)
            h = (h - mu) / jnp.sqrt(var + 1e-05) * lg + lb
            h = h @ w1 + b1
            a, g = jnp.split(h, 2, axis=-1)
            h = a * jax.nn.gelu(g, approximate=False)
            x = x + h @ w2 + b2
            return x
        key = jax.random.key(seed)
        ks = jax.random.split(key, 6)
        return {'x': jax.random.normal(ks[0], (B, N, DIM), jnp.float32), 'wqkv': jax.random.normal(ks[1], (DEPTH, DIM, 3 * INNER), jnp.float32) * 0.02, 'q_scale': jnp.ones((DEPTH, DIM_HEAD), jnp.float32), 'k_scale': jnp.ones((DEPTH, DIM_HEAD), jnp.float32), 'wo': jax.random.normal(ks[2], (DEPTH, INNER, DIM), jnp.float32) * 0.02, 'ln_g': jnp.ones((DEPTH, DIM), jnp.float32), 'ln_b': jnp.zeros((DEPTH, DIM), jnp.float32), 'w1': jax.random.normal(ks[3], (DEPTH, DIM, 2 * HID), jnp.float32) * 0.02, 'b1': jnp.zeros((DEPTH, 2 * HID), jnp.float32), 'w2': jax.random.normal(ks[4], (DEPTH, HID, DIM), jnp.float32) * 0.02, 'b2': jnp.zeros((DEPTH, DIM), jnp.float32)}
    _L1_ffn_in = _L1_ffn_setup()
    _d = {'L0_attn_x': _L0_attn_in['x'], 'L0_attn_w_qkv': _L0_attn_in['w_qkv'], 'L0_attn_w_proj': _L0_attn_in['w_proj'], 'L0_attn_b_proj': _L0_attn_in['b_proj'], 'L0_ffn_W_router': _L0_ffn_in['W_router'], 'L0_ffn_b_router': _L0_ffn_in['b_router'], 'L0_ffn_W1': _L0_ffn_in['W1'], 'L0_ffn_b1': _L0_ffn_in['b1'], 'L0_ffn_W2': _L0_ffn_in['W2'], 'L0_ffn_b2': _L0_ffn_in['b2'], 'L1_attn_a': _L1_attn_in['a'], 'L1_attn_b': _L1_attn_in['b'], 'L1_attn_out_w': _L1_attn_in['out_w'], 'L1_attn_out_b': _L1_attn_in['out_b'], 'L1_attn_n1_w': _L1_attn_in['n1_w'], 'L1_attn_n2_w': _L1_attn_in['n2_w'], 'L1_attn_w1_w': _L1_attn_in['w1_w'], 'L1_attn_w1_b': _L1_attn_in['w1_b'], 'L1_attn_w2_w': _L1_attn_in['w2_w'], 'L1_attn_w2_b': _L1_attn_in['w2_b'], 'L1_attn_w3_w': _L1_attn_in['w3_w'], 'L1_attn_w3_b': _L1_attn_in['w3_b'], 'L1_ffn_wqkv': _L1_ffn_in['wqkv'], 'L1_ffn_q_scale': _L1_ffn_in['q_scale'], 'L1_ffn_k_scale': _L1_ffn_in['k_scale'], 'L1_ffn_wo': _L1_ffn_in['wo'], 'L1_ffn_ln_g': _L1_ffn_in['ln_g'], 'L1_ffn_ln_b': _L1_ffn_in['ln_b'], 'L1_ffn_w1': _L1_ffn_in['w1'], 'L1_ffn_b1': _L1_ffn_in['b1'], 'L1_ffn_w2': _L1_ffn_in['w2'], 'L1_ffn_b2': _L1_ffn_in['b2']}
    _x0 = _d['L0_attn_x']
    _d['L0_attn_x'] = jax.random.normal(jax.random.fold_in(jax.random.key(seed), 1), (4, 1024, 128), dtype=_x0.dtype)
    del _x0
    return _d

def reference(L0_attn_x, L0_attn_w_qkv, L0_attn_w_proj, L0_attn_b_proj, L0_ffn_W_router, L0_ffn_b_router, L0_ffn_W1, L0_ffn_b1, L0_ffn_W2, L0_ffn_b2, L1_attn_a, L1_attn_b, L1_attn_out_w, L1_attn_out_b, L1_attn_n1_w, L1_attn_n2_w, L1_attn_w1_w, L1_attn_w1_b, L1_attn_w2_w, L1_attn_w2_b, L1_attn_w3_w, L1_attn_w3_b, L1_ffn_wqkv, L1_ffn_q_scale, L1_ffn_k_scale, L1_ffn_wo, L1_ffn_ln_g, L1_ffn_ln_b, L1_ffn_w1, L1_ffn_b1, L1_ffn_w2, L1_ffn_b2):

    def _L0_attn_ref(x, w_qkv, w_proj, b_proj):
        import jax, jax.numpy as jnp
        import numpy as np
        DIM = 128
        NUM_HEADS = 16
        NUM_GROUPS = 8

        def grouped_linear(x, w, b):
            B, N, Cin = x.shape
            G = w.shape[0]
            xg = x.reshape(B, N, G, Cin // G)
            out = jnp.einsum('bngi,gio->bngo', xg, w)
            out = out.reshape(B, N, -1)
            if b is not None:
                out = out + b
            return out
        B, N, C = x.shape
        H = NUM_HEADS
        D = C // H
        scale = D ** (-0.5)
        qkv = grouped_linear(x, w_qkv, None)
        qkv = qkv.reshape(B, N, 3, H, D)
        qkv = jnp.transpose(qkv, (2, 0, 3, 1, 4))
        q, k, v = (qkv[0] * scale, qkv[1], qkv[2])
        attn = jnp.einsum('bhnd,bhmd->bhnm', q, k)
        attn = jax.nn.softmax(attn, axis=-1)
        out = jnp.einsum('bhnm,bhmd->bhnd', attn, v)
        out = jnp.transpose(out, (0, 2, 1, 3)).reshape(B, N, C)
        out = grouped_linear(out, w_proj, b_proj)
        return out

    def _L0_ffn_ref(x, W_router, b_router, W1, b1, W2, b2):
        import jax, jax.numpy as jnp
        import numpy as np
        N_EMBD = 128
        NUM_EXPERTS = 8
        TOP_K = 2
        D_FF = 4 * N_EMBD
        B, S = (4, 256)
        Bv, Sv, D = x.shape
        flat_x = x.reshape(-1, D)
        T = flat_x.shape[0]
        logits = flat_x @ W_router + b_router
        top_vals, top_idx = jax.lax.top_k(logits, TOP_K)
        neg_inf = jnp.full_like(logits, -jnp.inf)
        sparse_logits = neg_inf.at[jnp.arange(T)[:, None], top_idx].set(top_vals)
        router_weights = jax.nn.softmax(sparse_logits, axis=-1)
        final_output = jnp.zeros_like(flat_x)
        for e in range(NUM_EXPERTS):
            expert_mask = jnp.any(top_idx == e, axis=-1)
            h = jax.nn.relu(flat_x @ W1[e] + b1[e])
            y = h @ W2[e] + b2[e]
            w = router_weights[:, e] * expert_mask.astype(x.dtype)
            final_output = final_output + y * w[:, None]
        return final_output.reshape(Bv, Sv, D)

    def _L1_attn_ref(x, a, b, out_w, out_b, n1_w, n2_w, w1_w, w1_b, w2_w, w2_b, w3_w, w3_b):
        import jax, jax.numpy as jnp
        import numpy as np
        EPS = 1e-05
        B, T, D, H = (4, 512, 128, 512)

        def rmsnorm(x, w):
            rms = jnp.sqrt(jnp.mean(x * x, axis=-1, keepdims=True) + EPS)
            return x / rms * w

        def diag_ssm(x, a, b, out_w, out_b):
            at = jnp.tanh(a)
            bx = x * b

            def step(prev, xt):
                nxt = at * prev + xt
                return (nxt, nxt)
            prev0 = jnp.zeros((x.shape[0], x.shape[-1]), x.dtype)
            _, y = jax.lax.scan(step, prev0, jnp.swapaxes(bx, 0, 1))
            y = jnp.swapaxes(y, 0, 1)
            return jnp.einsum('btd,ed->bte', y, out_w) + out_b

        def gated_mlp(x, w1_w, w1_b, w2_w, w2_b, w3_w, w3_b):
            g = jax.nn.silu(jnp.einsum('btd,hd->bth', x, w2_w) + w2_b)
            u = jnp.einsum('btd,hd->bth', x, w1_w) + w1_b
            return jnp.einsum('bth,dh->btd', g * u, w3_w) + w3_b
        x = x + diag_ssm(rmsnorm(x, n1_w), a, b, out_w, out_b)
        x = x + gated_mlp(rmsnorm(x, n2_w), w1_w, w1_b, w2_w, w2_b, w3_w, w3_b)
        return x

    def _L1_ffn_ref(x, wqkv, q_scale, k_scale, wo, ln_g, ln_b, w1, b1, w2, b2):
        import jax, jax.numpy as jnp
        import numpy as np
        DIM = 128
        DEPTH = 2
        HEADS = 8
        DIM_HEAD = 64
        WINDOW = 64
        INNER = HEADS * DIM_HEAD
        HID = int(DIM * 4 * 2 / 3)
        B, N = (2, 1024)
        QK_SCALE = 8.0

        def shift_token(t):
            t1, t2 = jnp.split(t, 2, axis=-1)
            t2 = jnp.pad(t2, ((0, 0), (1, 0), (0, 0)))[:, :-1]
            return jnp.concatenate([t1, t2], axis=-1)

        def l2norm(t):
            return t / jnp.clip(jnp.linalg.norm(t, axis=-1, keepdims=True), 1e-12)

        def rotate_half(x):
            x1, x2 = jnp.split(x, 2, axis=-1)
            return jnp.concatenate([-x2, x1], axis=-1)

        def rotary_xpos(q, k):
            n = q.shape[-2]
            half_idx = jnp.arange(0, DIM_HEAD, 2, dtype=jnp.float32)
            inv_freq = 1.0 / 10000.0 ** (half_idx / DIM_HEAD)
            t = jnp.arange(n, dtype=jnp.float32)
            freqs = t[:, None] * inv_freq[None, :]
            freqs = jnp.concatenate([freqs, freqs], axis=-1)
            base = (half_idx + 0.4 * DIM_HEAD) / (1.4 * DIM_HEAD)
            power = (t - n // 2) / float(WINDOW // 2)
            scale = base[None, :] ** power[:, None]
            scale = jnp.concatenate([scale, scale], axis=-1)
            cos, sin = (jnp.cos(freqs), jnp.sin(freqs))
            q = q * cos * scale + rotate_half(q) * sin * scale
            k = k * cos / scale + rotate_half(k) * sin / scale
            return (q, k)

        def local_attention(q, k, v):
            b, h, n, d = q.shape
            w = n // WINDOW
            bq = q.reshape(b, h, w, WINDOW, d) * QK_SCALE
            bk = k.reshape(b, h, w, WINDOW, d)
            bv = v.reshape(b, h, w, WINDOW, d)

            def look_around(t):
                p = jnp.pad(t, ((0, 0), (0, 0), (1, 0), (0, 0), (0, 0)))
                return jnp.concatenate([p[:, :, :w], p[:, :, 1:]], axis=3)
            bk, bv = (look_around(bk), look_around(bv))
            bt = jnp.arange(n).reshape(w, WINDOW)
            btp = jnp.pad(bt, ((1, 0), (0, 0)), constant_values=-1)
            btk = jnp.concatenate([btp[:w], btp[1:]], axis=1)
            sim = jnp.einsum('bhwid,bhwjd->bhwij', bq, bk)
            i = bt[:, :, None]
            j = btk[:, None, :]
            mask = (i < j) | (i > j + WINDOW) | (j == -1)
            sim = jnp.where(mask, -jnp.finfo(sim.dtype).max, sim)
            attn = jax.nn.softmax(sim, axis=-1)
            out = jnp.einsum('bhwij,bhwjd->bhwid', attn, bv)
            return out.reshape(b, h, n, d)

        def _layer(x, wqkv, qs, ksc, wo, lg, lb, w1, b1, w2, b2):
            b, n, _ = x.shape
            h = shift_token(x)
            qkv = h @ wqkv
            q, k, v = jnp.split(qkv, 3, axis=-1)
            to_heads = lambda t: t.reshape(b, n, HEADS, DIM_HEAD).transpose(0, 2, 1, 3)
            q, k, v = (to_heads(q), to_heads(k), to_heads(v))
            q = l2norm(q) * qs
            k = l2norm(k) * ksc
            q, k = rotary_xpos(q, k)
            o = local_attention(q, k, v)
            o = o.transpose(0, 2, 1, 3).reshape(b, n, INNER)
            x = x + o @ wo
            h = shift_token(x)
            mu = h.mean(-1, keepdims=True)
            var = h.var(-1, keepdims=True)
            h = (h - mu) / jnp.sqrt(var + 1e-05) * lg + lb
            h = h @ w1 + b1
            a, g = jnp.split(h, 2, axis=-1)
            h = a * jax.nn.gelu(g, approximate=False)
            x = x + h @ w2 + b2
            return x
        for l in range(DEPTH):
            x = _layer(x, wqkv[l], q_scale[l], k_scale[l], wo[l], ln_g[l], ln_b[l], w1[l], b1[l], w2[l], b2[l])
        return x
    x = L0_attn_x
    x = _layernorm(x + _L0_attn_ref(x, L0_attn_w_qkv, L0_attn_w_proj, L0_attn_b_proj), axis=-1)
    x = _layernorm(x + _L0_ffn_ref(x, L0_ffn_W_router, L0_ffn_b_router, L0_ffn_W1, L0_ffn_b1, L0_ffn_W2, L0_ffn_b2), axis=-1)
    x = _layernorm(x + _L1_attn_ref(x, L1_attn_a, L1_attn_b, L1_attn_out_w, L1_attn_out_b, L1_attn_n1_w, L1_attn_n2_w, L1_attn_w1_w, L1_attn_w1_b, L1_attn_w2_w, L1_attn_w2_b, L1_attn_w3_w, L1_attn_w3_b), axis=-1)
    x = _layernorm(x + _L1_ffn_ref(x, L1_ffn_wqkv, L1_ffn_q_scale, L1_ffn_k_scale, L1_ffn_wo, L1_ffn_ln_g, L1_ffn_ln_b, L1_ffn_w1, L1_ffn_b1, L1_ffn_w2, L1_ffn_b2), axis=-1)
    return x

_drawn_inputs = setup_inputs


def setup_inputs(seed=0):
    import zlib

    import numpy as np

    out = dict(_drawn_inputs(seed))
    spreads = {'L0_ffn_b_router': (0.0, 0.1),
     'L0_ffn_b1': (0.0, 0.1),
     'L0_ffn_b2': (0.0, 0.1),
     'L1_attn_b': (1.0, 0.2),
     'L1_attn_out_b': (0.0, 0.1),
     'L1_attn_n1_w': (1.0, 0.2),
     'L1_attn_n2_w': (1.0, 0.2),
     'L1_attn_w1_b': (0.0, 0.377),
     'L1_attn_w2_b': (0.0, 0.372),
     'L1_attn_w3_b': (0.0, 0.1),
     'L1_ffn_q_scale': (1.0, 0.6),
     'L1_ffn_k_scale': (1.0, 0.6),
     'L1_ffn_ln_g': (1.0, 0.6),
     'L1_ffn_ln_b': (0.0, 0.8),
     'L1_ffn_b1': (0.0, 0.8),
     'L1_ffn_b2': (0.0, 0.645)}
    factors = {'L1_ffn_w1': 6.608, 'L1_ffn_w2': 6.507}
    for name, (base, spread) in spreads.items():
        noise = np.random.default_rng([zlib.crc32(name.encode()), seed]).standard_normal(out[name].shape)
        drawn = base * np.exp(spread * noise) if base else spread * noise
        out[name] = jnp.asarray(drawn.astype(out[name].dtype))
    for name, factor in factors.items():
        out[name] = (out[name] * factor).astype(out[name].dtype)
    return out
```

```python
from contextlib import ExitStack

import numpy as np

import concourse.bass as bass
from concourse import mybir

ALU = mybir.AluOpType
ACT = mybir.ActivationFunctionType
AX = mybir.AxisListType
F32 = mybir.dt.float32
BF16 = mybir.dt.bfloat16
U32 = mybir.dt.uint32

P = 128
B, N, C = 4, 1024, 128
T = B * N
NT = T // P
NS = T // 512
TB = N // P

H0, D0, G0 = 16, 8, 8
HG = 4
NG = B * H0 // HG
TERMS = 9 * D0
ZROWS = 96
SROWS = ZROWS + 3
NBUF = 3

NE, FE = 8, 512
HE = FE // P

HID1 = 512
H1 = HID1 // P

L2, H2, DH, WINDOW = 2, 8, 64, 64
INNER = H2 * DH
PAIRS = H2 // 2
DIMF = 341
HF = -(-DIMF // P)
QK_SCALE = 8.0
MASKED = -1e30
LNS = 2 * NS

EPS = 1e-5




class Chain:

    def __init__(self, eng, sem, settled):
        self.settled = settled
        self.eng, self.sem, self.base, self.n, self.done = eng, sem, 0, 0, 0

    def loop(self, turn, per):
        self.done += self.n
        self.base, self.n, self.per = self.done + turn * per, 0, per

    def close(self, turns):
        assert self.n == self.per, (self.n, self.per)
        self.done += turns * self.per
        self.base, self.n = self.done, 0

    def link(self, ins, settle=False):
        self.n += 1
        ins.then_inc(self.sem, 1)
        self.eng.wait_ge(self.sem, self.base + self.n)
        if settle:
            self.settle()

    def settle(self):
        self.eng.nop().then_inc(self.settled, 1)


def ring_uses(second, first, outputs):
    uses = []
    if second:
        uses += [("next", 32 + i) for i in range(32)]
    rest = [("after", i) for i in range(32)] if first else []
    if second:
        uses += rest[:16] + [("max", 0)] + rest[16:]
    if outputs:
        uses += [("out", 0), ("out", 1)]
    return uses


def network_kernel(nc, d, out):
    ctx = ExitStack()
    with ctx:
        def sem(name):
            return ctx.enter_context(nc.semaphore(name))

        def sems(names):
            return [sem(name) for name in names.split()]

        def sb(name, shape, dt=F32, at=ctx):
            return at.enter_context(nc.sbuf_tensor(name, shape, dt))

        PS = ctx.enter_context(nc.psum_tensor("PS", [P, 8, 512], F32))

        parts_dram = nc.dram_tensor("parts_dram", [2, 3, B * P, N], BF16, kind="Internal").ap()
        max_dram = nc.dram_tensor("max_dram", [NBUF, 3, HG * N], BF16, kind="Internal").ap()

        x_tm = sb("x_tm", [P, NT, C])
        ident = sb("ident", [P, P])
        identb = sb("identb", [P, P], BF16)
        o_all = sb("o_all", [P, NG, 2, HG, HG * D0])
        neghalf = sb("neghalf", [P, 8])
        wq_bd = sb("wq_bd", [P, 3 * C])
        wp_bd = sb("wp_bd", [P, C])
        bp_row = sb("bp_row", [P, C])
        wr = sb("wr", [P, NE])
        br_row = sb("br_row", [P, NE])
        b2s = sb("b2s", [NE, C])
        iota8 = sb("iota8", [P, NE])
        cols1 = sb("cols1", [P, 4])
        a_tanh = sb("a_tanh", [P, 1])
        b1c = sb("b1c", [P, NE * HE])

        at = ExitStack()
        v_all = sb("v_all", [P, NG, TB, HG * D0], at=at)
        vaug = sb("vaug", [P, NBUF, TB, HG, 32], at=at)
        qst = sb("qst", [P, NBUF, HG, N], BF16, at=at)
        kst = sb("kst", [P, NBUF, HG, N], BF16, at=at)
        osb = sb("osb", [P, N], at=at)
        mx = sb("mx", [P, HG * TB, 2], at=at)
        mneg = sb("mneg", [P, 4, HG * TB], at=at)
        mparts = sb("mparts", [P, 3, HG * TB], BF16, at=at)
        mT = sb("mT", [ZROWS, P], BF16, at=at)
        orec = sb("orec", [P, 2, HG, HG, 1], at=at)
        pre = ExitStack()
        xcm = sb("xcm", [P, T], at=pre)
        qk32 = sb("qk32", [P, 2, 2, N], at=pre)
        parts = sb("parts", [P, 2, 2, 3, N], BF16, at=pre)
        res = sb("res", [P, N], at=pre)
        pre.close()
        probs = sb("probs", [P, 2, HG, N], at=at)
        at.close()

        rt = ExitStack()
        x_cm = sb("x_cm", [P, T], at=rt)
        w_all = sb("w_all", [P, NT, NE], at=rt)
        w1s = sb("w1s", [P, NE, FE], at=rt)
        w2s = sb("w2s", [P, NE, HE, C], at=rt)
        pj = ExitStack()
        ost = sb("ost", [P, 2, 4, C], at=pj)
        ocm = sb("ocm", [P, 2, 512], at=pj)
        y1 = sb("y1", [P, 2, 4, C], at=pj)
        xs = sb("xs", [P, 2, 4, C], at=pj)
        xc = sb("xc", [P, 2, 512], at=pj)
        st6 = sb("st6", [P, 2, 4, 6], at=pj)
        mv = sb("mv", [P, 2, 4, 2], at=pj)
        rstd = sb("rstd", [P, 2, 4], at=pj)
        lg = sb("lg", [P, 2, 4, NE], at=pj)
        v8 = sb("v8", [P, 2, 4, 8], at=pj)
        ix8 = sb("ix8", [P, 2, 4, 8], U32, at=pj)
        ixf = sb("ixf", [P, 2, 4, 2], at=pj)
        gap = sb("gap", [P, 2, 4], at=pj)
        e2 = sb("e2", [P, 2, 4], at=pj)
        wpair = sb("wpair", [P, 2, 3, 4], at=pj)
        hot = sb("hot", [P, 2, 2, 4, NE], at=pj)
        wts = sb("wts", [P, 2, 4, NE], at=pj)
        wT = sb("wT", [NE, 2, 512], at=pj)
        pj.close()
        hid = sb("hid", [P, 2, HE, 512], at=rt)
        rt.close()
        dd = ExitStack()
        x_n = sb("x_n", [P, T], at=dd)
        ow = sb("ow", [P, C], at=dd)
        ob_row = sb("ob_row", [P, C], at=dd)
        w3b_row = sb("w3b_row", [P, C], at=dd)
        wu = sb("wu", [P, HID1], at=dd)
        wg = sb("wg", [P, HID1], at=dd)
        w3 = sb("w3", [P, H1, C], at=dd)
        gu_b = sb("gu_b", [P, 2, H1], at=dd)
        yin = sb("yin", [P, 2, 4, C], at=dd)
        x2 = sb("x2", [P, 2, 4, C], at=dd)
        x3 = sb("x3", [P, 2, 4, C], at=dd)
        xr = sb("xr", [P, 2, 4, C], at=dd)
        st6d = sb("st6d", [P, 2, 4, 6], at=dd)
        mvd = sb("mvd", [P, 2, 4, 2], at=dd)
        sqd = sb("sqd", [P, 2, 4], at=dd)
        rsd = sb("rsd", [P, 2, 4], at=dd)
        u_cm = sb("u_cm", [P, N], at=dd)
        y_cm = sb("y_cm", [P, N], at=dd)
        sg = sb("sg", [P, 2, 512], at=dd)
        hm = sb("hm", [P, H1, 512], at=dd)
        dd.close()

        lo = ExitStack()
        x5 = sb("x5", [P, NT, C], at=lo)
        h_all = sb("h_all", [P, B, N + 1], at=lo)
        n_all = o_all[:].rearrange("p g a t c -> p (g a t c)")
        wl = sb("wl", [P, L2, 3 * INNER], at=lo)
        wo = sb("wo", [P, L2, PAIRS, C], at=lo)
        ff1 = sb("ff1", [P, L2, 2, HF * P], at=lo)
        ff2 = sb("ff2", [P, L2, HF, C], at=lo)
        ffb1 = sb("ffb1", [P, L2, 2, HF], at=lo)
        ffb2 = sb("ffb2", [P, L2, C], at=lo)
        lgb = sb("lgb", [P, 2, L2], at=lo)
        mask = sb("mask", [P, TB, 192], BF16, at=lo)
        rot = sb("rot", [P, 4, TB, DH], at=lo)
        rotl = sb("rotl", [P, 4, TB, DH], at=lo)
        qks = sb("qks", [P, L2, 2, DH], at=lo)
        yl = sb("yl", [P, 2, 4, C], at=lo)
        xl = sb("xl", [P, 2, 4, C], at=lo)
        hb = sb("hb", [P, 2, 512], at=lo)
        st6l = sb("st6l", [P, 2, 4, 6], at=lo)
        mvl = sb("mvl", [P, 2, 4, 2], at=lo)
        rsl = sb("rsl", [P, 2, 4], at=lo)
        la = ExitStack()
        hs = sb("hs", [P, 2, P], at=la)
        sqb = sb("sqb", [P, 2, INNER], at=la)
        ssq = sb("ssq", [P, 2, 2, H2], at=la)
        rin = sb("rin", [P, 2, H2], at=la)
        rqk = sb("rqk", [P, 2, 2, H2], at=la)
        prod = sb("prod", [P, 2, 2, INNER], at=la)
        ksum = sb("ksum", [P, INNER], at=la)
        qkr = sb("qkr", [P, 2, INNER], at=la)
        vring = sb("vring", [P, 4, INNER], at=la)
        qz = sb("qz", [P, PAIRS, 2, P], at=la)
        kwin = sb("kwin", [P, 2, PAIRS, 256], at=la)
        mx2 = sb("mx2", [P, 2, H2], at=la)
        nb = sb("nb", [P, 2, H2], at=la)
        rsum = sb("rsum", [P, 2, H2], at=la)
        rrec = sb("rrec", [P, 2, H2], at=la)
        pbuf = sb("pbuf", [P, 2, H2, 256], at=la)
        pT = sb("pT", [P, 2, 2, 2, P], at=la)
        oT = sb("oT", [P, PAIRS, P], at=la)
        la.close()
        sgf = sb("sgf", [P, HF, 512], at=lo)
        hf = sb("hf", [P, HF, 512], at=lo)
        lo.close()


        (const_ready, blocks_zeroed, weights_loaded, x_loaded) = \
            sems("const_ready blocks_zeroed weights_loaded x_loaded")
        (q_done, k_done, v_done, q_evac, k_evac, v_evac, split) = \
            sems("q_done k_done v_done q_evac k_evac v_evac split")
        (rows_filled, vaug_filled, vaug_ready) = \
            sems("rows_filled vaug_filled vaug_ready")
        (st_ready, exp_done, av_done, o_evac, ring_ready, ring_used, maxsplit, max_stored, out_norm) = \
            sems("st_ready exp_done av_done o_evac ring_ready ring_used maxsplit max_stored out_norm")
        attn_done = sem("attn_done")
        (ost_ready, oT_done, ocm_ready, proj_done, sum_ready, var_ready, rstd_ready, x1_ready, x1T_done) = \
            sems("ost_ready oT_done ocm_ready proj_done sum_ready var_ready rstd_ready x1_ready x1T_done")
        (xc_ready, route_done, gap_ready, e2_ready, wts_ready, wT_done, wT_ready, b2_done, acc_ready) = \
            sems("xc_ready route_done gap_ready e2_ready wts_ready wT_done wT_ready b2_done acc_ready")
        (cm_ready, experts_loaded, out_stored) = \
            sems("cm_ready experts_loaded out_stored")
        (dve_chain, pool_chain, dve_settled, pool_settled) = \
            sems("dve_chain pool_chain dve_settled pool_settled")
        act_settled = sem("act_settled")
        (up_done, relu_done, down_done, moe_added) = \
            sems("up_done relu_done down_done moe_added")
        (mid_loaded, yin_ready, var2_ready, rstd2_ready, xr_ready, xrT_done, u_ready, scanned, ssm_done) = \
            sems("mid_loaded yin_ready var2_ready rstd2_ready xr_ready xrT_done u_ready scanned ssm_done")
        (x3_done, xrT2_done, xn_ready, z_ready, tanh_ready) = \
            sems("x3_done xrT2_done xn_ready z_ready tanh_ready")
        (g_done, u_done, silu_done, gate_done, mlp_done, z_added) = \
            sems("g_done u_done silu_done gate_done mlp_done z_added")
        (late_loaded, yl_ready, var3_ready, rstd3_ready, xl_ready, xlT_done, h_ready, kept) = \
            sems("late_loaded yl_ready var3_ready rstd3_ready xl_ready xlT_done h_ready kept")
        (late_filled, hs_ready, qp_done, kp_done, vp_done, sq_ready, ssq_ready, rqk_ready) = \
            sems("late_filled hs_ready qp_done kp_done vp_done sq_ready ssq_ready rqk_ready")
        (qpart_ready, kpart_ready, q_rot, k_rot, qT_done, kT_done, qz_ready, kwin_ready) = \
            sems("qpart_ready kpart_ready q_rot k_rot qT_done kT_done qz_ready kwin_ready")
        (v_kept, sc_done, max_ready, wexp_done, pn_ready, pT_done, pTa_ready, pTd_ready) = \
            sems("v_kept sc_done max_ready wexp_done pn_ready pT_done pTa_ready pTd_ready")
        (pv_done, oTs_ready, wo_done, xw_ready) = \
            sems("pv_done oTs_ready wo_done xw_ready")
        (hb_ready, hbT_done, n_ready, fg_done, fa_done, gelu_done, fgate_done, ff_done, ff_added) = \
            sems("hb_ready hbT_done n_ready fg_done fa_done gelu_done fgate_done ff_done ff_added")
        stack_loaded = [sem(f"stack_loaded{i}") for i in range(NBUF)]
        xcm_loaded = [sem(f"xcm_loaded{b}") for b in range(B)]
        parts_stored = [[sem(f"parts_stored{b}_{w}") for w in "qk"] for b in range(B)]
        maxrow_loaded = [sem(f"maxrow_loaded{i}") for i in range(NBUF)]
        LOADS = 18 * 16
        PRE_USES = 64 + 1 + 32
        RING, VALUES = 5, 3
        BODY_USES = len(ring_uses(True, True, True))
        NFULL = NG - 4
        WEIGHTS = 16 * (2 * G0 + 7)

        def later(it, u, k):
            return it + (u + k) // NBUF, (u + k) % NBUF

        def ring_base(g):
            n = PRE_USES
            for i in range(g):
                n += len(ring_uses(i + 1 < NG, i + 2 < NG, True))
            return n

        def ring_bank(use):
            return RING + use % 3

        def score_bank(u, kt, i):
            return ((u * TB + kt) * (2 * HG) + i) % 3

        def attention_bodies(eng, body):
            def three(it):
                for u in range(NBUF):
                    used = PRE_USES + u * BODY_USES
                    body(it, u, used + it * (NBUF * BODY_USES), used % 3, True, True)
            with eng.Fori(0, NFULL // NBUF) as it:
                three(it)
            for g in range(NFULL, NG):
                body(g // NBUF, g % NBUF, ring_base(g), ring_base(g) % 3, g + 1 < NG, g + 2 < NG)

        def norm_stats(dve, ch, src, st, mvx, h, ready, square=None):
            for t in range(4):
                ins = dve.bn_stats(st[:, h, t, :], src[:, t, :])
            ch.link(ins, settle=True)
            for t in range(4):
                ins = dve.bn_aggr(mvx[:, h, t, :], st[:, h, t, :])
            if square is not None:
                ch.link(ins)
                ch.link(dve.tensor_tensor(square[:, h, :], mvx[:, h, :, 0], mvx[:, h, :, 0], ALU.mult))
                ins = dve.tensor_tensor(mvx[:, h, :, 1], mvx[:, h, :, 1], square[:, h, :], ALU.add)
            ins.then_inc(ready, 1)

        def rstds(pool, ch, pairs, base, ready, done, mvx, r):
            def pair(i):
                ch.loop(i, 2)
                for h in range(2):
                    pool.wait_ge(ready, base + i * 2 + h + 1)
                    ch.settle()
                    ch.link(pool.tensor_scalar(r[:, h, :], mvx[:, h, :, 1], EPS, None, ALU.add))
                    pool.tensor_tensor(r[:, h, :], r[:, h, :], neghalf[:, 0:4], ALU.pow).then_inc(done, 1)
            with pool.Fori(0, pairs) as i:
                pair(i)
            ch.close(pairs)

        def turn4(pe, bank, src, done):
            for t in range(4):
                mm = pe.transpose(PS[:, bank, t * P:(t + 1) * P], src(t), ident[:])
            mm.then_inc(done, 1)

        def four(bank):
            return PS[:, bank, :].rearrange("p (t c) -> p t c", t=4)

        def every4(row):
            return row.unsqueeze(1).broadcast_to([P, 4, C])

        def tile_steps(eng, step, ch=None, per=0):
            for i in range(4):
                step(i, i, True, i >= 1, i >= 2)
            with eng.Fori(0, NT // 4 - 2) as it:
                if ch is not None:
                    ch.loop(it, 4 * per)
                for r in range(4):
                    step(it * 4 + (4 + r), r, True, True, True)
            if ch is not None:
                ch.close(NT // 4 - 2)
            for i in range(NT - 4, NT + 2):
                step(i, i % 4, i < NT, i <= NT, True)

        def settle(eng):
            eng.nop().then_inc(act_settled, 1)

        def wait(eng, what, value):
            if not isinstance(value, int) or value > 0:
                eng.wait_ge(what, value)

        block = ctx.enter_context(nc.Block())

        @block.sync
        def _(sp):
            for b in range(B):
                sp.dma_start(xcm[:, b * N:(b + 1) * N], d["x_cm"][:, b * N:(b + 1) * N]).then_inc(xcm_loaded[b], 16)
                if b == 0:
                    sp.wait_ge(blocks_zeroed, 2)
                    for g in range(G0):
                        c = C // G0
                        sp.dma_start(wq_bd[g * c:(g + 1) * c, 3 * g * c:3 * (g + 1) * c], d["w_qkv"][g])\
                          .then_inc(weights_loaded, 16)
                        sp.dma_start(wp_bd[g * c:(g + 1) * c, g * c:(g + 1) * c], d["w_proj"][g])\
                          .then_inc(weights_loaded, 16)
            sp.dma_start(x_tm[:], d["x_tm"]).then_inc(x_loaded, 16)
            sp.dma_start(bp_row[:], d["b_proj"].partition_broadcast(P)).then_inc(weights_loaded, 16)
            sp.dma_start(wr[:], d["w_router"]).then_inc(weights_loaded, 16)
            sp.dma_start(br_row[:], d["b_router"].partition_broadcast(P)).then_inc(weights_loaded, 16)
            sp.dma_start(b2s[:], d["moe_b2"]).then_inc(weights_loaded, 16)
            sp.dma_start(b1c[:], d["moe_b1"]).then_inc(weights_loaded, 16)
            sp.dma_start(cols1[:], d["cols1"]).then_inc(weights_loaded, 16)
            sp.dma_start(iota8[:], d["iota8"].partition_broadcast(P)).then_inc(weights_loaded, 16)
            for b in range(B):
                for w in range(2):
                    sp.wait_ge(split, 8 * b + 4 * w + 4)
                    sp.dma_start(parts_dram[w, :, b * P:(b + 1) * P, :].rearrange("s r t -> r s t"),
                                 parts[:, b % 2, w, :, :]).then_inc(parts_stored[b][w], 16)
            for stored in parts_stored:
                for one in stored:
                    sp.wait_ge(one, 16)
            sp.wait_ge(rows_filled, 3)

            def load_stack(g, u):
                for i in range(3):
                    for j in range(3):
                        r = (3 * i + j) * D0
                        for dst, w, part in ((qst, 0, i), (kst, 1, j)):
                            src = parts_dram[w, part, bass.ds(g * (HG * D0), HG * D0), :]\
                                .rearrange("(h d) t -> d h t", d=D0)
                            sp.dma_start(dst[r:r + D0, u, :, :], src).then_inc(stack_loaded[u], 16)

            def turn_max(it, u, used):
                sp.wait_ge(ring_used, used)
                sp.dma_start(max_dram[u].rearrange("s (r t) -> (s r) t", t=P), mT[:]).then_inc(max_stored, 16)
                sp.wait_ge(max_stored, 16 * (it * NBUF + u) + 16)
                sp.dma_start(qst[ZROWS:SROWS, u, :, :], max_dram[u].rearrange("s (h t) -> s h t", h=HG))\
                  .then_inc(maxrow_loaded[u], 16)

            load_stack(0, 0)
            load_stack(1, 1)
            turn_max(0, 0, 65)

            def body(it, u, used, phase, nxt, aft):
                if aft:
                    it2, u2 = later(it, u, 2)
                    sp.wait_ge(st_ready, (it * NBUF + u) * (2 * HG * TB) + 1)
                    load_stack(it2 * NBUF + u2, u2)
                if nxt:
                    it1, u1 = later(it, u, 1)
                    turn_max(it1, u1, used + 32 + 16 * aft + 1)
            attention_bodies(sp, body)

            sp.wait_ge(out_norm, 2 * NG + 1)
            for e in range(NE):
                sp.dma_start(w1s[:, e, :], d["moe_w1"][:, e, :]).then_inc(experts_loaded, 16)
                sp.dma_start(w2s[:, e, :, :], d["moe_w2"][:, e, :, :]).then_inc(experts_loaded, 16)
            sp.wait_ge(moe_added, NS * NE + 2)
            for dst, src in ((ow[:], d["out_w"]), (ob_row[:], d["out_b"].partition_broadcast(P)),
                             (w3b_row[:], d["w3_b"].partition_broadcast(P)), (wu[:], d["w1_w"]), (wg[:], d["w2_w"]),
                             (w3[:], d["w3_w"]), (gu_b[:], d["gu_b"])):
                sp.dma_start(dst, src).then_inc(mid_loaded, 16)
            sp.wait_ge(z_added, NS + 1)
            for dst, src in ((wl[:], d["wqkv"]), (wo[:], d["wo"]), (ff1[:], d["ff1"]), (ff2[:], d["ff2"]), (ffb1[:], d["ffb1"]),
                             (ffb2[:], d["ffb2"].partition_broadcast(P)), (lgb[:], d["lgb"]), (mask[:], d["mask"]),
                             (rot[:], d["rot"]), (qks[:], d["qks"].partition_broadcast(P))):
                sp.dma_start(dst, src).then_inc(late_loaded, 16)
            sp.wait_ge(kept, LNS + NS)
            sp.dma_start(out, x_tm[:]).then_inc(out_stored, 16)
            sp.wait_ge(out_stored, 16)

        @block.gpsimd
        def _(pool):
            ch = Chain(pool, pool_chain, pool_settled)
            pool.memset(wq_bd[:], 0.0).then_inc(blocks_zeroed, 1)
            pool.memset(wp_bd[:], 0.0).then_inc(blocks_zeroed, 1)
            for t in (ident, identb):
                ch.link(pool.memset(t[:], 0.0))
                pool.affine_select(out=t[:], in_=t[:], compare_op=ALU.not_equal, fill=1.0, base=0,
                                   pattern=[[-1, P]], channel_multiplier=1).then_inc(const_ready, 1)
            pool.memset(neghalf[:], -0.5).then_inc(const_ready, 1)
            ch.link(pool.memset(vaug[:], 0.0))
            ch.link(pool.memset(vaug[:, :, :, :, D0:D0 + 1], 1.0))
            pool.nop().then_inc(vaug_filled, 1)
            ch.link(pool.memset(qst[64:ZROWS, :, :, :].bitcast(F32), 0.0))
            pool.nop().then_inc(rows_filled, 1)
            ch.link(pool.memset(kst[64:ZROWS, :, :, :].bitcast(F32), 0.0))
            pool.nop().then_inc(rows_filled, 1)
            pool.memset(kst[ZROWS:SROWS, :, :, :], 1.0).then_inc(rows_filled, 1)

            PERB = 2
            with pool.Fori(0, B) as b:
                ch.loop(b, PERB)
                for h in range(2):
                    pool.wait_ge(var_ready, b * 2 + h + 1)
                    ch.settle()
                    ch.link(pool.tensor_scalar(rstd[:, h, :], mv[:, h, :, 1], EPS, None, ALU.add))
                    pool.tensor_tensor(rstd[:, h, :], rstd[:, h, :], neghalf[:, 0:4], ALU.pow)\
                        .then_inc(rstd_ready, 1)
            ch.close(B)
            rstds(pool, ch, 3 * B, 0, var2_ready, rstd2_ready, mvd, rsd)
            rstds(pool, ch, B, 0, var3_ready, rstd3_ready, mvl, rsl)
            for t in (qz, kwin, pbuf, vring):
                ch.link(pool.memset(t[:], 0.0))
            pool.nop().then_inc(late_filled, 1)
            for l in range(L2):
                def step(i, r, proj, scores, output):
                    n, u = l * NT + i, r % 2
                    if proj:
                        pool.wait_ge(qpart_ready, n + 1)
                        wait(pool, qT_done, n)
                        pool.tensor_tensor(qkr[:, 0, :], prod[:, 0, 0, :], prod[:, 0, 1, :], ALU.add).then_inc(q_rot, 1)
                        pool.wait_ge(kpart_ready, n + 1)
                        pool.tensor_tensor(ksum[:], prod[:, 1, 0, :], prod[:, 1, 1, :], ALU.add)
                        pool.wait_ge(ssq_ready, 2 * n + 2)
                        ch.settle()
                        pool.tensor_scalar(rin[:, 0, :], ssq[:, u, 0, :], 1e-24, 1.0 / QK_SCALE ** 2,
                                           ALU.max, ALU.mult)
                        ch.link(pool.tensor_scalar(rin[:, 1, :], ssq[:, u, 1, :], 1e-24, None, ALU.max))
                        wait(pool, wexp_done, (n - 1) * H2)
                        ch.link(pool.tensor_tensor(rqk[:, u, :, :], rin[:],
                                                   neghalf[:, 0:1].unsqueeze(2).broadcast_to([P, 2, H2]), ALU.pow))
                        pool.nop().then_inc(rqk_ready, 1)
                        wait(pool, kT_done, n)
                        pool.tensor_tensor(qkr[:, 1, :].rearrange("p (h c) -> p h c", h=H2),
                                           ksum[:].rearrange("p (h c) -> p h c", h=H2),
                                           rqk[:, u, 1, :].unsqueeze(2).broadcast_to([P, H2, DH]), ALU.mult)\
                            .then_inc(k_rot, 1)
                tile_steps(pool, step, ch, 2)
                rstds(pool, ch, B, (l + 1) * NS, var3_ready, rstd3_ready, mvl, rsl)
            rstds(pool, ch, B, (L2 + 1) * NS, var3_ready, rstd3_ready, mvl, rsl)

        @block.scalar
        def _(act):
            for credit in (o_evac, h_ready):
                act.nop().then_inc(credit, 1)
            for b in range(B):
                p2 = b % 2
                act.wait_ge(q_done, b + 1)
                if b >= 2:
                    act.wait_ge(split, 8 * (b - 2) + 8)
                act.activation(qk32[:, p2, 0, :], PS[:, 0:2, :].rearrange("p a b -> p (a b)"), ACT.Copy,
                               scale=float(D0) ** -0.5).then_inc(q_evac, 1)
                act.wait_ge(k_done, b + 1)
                act.activation(qk32[:, p2, 1, :], PS[:, 2:4, :].rearrange("p a b -> p (a b)"), ACT.Copy)\
                   .then_inc(k_evac, 1)
                act.wait_ge(v_done, b + 1)
                for t in range(2):
                    act.activation(
                        v_all[:, b * HG:(b + 1) * HG, 4 * t:4 * t + 4, :].rearrange("p g t c -> p t g c"),
                        PS[:, 4 + t, :].rearrange("p (t g c) -> p t g c", t=4, g=HG), ACT.Copy)\
                       .then_inc(v_evac, 1)

            def exps(it, u, kt):
                g = it * NBUF + u
                for i in range(2 * HG):
                    act.wait_ge(st_ready, (g * TB + kt) * (2 * HG) + i + 1)
                    if i == 0 and not (kt < 2 and isinstance(g, int) and g == 0):
                        act.wait_ge(av_done, g * (2 * TB) + 2 * kt - 2 + 1)
                    act.activation(probs[:, kt % 2, i // 2, i % 2 * 512:i % 2 * 512 + 512],
                                   PS[:, score_bank(u, kt, i), :], ACT.Exp).then_inc(exp_done, 1)

            act.wait_ge(split, 8 * B)
            for stored in parts_stored:
                for one in stored:
                    act.wait_ge(one, 16)
            exps(0, 0, 0)

            def body(it, u, used, phase, nxt, aft):
                g = it * NBUF + u
                for kt in range(1, TB):
                    exps(it, u, kt)
                if nxt:
                    exps(*later(it, u, 1), 0)
                act.wait_ge(av_done, g * (2 * TB) + 2 * TB + 1)
                act.wait_ge(out_norm, g * 2 + 1)
                for t in range(2):
                    act.activation(osb[:, 512 * t:512 * t + 512], PS[:, VALUES + t, :], ACT.Copy)\
                       .then_inc(o_evac, 1)
            attention_bodies(act, body)

            with act.Fori(0, B) as b:
                for h in range(2):
                    act.wait_ge(oT_done, b * 2 + h + 1)
                    act.activation(ocm[:, h, :], PS[:, 4 * h, :], ACT.Copy).then_inc(ocm_ready, 1)
                for h in range(2):
                    act.wait_ge(x1T_done, b * 2 + h + 1)
                    act.activation(xc[:, h, :], PS[:, 4 * h + 2, :], ACT.Copy).then_inc(xc_ready, 1)
                for h in range(2):
                    act.activation(x_cm[:, bass.ds(b * N + h * 512, 512)], PS[:, 4 * h + 2, :], ACT.Copy)\
                       .then_inc(cm_ready, 1)
                for h in range(2):
                    act.wait_ge(gap_ready, b * 2 + h + 1)
                    act.activation(e2[:, h, :], gap[:, h, :], ACT.Exp).then_inc(e2_ready, 1)
                for h in range(2):
                    act.wait_ge(wT_done, b * 2 + h + 1)
                    act.activation(wT[:, h, :], PS[0:NE, 4 * h, :], ACT.Copy).then_inc(wT_ready, 1)
            act.nop().then_inc(relu_done, HE)
            act.wait_ge(acc_ready, NS)
            with act.Fori(0, NS) as i:
                for e in range(NE):
                    m = i * NE + e
                    act.wait_ge(down_done, m + 1)
                    for t in range(HE):
                        act.wait_ge(up_done, m * HE + t + 1)
                        act.activation(hid[:, e % 2, t, :], PS[:, t, :], ACT.Relu,
                                       bias=b1c[:, e * HE + t:e * HE + t + 1]).then_inc(relu_done, 1)
            act.wait_ge(moe_added, NS * NE + 2)
            act.activation(a_tanh[:], cols1[:, 0:1], ACT.Tanh).then_inc(tanh_ready, 1)
            with act.Fori(0, B) as b:
                for h in range(2):
                    act.wait_ge(z_ready, b * 2 + 1)
                    settle(act)
                    act.activation(yin[:, h, :, :], x_tm[:, bass.ds(b * TB + h * 4, 4), :], ACT.Copy)\
                       .then_inc(yin_ready, 1)
            with act.Fori(0, NS) as i:
                for t in range(H1):
                    act.wait_ge(g_done, i * H1 + t + 1)
                    act.wait_ge(gate_done, i * H1 + t + 1)
                    act.activation(sg[:, t % 2, :], PS[:, t % 2, :], ACT.Silu, bias=gu_b[:, 1, t:t + 1])\
                       .then_inc(silu_done, 1)
            act.wait_ge(z_added, NS + 1)
            def to_shifted(b, h, base):
                act.wait_ge(xlT_done, base + b * 2 + h + 1 + 1)
                settle(act)
                act.activation(h_all[0:64, b, h * 512:h * 512 + 512], PS[0:64, 4 * h, :], ACT.Copy)
                act.activation(h_all[64:P, b, h * 512 + 1:h * 512 + 513], PS[64:P, 4 * h, :], ACT.Copy)\
                   .then_inc(h_ready, 1)
            with act.Fori(0, B) as b:
                for h in range(2):
                    act.wait_ge(xlT_done, b * 2 + 1)
                    settle(act)
                    act.activation(yl[:, h, :, :], x_tm[:, bass.ds(b * TB + h * 4, 4), :], ACT.Copy)\
                       .then_inc(yl_ready, 1)
                for h in range(2):
                    to_shifted(b, h, 0)
            act.wait_ge(late_filled, 1)

            def keep_tile(i, u):
                at = (i % TB) * P
                act.activation(hs[:, u, :], h_all[:, i // TB, bass.ds(at, P)], ACT.Copy).then_inc(hs_ready, 1)

            for l in range(L2):
                act.wait_ge(h_ready, (2 * l + 1) * NS + 1)
                def step(i, r, proj, scores, output):
                    n, u = l * NT + i, r % 2
                    if scores:
                        act.wait_ge(qT_done, n)
                        wait(act, sc_done, 2 * (n - 1))
                        for k in range(2):
                            rows = slice(64 * k, 64 * k + 64)
                            ins = act.activation(qz[rows, :, k, :],
                                                 PS[rows, 5, :].rearrange("p (c t) -> p c t", c=PAIRS), ACT.Copy)
                        ins.then_inc(qz_ready, 1)
                    if proj:
                        wait(act, ssq_ready, 2 * n)
                        for k, done in enumerate((qp_done, kp_done)):
                            act.wait_ge(done, n + 1)
                            act.activation(sqb[:, k, :], PS[:, k, :], ACT.Square).then_inc(sq_ready, 1)
                        act.wait_ge(vp_done, n + 1)
                        wait(act, pv_done, 4 * (n - 2))
                        act.activation(vring[:, r, :], PS[:, 2, :], ACT.Copy).then_inc(v_kept, 1)
                        if not (isinstance(i, int) and i == NT - 1):
                            keep_tile(i + 1, 1 - u)
                    if output:
                        act.wait_ge(pT_done, 4 * (n - 2) + 1)
                        wait(act, pv_done, 4 * (n - 2) - 1)
                        act.activation(pT[:, 0, :, :, :].rearrange("p a b c -> p (a b c)"), PS[:, 5, :], ACT.Copy)\
                           .then_inc(pTa_ready, 1)
                    for c in range(2):
                        if scores:
                            j = n - 1
                            act.wait_ge(max_ready, 2 * j + c + 1)
                            if c == 0:
                                wait(act, pT_done, 4 * (j - 1))
                            for h in range(4 * c, 4 * c + 4):
                                act.activation(pbuf[:, 1 - u, h, 64:256],
                                               PS[:, 3 + h % 4 // 2, (h % 2) * 192:(h % 2) * 192 + 192], ACT.Exp,
                                               bias=nb[:, 1 - u, h:h + 1], scale=rqk[:, 1 - u, 0, h:h + 1],
                                               accum_out=rsum[:, 1 - u, h:h + 1]).then_inc(wexp_done, 1)
                        if output and c == 0:
                            act.wait_ge(pv_done, 4 * (n - 2) + 4)
                            wait(act, wo_done, n - 2)
                            act.activation(oT[:].rearrange("p c t -> p (c t)"), PS[:, 7, :], ACT.Copy)\
                               .then_inc(oTs_ready, 1)
                keep_tile(0, 0)
                tile_steps(act, step)
                fb = (2 * l + 1) * NS
                act.wait_ge(xw_ready, (l + 1) * NT)
                with act.Fori(0, B) as b:
                    for h in range(2):
                        act.wait_ge(xlT_done, fb + b * 2 + 1)
                        settle(act)
                        act.activation(yl[:, h, :, :], x_tm[:, bass.ds(b * TB + h * 4, 4), :], ACT.Copy)\
                           .then_inc(yl_ready, 1)
                    for h in range(2):
                        to_shifted(b, h, fb)
                    act.wait_ge(h_ready, fb + b * 2 + 2 + 1)
                    for h in range(2):
                        act.wait_ge(hbT_done, l * NS + b * 2 + 1)
                        settle(act)
                        act.activation(hb[:, h, :], h_all[:, b, h * 512:h * 512 + 512], ACT.Copy)\
                           .then_inc(hb_ready, 1)
                with act.Fori(0, NS) as i:
                    for t in range(HF):
                        k = l * NS * HF + i * HF + t
                        act.wait_ge(fg_done, k + 1)
                        act.wait_ge(fgate_done, k + 1)
                        act.activation(sgf[:, t, :], PS[:, t, :], ACT.Gelu,
                                       bias=ffb1[:, l, 1, t:t + 1]).then_inc(gelu_done, 1)
                act.wait_ge(ff_added, (l + 1) * NS + 1)
                fb = (2 * l + 2) * NS
                if l + 1 < L2:
                    with act.Fori(0, B) as b:
                        for h in range(2):
                            act.wait_ge(xlT_done, fb + b * 2 + 1)
                            settle(act)
                            act.activation(yl[:, h, :, :], x_tm[:, bass.ds(b * TB + h * 4, 4), :], ACT.Copy)\
                               .then_inc(yl_ready, 1)
                        for h in range(2):
                            to_shifted(b, h, fb)

        @block.tensor
        def _(pe):
            for credit in (av_done, xlT_done, hbT_done, ff_done):
                pe.nop().then_inc(credit, 1)
            pe.wait_ge(weights_loaded, WEIGHTS)
            pe.wait_ge(const_ready, 2)
            for b in range(B):
                pe.wait_ge(xcm_loaded[b], 16)
                for w, (done, evac) in enumerate(((q_done, q_evac), (k_done, k_evac))):
                    if b:
                        pe.wait_ge(evac, b)
                    for t in range(2):
                        mm = pe.matmul(PS[:, 2 * w + t, :], wq_bd[:, w * C:(w + 1) * C],
                                       xcm[:, b * N + 512 * t:b * N + 512 * t + 512], start=True, stop=True)
                    mm.then_inc(done, 1)
                if b:
                    pe.wait_ge(v_evac, 2 * b)
                for t in range(TB):
                    mm = pe.matmul(PS[:, 4 + t // 4, (t % 4) * P:(t % 4 + 1) * P],
                                   xcm[:, b * N + t * P:b * N + (t + 1) * P], wq_bd[:, 2 * C:3 * C],
                                   start=True, stop=True)
                mm.then_inc(v_done, 1)

            pe.wait_ge(v_evac, 2 * B)
            ring = {"base": 0, "phase": 0, "n": 0}

            def ring_slot():
                if not (isinstance(ring["base"], int) and ring["base"] + ring["n"] < 3):
                    pe.wait_ge(ring_used, ring["base"] + ring["n"] - 2)
                ring["n"] += 1
                return ring_bank(ring["phase"] + ring["n"] - 1)

            def max_unit(it, u, i):
                h, qt, half = i // 16, i // 2 % TB, i % 2
                if i == 0:
                    pe.wait_ge(stack_loaded[u], it * LOADS + LOADS)
                bank = ring_slot()
                pe.matmul(PS[:, bank, :], qst[0:ZROWS, u, h, qt * P:(qt + 1) * P],
                          kst[0:ZROWS, u, h, half * 512:half * 512 + 512], start=True, stop=True)\
                  .then_inc(ring_ready, 1)

            def max_turn(it, u):
                pe.wait_ge(maxsplit, (it * NBUF + u) * 5 + 5)
                bank = ring_slot()
                pe.transpose(PS[:, bank, :].bitcast(BF16)[0:ZROWS, 0:P],
                             mparts[:].rearrange("p s r -> p (s r)"), identb[:]).then_inc(ring_ready, 1)

            def score_unit(it, u, kt, i):
                g, h, half = it * NBUF + u, i // 2, i % 2
                if kt == 0 and i == 0:
                    pe.wait_ge(maxrow_loaded[u], it * 16 + 16)
                if not (isinstance(g, int) and g == 0 and kt == 0 and i < 3):
                    pe.wait_ge(exp_done, (g * TB + kt) * (2 * HG) + i - 2)
                pe.matmul(PS[:, score_bank(u, kt, i), :], kst[0:SROWS, u, h, kt * P:(kt + 1) * P],
                          qst[0:SROWS, u, h, 512 * half:512 * half + 512], start=True, stop=True)\
                  .then_inc(st_ready, 1)

            def value_unit(it, u, kt, half):
                g = it * NBUF + u
                if half == 0:
                    pe.wait_ge(exp_done, (g * TB + kt + 1) * (2 * HG))
                    if kt == 0:
                        pe.wait_ge(vaug_ready, g + 1)
                        pe.wait_ge(o_evac, g * 2 + 1)
                for h in range(HG):
                    mm = pe.matmul(PS[32 * h:32 * h + 32, VALUES + half, :], vaug[:, u, kt, h, :],
                                   probs[:, kt % 2, h, 512 * half:512 * half + 512],
                                   start=(kt == 0), stop=(kt == TB - 1))
                mm.then_inc(av_done, 1)

            def out_turn(it, u, half):
                pe.wait_ge(o_evac, (it * NBUF + u) * 2 + half + 1 + 1)
                bank = ring_slot()
                for t in range(4):
                    mm = pe.transpose(PS[:, bank, t * P:(t + 1) * P],
                                      osb[:, 512 * half + t * P:512 * half + (t + 1) * P], ident[:])
                mm.then_inc(ring_ready, 1)

            for i in range(64):
                max_unit(0, 0, i)
            max_turn(0, 0)
            for i in range(32):
                max_unit(0, 1, i)
            for i in range(2 * HG):
                score_unit(0, 0, 0, i)

            def body(it, u, used, phase, nxt, aft):
                ring["base"], ring["phase"], ring["n"] = used, phase, 0
                for kt in range(1, TB + 1):
                    units = []
                    if kt <= 4 and nxt:
                        units = [(*later(it, u, 1), 32 + 8 * (kt - 1) + i) for i in range(8)]
                    if kt > 4 and aft:
                        units = [(*later(it, u, 2), 8 * (kt - 5) + i) for i in range(8)]
                    if kt == 7 and nxt:
                        max_turn(*later(it, u, 1))
                    for i in range(2 * HG):
                        for x in units[i:i + 1]:
                            max_unit(*x)
                        if kt < TB:
                            score_unit(it, u, kt, i)
                        elif nxt:
                            score_unit(*later(it, u, 1), 0, i)
                        if i % HG == HG - 1:
                            value_unit(it, u, kt - 1, i // HG)
                for half in range(2):
                    out_turn(it, u, half)
            attention_bodies(pe, body)

            with pe.Fori(0, B) as b:
                for h in range(2):
                    pe.wait_ge(ost_ready, b * 2 + h + 1)
                    for t in range(4):
                        mm = pe.transpose(PS[:, 4 * h, t * P:(t + 1) * P], ost[:, h, t, :], ident[:])
                    mm.then_inc(oT_done, 1)
                for h in range(2):
                    pe.wait_ge(ocm_ready, b * 2 + h + 1)
                    for t in range(4):
                        mm = pe.matmul(PS[:, 4 * h + 1, t * P:(t + 1) * P], ocm[:, h, t * P:(t + 1) * P],
                                       wp_bd[:], start=True, stop=True)
                    mm.then_inc(proj_done, 1)
                for h in range(2):
                    pe.wait_ge(x1_ready, b * 2 + h + 1)
                    for t in range(4):
                        mm = pe.transpose(PS[:, 4 * h + 2, t * P:(t + 1) * P], xs[:, h, t, :], ident[:])
                    mm.then_inc(x1T_done, 1)
                for h in range(2):
                    pe.wait_ge(xc_ready, b * 2 + h + 1)
                    for t in range(4):
                        mm = pe.matmul(PS[:, 4 * h + 3, t * NE:(t + 1) * NE], xc[:, h, t * P:(t + 1) * P],
                                       wr[:], start=True, stop=True)
                    mm.then_inc(route_done, 1)
                for h in range(2):
                    pe.wait_ge(wts_ready, b * 2 + h + 1)
                    for t in range(4):
                        mm = pe.transpose(PS[0:NE, 4 * h, t * P:(t + 1) * P], wts[:, h, t, :], ident[:])
                    mm.then_inc(wT_done, 1)
                for h in range(2):
                    pe.wait_ge(wT_ready, b * 2 + h + 1)
                    for t in range(4):
                        mm = pe.matmul(PS[:, 4 * h + 1, t * P:(t + 1) * P], wT[:, h, t * P:(t + 1) * P],
                                       b2s[:], start=True, stop=True)
                    mm.then_inc(b2_done, 1)
                pe.wait_ge(acc_ready, b * 2 + 2)
                pe.wait_ge(cm_ready, b * 2 + 2)
            pe.nop().then_inc(down_done, 2)
            pe.wait_ge(experts_loaded, 16 * 2 * NE)
            with pe.Fori(0, NS) as i:
                def up(e):
                    for t in range(HE):
                        pe.wait_ge(relu_done, (i * NE + e) * HE + t + 1)
                        pe.matmul(PS[:, t, :], w1s[:, e, t * P:(t + 1) * P], x_cm[:, bass.ds(i * 512, 512)],
                                  start=True, stop=True).then_inc(up_done, 1)

                def down(e):
                    m = i * NE + e
                    pe.wait_ge(relu_done, m * HE + 2 * HE)
                    pe.wait_ge(moe_added, m + 1)
                    for t in range(4):
                        for k in range(HE):
                            mm = pe.matmul(PS[:, 4 + e % 2, t * P:(t + 1) * P], hid[:, e % 2, k, t * P:(t + 1) * P],
                                           w2s[:, e, k, :], start=(k == 0), stop=(k == HE - 1))
                    mm.then_inc(down_done, 1)
                up(0)
                for e in range(1, NE):
                    up(e)
                    down(e - 1)
                down(NE - 1)
            pe.wait_ge(mid_loaded, 16 * 7)
            with pe.Fori(0, B) as b:
                for h in range(2):
                    pe.wait_ge(xr_ready, b * 4 + h + 1)
                    turn4(pe, 4 * h, lambda t: xr[:, h, t, :], xrT_done)
                pe.wait_ge(scanned, b + 1)
                for h in range(2):
                    for t in range(4):
                        mm = pe.matmul(PS[:, 4 * h + 1, t * P:(t + 1) * P], y_cm[:, h * 512 + t * P:h * 512 + (t + 1) * P],
                                       ow[:], start=True, stop=True)
                    mm.then_inc(ssm_done, 1)
                for h in range(2):
                    pe.wait_ge(xr_ready, b * 4 + 2 + h + 1)
                    turn4(pe, 4 * h + 2, lambda t: xr[:, h, t, :], xrT2_done)
                pe.wait_ge(xn_ready, b * 2 + 2)
            pe.wait_ge(z_ready, NS + 1)
            pe.nop().then_inc(mlp_done, 1)
            with pe.Fori(0, NS) as i:
                for t in range(H1):
                    pe.wait_ge(gate_done, i * H1 + t + 1)
                    for w, done, bank in ((wg, g_done, 0), (wu, u_done, 2)):
                        pe.matmul(PS[:, bank + t % 2, :], w[:, t * P:(t + 1) * P], x_n[:, bass.ds(i * 512, 512)],
                                  start=True, stop=True).then_inc(done, 1)
                pe.wait_ge(gate_done, i * H1 + H1 + 2)
                wait(pe, z_added, i + 1)
                for t in range(4):
                    for k in range(H1):
                        mm = pe.matmul(PS[:, 4, t * P:(t + 1) * P], hm[:, k, t * P:(t + 1) * P], w3[:, k, :],
                                       start=(k == 0), stop=(k == H1 - 1))
                mm.then_inc(mlp_done, 1)
            pe.wait_ge(late_loaded, 16 * 10)
            def turned_inputs(src, ready, base):
                with pe.Fori(0, B) as b:
                    for h in range(2):
                        pe.wait_ge(ready, base + b * 2 + h + 1)
                        wait(pe, h_ready, base + b * 2 + 1)
                        turn4(pe, 4 * h, lambda t: src[:, h, t, :], xlT_done)
            turned_inputs(xl, xl_ready, 0)
            pe.wait_ge(h_ready, NS + 1)
            for l in range(L2):
                def step(i, r, proj, scores, output):
                    n, u = l * NT + i, r % 2
                    j, m, w = n - 1, n - 2, 1 - u
                    if scores:
                        pe.wait_ge(q_rot, j + 1)
                        wait(pe, pTd_ready, 3 * m - 1)
                        turn4(pe, 5, lambda c: qkr[:, 0, c * P:(c + 1) * P], qT_done)
                        pe.wait_ge(k_rot, j + 1)
                        wait(pe, pTd_ready, 3 * m)
                        turn4(pe, 6, lambda c: qkr[:, 1, c * P:(c + 1) * P], kT_done)
                    if proj:
                        pe.wait_ge(hs_ready, n + 1)
                        for k, (done, free) in enumerate(((qp_done, qpart_ready), (kp_done, kpart_ready),
                                                          (vp_done, v_kept))):
                            wait(pe, free, n)
                            if k == 0:
                                wait(pe, sq_ready, 2 * n)
                            pe.matmul(PS[:, k, :], hs[:, u, :], wl[:, l, k * INNER:(k + 1) * INNER],
                                      start=True, stop=True).then_inc(done, 1)

                    def half_scores(c):
                        pe.wait_ge(qz_ready, j + 1)
                        pe.wait_ge(kwin_ready, j + 1)
                        wait(pe, wexp_done, H2 * j + 4 * c)
                        for h in range(4 * c, 4 * c + 4):
                            to = PS[:, 3 + h % 4 // 2, (h % 2) * 192:(h % 2) * 192 + 192]
                            pe.matmul(to, identb[:], mask[:, (i - 1) % TB, :], start=True, stop=False)
                            mm = pe.matmul(to, qz[:, h // 2, h % 2, :], kwin[:, w, h // 2, 64:256],
                                           start=False, stop=True)
                        mm.then_inc(sc_done, 1)

                    def turn_probs(c):
                        if c == 0:
                            pe.wait_ge(pn_ready, 2 * m + 1)
                            if scores:
                                pe.wait_ge(qz_ready, j + 1)
                        if c == 1 and scores:
                            pe.wait_ge(kwin_ready, j + 1)
                        if c == 2:
                            pe.wait_ge(pn_ready, 2 * m + 2)
                            pe.wait_ge(pTa_ready, m + 1)
                        if c == 3:
                            pe.wait_ge(pTd_ready, 3 * m + 1)
                        turn4(pe, 5 + c % 2, lambda k: pbuf[:, u, 2 * c + k // 2, (k % 2) * P:(k % 2 + 1) * P], pT_done)

                    def values(c):
                        if c == 0:
                            pe.wait_ge(v_kept, m + 1)
                            wait(pe, xw_ready, m)
                            pe.wait_ge(pTa_ready, m + 1)
                        else:
                            pe.wait_ge(pTd_ready, 3 * m + c)
                        for chunk in range(2):
                            v = vring[:, (r + 1 + chunk) % 4, :]
                            for k in range(2):
                                h = 2 * c + k
                                mm = pe.matmul(PS[64 * k:64 * k + 64, 7, c * P:(c + 1) * P], v[:, h * DH:(h + 1) * DH],
                                               pT[:, c % 2, k, chunk, :], start=(chunk == 0), stop=(chunk == 1))
                        mm.then_inc(pv_done, 1)

                    if output:
                        turn_probs(0)
                        turn_probs(1)
                    if scores:
                        half_scores(0)
                    if output:
                        values(0)
                        turn_probs(2)
                        values(1)
                        turn_probs(3)
                        values(2)
                        values(3)
                    if scores:
                        half_scores(1)
                    if output:
                        pe.wait_ge(oTs_ready, m + 1)
                        for c in range(PAIRS):
                            mm = pe.matmul(PS[:, 7, 0:C], oT[:, c, :], wo[:, l, c, :], start=(c == 0),
                                           stop=(c == PAIRS - 1))
                        mm.then_inc(wo_done, 1)
                tile_steps(pe, step)
                pe.wait_ge(xw_ready, (l + 1) * NT)
                fb = (2 * l + 1) * NS
                with pe.Fori(0, B) as b:
                    for h in range(2):
                        pe.wait_ge(yl_ready, fb + b * 2 + h + 1)
                        turn4(pe, 4 * h, lambda t: yl[:, h, t, :], xlT_done)
                    for h in range(2):
                        pe.wait_ge(hb_ready, l * NS + b * 2 + h + 1)
                        turn4(pe, 4 * h + 1, lambda t: hb[:, h, t * P:(t + 1) * P], hbT_done)
                    for h in range(2):
                        pe.wait_ge(xl_ready, (l + 1) * NS + b * 2 + h + 1)
                        turn4(pe, 4 * h + 2, lambda t: xl[:, h, t, :], xrT_done)
                    pe.wait_ge(n_ready, l * NS + b * 2 + 2)
                with pe.Fori(0, NS) as i:
                    for t in range(HF):
                        k = l * NS * HF + i * HF + t
                        pe.wait_ge(fgate_done, k + 1)
                        for g, done, bank in ((1, fg_done, t), (0, fa_done, 5 + t)):
                            pe.matmul(PS[:, bank, :], ff1[:, l, g, t * P:(t + 1) * P], n_all[:, bass.ds(i * 512, 512)],
                                      start=True, stop=True).then_inc(done, 1)
                    pe.wait_ge(fgate_done, l * NS * HF + i * HF + 2 * HF)
                    wait(pe, ff_added, l * NS + i + 1)
                    for t in range(4):
                        for k in range(HF):
                            mm = pe.matmul(PS[:, 4, t * P:(t + 1) * P], hf[:, k, t * P:(t + 1) * P], ff2[:, l, k, :],
                                           start=(k == 0), stop=(k == HF - 1))
                    mm.then_inc(ff_done, 1)
                if l + 1 < L2:
                    turned_inputs(yl, yl_ready, (2 * l + 2) * NS)
                    pe.wait_ge(h_ready, (2 * l + 3) * NS + 1)

        @block.vector
        def _(dve):
            for credit in (out_norm, z_ready, z_added, ff_added):
                dve.nop().then_inc(credit, 1)
            ch = Chain(dve, dve_chain, dve_settled)
            for b in range(B):
                for w, evac in enumerate((q_evac, k_evac)):
                    src, to, n = qk32[:, b % 2, w, :], parts[:, b % 2, w, :, :], 8 * b + 4 * w
                    dve.wait_ge(evac, b + 1)
                    if b >= 2:
                        dve.wait_ge(parts_stored[b - 2][w], 16)
                    dve.tensor_copy(to[:, 0, :], src).then_inc(split, 1)
                    dve.wait_ge(split, n + 1)
                    dve.tensor_tensor(res[:], src, to[:, 0, :], ALU.subtract).then_inc(split, 1)
                    dve.wait_ge(split, n + 2)
                    dve.tensor_copy(to[:, 1, :], res[:]).then_inc(split, 1)
                    dve.wait_ge(split, n + 3)
                    dve.tensor_tensor(to[:, 2, :], res[:], to[:, 1, :], ALU.subtract).then_inc(split, 1)

            def fill_v(g, u):
                src = v_all[:, g, :, :].rearrange("p t (h c) -> p t h c", h=HG)
                dve.tensor_scalar(vaug[:, u, :, :, 0:D0], src, 1.0, None, ALU.mult).then_inc(vaug_ready, 1)

            dve.wait_ge(vaug_filled, 1)
            dve.wait_ge(v_evac, 2 * B)
            fill_v(0, 0)
            fill_v(1, 1)

            def unit_max(i, use, bank):
                dve.wait_ge(ring_ready, use + 1)
                dve.tensor_reduce(mx[:, i // 2, i % 2:i % 2 + 1], PS[:, bank, :], AX.X, ALU.max)\
                   .then_inc(ring_used, 1)

            def split_max(it, u, used):
                n = (it * NBUF + u) * 5
                dve.wait_ge(ring_used, used)
                ch.link(dve.tensor_reduce(mneg[:, 0, :], mx[:], AX.X, ALU.max))
                dve.tensor_scalar(mneg[:, 1, :], mneg[:, 0, :], -1.0, None, ALU.mult).then_inc(maxsplit, 1)
                dve.wait_ge(maxsplit, n + 1)
                dve.tensor_copy(mparts[:, 0, :], mneg[:, 1, :]).then_inc(maxsplit, 1)
                dve.wait_ge(maxsplit, n + 2)
                dve.tensor_tensor(mneg[:, 2, :], mneg[:, 1, :], mparts[:, 0, :], ALU.subtract).then_inc(maxsplit, 1)
                dve.wait_ge(maxsplit, n + 3)
                dve.tensor_copy(mparts[:, 1, :], mneg[:, 2, :]).then_inc(maxsplit, 1)
                dve.wait_ge(maxsplit, n + 4)
                dve.tensor_tensor(mparts[:, 2, :], mneg[:, 2, :], mparts[:, 1, :], ALU.subtract).then_inc(maxsplit, 1)

            def keep_turned(it, u, use, bank):
                dve.wait_ge(ring_ready, use + 1)
                if not (isinstance(it, int) and it == 0 and u == 0):
                    dve.wait_ge(max_stored, 16 * (it * NBUF + u))
                dve.tensor_copy(mT[:], PS[:, bank, :].bitcast(BF16)[0:ZROWS, 0:P]).then_inc(ring_used, 1)

            for i in range(64):
                unit_max(i, i, ring_bank(i))
            split_max(0, 0, 64)
            keep_turned(0, 0, 64, ring_bank(64))
            for i in range(32):
                unit_max(i, 65 + i, ring_bank(65 + i))

            def body(it, u, used, phase, nxt, aft):
                g = it * NBUF + u
                if aft:
                    it2, u2 = later(it, u, 2)
                    dve.wait_ge(av_done, g * (2 * TB) + 1)
                    fill_v(it2 * NBUF + u2, u2)
                for n, (what, i) in enumerate(ring_uses(nxt, aft, True)):
                    bank = ring_bank(phase + n)
                    if what in ("next", "after"):
                        unit_max(i, used + n, bank)
                        if what == "next" and i == 63:
                            split_max(*later(it, u, 1), used + 32)
                    elif what == "max":
                        keep_turned(*later(it, u, 1), used + n, bank)
                    elif what == "out":
                        ps = PS[:, bank, :].rearrange("p (t h c) -> p t h c", t=4, h=HG)
                        dve.wait_ge(ring_ready, used + n + 1)
                        ch.link(dve.reciprocal(orec[:, i, :, :, :], ps[:, :, :, D0:D0 + 1]))
                        dve.tensor_tensor(o_all[:, g, i, :, :].rearrange("p t (h c) -> p t h c", h=HG),
                                          ps[:, :, :, 0:D0], orec[:, i, :, :, :].broadcast_to([P, 4, HG, D0]), ALU.mult)\
                           .then_inc(ring_used, 1)
                        dve.nop().then_inc(out_norm, 1)

            def body_chained(it, u, used, phase, nxt, aft):
                if not isinstance(it, int):
                    if u == 0:
                        ch.loop(it, NBUF * 3)
                elif u == NFULL % NBUF and it == NFULL // NBUF:
                    ch.close(NFULL // NBUF)
                body(it, u, used, phase, nxt, aft)
            attention_bodies(dve, body_chained)

            dve.wait_ge(x_loaded, 16)
            PERB = 2 * (3 + 4 + 6)
            with dve.Fori(0, B) as b:
                ch.loop(b, PERB)
                for h in range(2):
                    src = o_all[:, bass.ds(b * HG, HG), h, :, :].rearrange("p g t c -> p t g c")
                    dve.tensor_scalar(ost[:, h, :, :].rearrange("p t (g c) -> p t g c", g=HG), src, 1.0, None,
                                      ALU.mult).then_inc(ost_ready, 1)
                for h in range(2):
                    dve.wait_ge(proj_done, b * 2 + h + 1)
                    ch.link(dve.tensor_tensor(y1[:, h, :, :], PS[:, 4 * h + 1, :].rearrange("p (t c) -> p t c", t=4),
                                              x_tm[:, bass.ds(b * TB + h * 4, 4), :], ALU.add))
                    ch.link(dve.tensor_tensor(y1[:, h, :, :], y1[:, h, :, :],
                                              bp_row[:].unsqueeze(1).broadcast_to([P, 4, C]), ALU.add))
                    for t in range(4):
                        ins = dve.bn_stats(st6[:, h, t, :], y1[:, h, t, :])
                    ch.link(ins, settle=True)
                    for t in range(4):
                        ins = dve.bn_aggr(mv[:, h, t, :], st6[:, h, t, :])
                    ins.then_inc(var_ready, 1)
                for h in range(2):
                    dve.wait_ge(rstd_ready, b * 2 + h + 1)
                    for t in range(4):
                        ins = dve.tensor_scalar(xs[:, h, t, :], y1[:, h, t, :], mv[:, h, t, 0:1],
                                                rstd[:, h, t:t + 1], ALU.subtract, ALU.mult)
                    ins.then_inc(x1_ready, 1)
                for h in range(2):
                    dve.wait_ge(route_done, b * 2 + h + 1)
                    ch.link(dve.tensor_tensor(lg[:, h, :, :], PS[:, 4 * h + 3, 0:4 * NE].rearrange("p (t e) -> p t e", t=4),
                                              br_row[:].unsqueeze(1).broadcast_to([P, 4, NE]), ALU.add), settle=True)
                    for t in range(4):
                        ins = dve.max(v8[:, h, t, :], lg[:, h, t, :])
                    ch.link(ins)
                    dve.tensor_tensor(gap[:, h, :], v8[:, h, :, 1], v8[:, h, :, 0], ALU.subtract).then_inc(gap_ready, 1)
                    for t in range(4):
                        ins = dve.max_index(ix8[:, h, t, :], v8[:, h, t, :], lg[:, h, t, :])
                    ch.link(ins)
                    ch.link(dve.tensor_copy(ixf[:, h, :, :], ix8[:, h, :, 0:2]))
                for h in range(2):
                    dve.wait_ge(e2_ready, b * 2 + h + 1)
                    ch.link(dve.tensor_scalar(wpair[:, h, 2, :], e2[:, h, :], 1.0, None, ALU.add))
                    ch.link(dve.reciprocal(wpair[:, h, 0, :], wpair[:, h, 2, :]))
                    ch.link(dve.tensor_tensor(wpair[:, h, 1, :], wpair[:, h, 0, :], e2[:, h, :], ALU.mult))
                    for k in range(2):
                        ins = dve.tensor_tensor(hot[:, h, k, :, :], iota8[:].unsqueeze(1).broadcast_to([P, 4, NE]),
                                                ixf[:, h, :, k:k + 1].broadcast_to([P, 4, NE]), ALU.is_equal)
                    ch.link(ins)
                    for k in range(2):
                        ins = dve.tensor_tensor(hot[:, h, k, :, :], hot[:, h, k, :, :],
                                                wpair[:, h, k, :].unsqueeze(2).broadcast_to([P, 4, NE]), ALU.mult)
                    ch.link(ins)
                    ch.link(dve.tensor_tensor(wts[:, h, :, :], hot[:, h, 0, :, :], hot[:, h, 1, :, :], ALU.add))
                    dve.tensor_copy(w_all[:, bass.ds(b * TB + h * 4, 4), :], wts[:, h, :, :]).then_inc(wts_ready, 1)
                for h in range(2):
                    dve.wait_ge(b2_done, b * 2 + h + 1)
                    dve.tensor_tensor(x_tm[:, bass.ds(b * TB + h * 4, 4), :],
                                      PS[:, 4 * h + 1, :].rearrange("p (t c) -> p t c", t=4), xs[:, h, :, :], ALU.add)\
                       .then_inc(acc_ready, 1)
                dve.wait_ge(acc_ready, b * 2 + 2)
            ch.close(B)
            dve.nop().then_inc(moe_added, 2)
            with dve.Fori(0, NS) as i:
                for e in range(NE):
                    m = i * NE + e
                    dve.wait_ge(down_done, m + 3)
                    dve.wait_ge(moe_added, m + 2)
                    for t in range(4):
                        x = x_tm[:, i * 4 + t, :]
                        ins = dve.scalar_tensor_tensor(out=x, in0=PS[:, 4 + e % 2, t * P:(t + 1) * P],
                                                       scalar=w_all[:, i * 4 + t, e:e + 1], in1=x,
                                                       op0=ALU.mult, op1=ALU.add)
                    ins.then_inc(moe_added, 1)
            dve.wait_ge(mid_loaded, 16 * 7)
            dve.wait_ge(tanh_ready, 1)
            with dve.Fori(0, B) as b:
                ch.loop(b, 23)
                for h in range(2):
                    dve.wait_ge(yin_ready, b * 2 + h + 1)
                    norm_stats(dve, ch, yin[:, h, :, :], st6d, mvd, h, var2_ready)
                for h in range(2):
                    dve.wait_ge(rstd2_ready, b * 6 + h + 1)
                    for t in range(4):
                        ins = dve.tensor_scalar(x2[:, h, t, :], yin[:, h, t, :], mvd[:, h, t, 0:1],
                                                rsd[:, h, t:t + 1], ALU.subtract, ALU.mult)
                    ch.link(ins)
                    norm_stats(dve, ch, x2[:, h, :, :], st6d, mvd, h, var2_ready, sqd)
                for h in range(2):
                    dve.wait_ge(rstd2_ready, b * 6 + 2 + h + 1)
                    for t in range(4):
                        ins = dve.tensor_scalar(xr[:, h, t, :], x2[:, h, t, :], rsd[:, h, t:t + 1], None, ALU.mult)
                    ins.then_inc(xr_ready, 1)
                for h in range(2):
                    dve.wait_ge(xrT_done, b * 2 + h + 1)
                    ins = dve.tensor_scalar(u_cm[:, h * 512:h * 512 + 512], PS[:, 4 * h, :], cols1[:, 2:3], cols1[:, 1:2],
                                            ALU.mult, ALU.mult)
                ch.link(ins)
                dve.tensor_tensor_scan(y_cm[:], a_tanh[:].broadcast_to([P, N]), u_cm[:], 0.0, ALU.mult, ALU.add)\
                   .then_inc(scanned, 1)
                for h in range(2):
                    dve.wait_ge(ssm_done, b * 2 + h + 1)
                    ch.link(dve.tensor_tensor(x3[:, h, :, :], four(4 * h + 1), x2[:, h, :, :], ALU.add))
                    ch.link(dve.tensor_tensor(x3[:, h, :, :], x3[:, h, :, :], every4(ob_row[:]), ALU.add))
                    norm_stats(dve, ch, x3[:, h, :, :], st6d, mvd, h, var2_ready, sqd)
                for h in range(2):
                    dve.wait_ge(rstd2_ready, b * 6 + 4 + h + 1)
                    for t in range(4):
                        ins = dve.tensor_scalar(xr[:, h, t, :], x3[:, h, t, :], rsd[:, h, t:t + 1], None, ALU.mult)
                    ins.then_inc(xr_ready, 1)
                for h in range(2):
                    ch.link(dve.tensor_tensor(x2[:, h, :, :], x2[:, h, :, :], x3[:, h, :, :], ALU.add))
                    dve.tensor_tensor(x_tm[:, bass.ds(b * TB + h * 4, 4), :], x2[:, h, :, :], every4(w3b_row[:]), ALU.add)\
                       .then_inc(z_ready, 1)
                for h in range(2):
                    dve.wait_ge(xrT2_done, b * 2 + h + 1)
                    dve.tensor_scalar(x_n[:, bass.ds(b * N + h * 512, 512)], PS[:, 4 * h + 2, :], cols1[:, 3:4], None,
                                      ALU.mult).then_inc(xn_ready, 1)
                dve.wait_ge(z_ready, b * 2 + 2 + 1)
            ch.close(B)
            dve.nop().then_inc(gate_done, 2)
            with dve.Fori(0, NS) as i:
                for t in range(H1):
                    dve.wait_ge(u_done, i * H1 + t + 1)
                    dve.wait_ge(silu_done, i * H1 + t + 1)
                    dve.wait_ge(mlp_done, i + 1)
                    dve.scalar_tensor_tensor(out=hm[:, t, :], in0=PS[:, 2 + t % 2, :], scalar=gu_b[:, 0, t:t + 1],
                                             in1=sg[:, t % 2, :], op0=ALU.add, op1=ALU.mult).then_inc(gate_done, 1)
                dve.wait_ge(mlp_done, i + 2)
                x = x_tm[:, bass.ds(i * 4, 4), :]
                dve.tensor_tensor(x, four(4), x, ALU.add).then_inc(z_added, 1)
            dve.wait_ge(z_added, NS + 1)
            ch.link(dve.memset(h_all[64:P, :, 0:1], 0.0))
            with dve.Fori(0, B) as b:
                ch.loop(b, 2)
                for h in range(2):
                    dve.wait_ge(yl_ready, b * 2 + h + 1)
                    norm_stats(dve, ch, yl[:, h, :, :], st6l, mvl, h, var3_ready)
                for h in range(2):
                    dve.wait_ge(rstd3_ready, b * 2 + h + 1)
                    for t in range(4):
                        ins = dve.tensor_scalar(xl[:, h, t, :], yl[:, h, t, :], mvl[:, h, t, 0:1],
                                                rsl[:, h, t:t + 1], ALU.subtract, ALU.mult)
                    ins.then_inc(xl_ready, 1)
                dve.wait_ge(xl_ready, b * 2 + 2)
                for h in range(2):
                    for to in (x5, x_tm):
                        dve.tensor_scalar(to[:, bass.ds(b * TB + h * 4, 4), :], xl[:, h, :, :], 1.0, None, ALU.mult)\
                           .then_inc(kept, 1)
                dve.wait_ge(kept, b * 4 + 4)
            ch.close(B)
            dve.wait_ge(late_loaded, 16 * 10)
            dve.wait_ge(late_filled, 1)
            for l in range(L2):
                for k in range(2):
                    qs = qks[:, l, k, :]
                    ins = dve.tensor_tensor(rotl[:, 2 * k, :, :], rot[:, 2 * k, :, :],
                                            qs.unsqueeze(1).broadcast_to([P, TB, DH]), ALU.mult)
                    for a, b2 in ((0, 32), (32, 0)):
                        ins = dve.tensor_tensor(rotl[:, 2 * k + 1, :, a:a + 32], rot[:, 2 * k + 1, :, a:a + 32],
                                                qs[:, b2:b2 + 32].unsqueeze(1).broadcast_to([P, TB, 32]), ALU.mult)
                ch.link(ins)

                def step(i, r, proj, scores, output):
                    n, u = l * NT + i, r % 2
                    j, m, w = n - 1, n - 2, 1 - u

                    def parts(k, ready, rotated):
                        dve.wait_ge(sq_ready, 2 * n + k + 1)
                        wait(dve, rotated, n)
                        src = PS[:, k, :].rearrange("p (h c) -> p h c", h=H2)
                        a, b2 = (prod[:, k, x, :].rearrange("p (h c) -> p h c", h=H2) for x in range(2))
                        dve.tensor_tensor(a, src, rotl[:, 2 * k, i % TB, :].unsqueeze(1).broadcast_to([P, H2, DH]),
                                          ALU.mult)
                        for to, of in ((0, 32), (32, 0)):
                            ins = dve.tensor_tensor(b2[:, :, to:to + 32], src[:, :, of:of + 32],
                                                    rotl[:, 2 * k + 1, i % TB, to:to + 32].unsqueeze(1)
                                                    .broadcast_to([P, H2, 32]), ALU.mult)
                        ins.then_inc(ready, 1)

                    def turned_probs(c):
                        dve.wait_ge(pT_done, 4 * m + c + 1)
                        wait(dve, pv_done, 4 * m + c - 1)
                        dve.tensor_copy(pT[:, c % 2, :, :, :].rearrange("p a b c -> p (a b c)"), PS[:, 5 + c % 2, :])\
                           .then_inc(pTd_ready, 1)

                    def half_max(c):
                        hh = slice(4 * c, 4 * c + 4)
                        dve.wait_ge(sc_done, 2 * j + c + 1)
                        dve.wait_ge(rqk_ready, j + 1)
                        ch.link(dve.tensor_reduce(mx2[:, w, hh], PS[:, 3:5, 0:384].rearrange("p b (h k) -> p b h k", h=2),
                                                  AX.X, ALU.max))
                        dve.scalar_tensor_tensor(out=nb[:, w, hh], in0=mx2[:, w, hh], scalar=-1.0,
                                                 in1=rqk[:, w, 0, hh], op0=ALU.mult, op1=ALU.mult)\
                           .then_inc(max_ready, 1)

                    def half_norm(c):
                        hh = slice(4 * c, 4 * c + 4)
                        dve.wait_ge(wexp_done, H2 * j + 4 * c + 4)
                        ch.link(dve.reciprocal(rrec[:, w, hh], rsum[:, w, hh]))
                        p = pbuf[:, w, hh, 64:256]
                        dve.tensor_tensor(p, p, rrec[:, w, hh].unsqueeze(2).broadcast_to([P, 4, 192]), ALU.mult)\
                           .then_inc(pn_ready, 1)

                    if scores:
                        dve.wait_ge(kT_done, j + 1)
                        wait(dve, sc_done, 2 * j)
                        src = PS[:, 6, :].rearrange("p (c t) -> p c t", c=PAIRS)
                        dve.tensor_copy(kwin[:, w, :, 128:256], src)
                        dve.tensor_copy(kwin[:, u, :, 64:128], src[:, :, 64:128]).then_inc(kwin_ready, 1)
                    if proj:
                        parts(0, qpart_ready, q_rot)
                        parts(1, kpart_ready, k_rot)
                    if output:
                        turned_probs(1)
                    if proj:
                        for k in range(2):
                            dve.tensor_reduce(ssq[:, u, k, :], sqb[:, k, :].rearrange("p (h c) -> p h c", h=H2),
                                              AX.X, ALU.add).then_inc(ssq_ready, 1)
                    if scores:
                        half_max(0)
                    if output:
                        turned_probs(2)
                        turned_probs(3)
                    if scores:
                        half_norm(0)
                        half_max(1)
                    if output:
                        dve.wait_ge(wo_done, m + 1)
                        x = x_tm[:, i - 2, :]
                        dve.tensor_tensor(x, PS[:, 7, 0:C], x, ALU.add).then_inc(xw_ready, 1)
                    if scores:
                        half_norm(1)
                tile_steps(dve, step, ch, 4)
                dve.wait_ge(xw_ready, (l + 1) * NT)
                vb = (l + 1) * NS
                with dve.Fori(0, B) as b:
                    ch.loop(b, 2)
                    for h in range(2):
                        dve.wait_ge(hbT_done, l * NS + b * 2 + h + 1 + 1)
                        norm_stats(dve, ch, four(4 * h + 1), st6l, mvl, h, var3_ready)
                    for h in range(2):
                        dve.wait_ge(rstd3_ready, vb + b * 2 + h + 1)
                        for t in range(4):
                            ins = dve.tensor_scalar(xl[:, h, t, :], four(4 * h + 1)[:, t, :], mvl[:, h, t, 0:1],
                                                    rsl[:, h, t:t + 1], ALU.subtract, ALU.mult)
                        ins.then_inc(xl_ready, 1)
                    for h in range(2):
                        dve.wait_ge(xrT_done, NS + l * NS + b * 2 + h + 1)
                        dve.tensor_scalar(n_all[:, bass.ds(b * N + h * 512, 512)], PS[:, 4 * h + 2, :],
                                          lgb[:, 0, l:l + 1], lgb[:, 1, l:l + 1], ALU.mult, ALU.add).then_inc(n_ready, 1)
                ch.close(B)
                if l == 0:
                    dve.nop().then_inc(fgate_done, HF)
                with dve.Fori(0, NS) as i:
                    ch.loop(i, 1)
                    for t in range(HF):
                        k = l * NS * HF + i * HF + t
                        dve.wait_ge(fa_done, k + 1)
                        dve.wait_ge(gelu_done, k + 1)
                        wait(dve, ff_done, l * NS + i + 1)
                        dve.scalar_tensor_tensor(out=hf[:, t, :], in0=PS[:, 5 + t, :], scalar=ffb1[:, l, 0, t:t + 1],
                                                 in1=sgf[:, t, :], op0=ALU.add, op1=ALU.mult).then_inc(fgate_done, 1)
                    dve.wait_ge(ff_done, l * NS + i + 1 + 1)
                    x = x_tm[:, bass.ds(i * 4, 4), :]
                    ch.link(dve.tensor_tensor(x, four(4), x, ALU.add))
                    dve.tensor_tensor(x, x, every4(ffb2[:, l, :]), ALU.add).then_inc(ff_added, 1)
                ch.close(NS)
            dve.wait_ge(ff_added, L2 * NS + 1)
            with dve.Fori(0, B) as b:
                ch.loop(b, 2 + 2)
                for h in range(2):
                    at_x = bass.ds(b * TB + h * 4, 4)
                    ch.link(dve.tensor_tensor(yl[:, h, :, :], x_tm[:, at_x, :], x5[:, at_x, :], ALU.add))
                    norm_stats(dve, ch, yl[:, h, :, :], st6l, mvl, h, var3_ready)
                for h in range(2):
                    dve.wait_ge(rstd3_ready, (L2 + 1) * NS + b * 2 + h + 1)
                    for t in range(4):
                        ins = dve.tensor_scalar(x_tm[:, b * TB + h * 4 + t, :], yl[:, h, t, :], mvl[:, h, t, 0:1],
                                                rsl[:, h, t:t + 1], ALU.subtract, ALU.mult)
                    ins.then_inc(kept, 1)
                dve.wait_ge(kept, LNS + b * 2 + 2)
            ch.close(B)


def shape_constants():
    q = np.arange(P)[:, None]
    k = np.arange(192)[None, :]
    inside = (k >= q) & (k <= q + WINDOW)
    mask = np.zeros((P, TB, 192), np.float32)
    mask[:] = np.where(inside, 0.0, MASKED)[:, None, :]
    mask[:, 0, :] = np.where(inside & (k >= WINDOW), 0.0, MASKED)
    f = np.float32
    half = np.arange(0, DH, 2, dtype=f)
    inv = (f(1.0) / np.power(f(10000.0), half / f(DH))).astype(f)
    t = np.arange(N, dtype=f)
    ang = t[:, None] * inv[None, :]
    base = (half + f(0.4 * DH)) / f(1.4 * DH)
    power = (t - f(N // 2)) / f(WINDOW // 2)
    scale = np.power(base[None, :], power[:, None]).astype(f)
    cos, sin = np.cos(ang), np.sin(ang)
    rows = [np.concatenate([cos * scale] * 2, 1), np.concatenate([-sin * scale, sin * scale], 1),
            np.concatenate([cos / scale] * 2, 1), np.concatenate([-sin / scale, sin / scale], 1)]
    rot = np.stack(rows).reshape(4, TB, P, DH).transpose(2, 0, 1, 3)
    return mask, np.ascontiguousarray(rot.astype(f)), np.arange(NE, dtype=f)


def build(nc, aps, out):
    d = dict(aps)
    mask, rot, iota = shape_constants()
    d["mask"] = nc.inline_tensor((mask.view(np.uint32) >> 16).astype(np.uint16), name="window_mask")[:].bitcast(BF16)
    d["rot"] = nc.inline_tensor(rot, name="rotation")[:]
    d["iota8"] = nc.inline_tensor(iota, name="expert_numbers")[:]
    network_kernel(nc, d, out)


def layout(i):
    hid = DIMF

    def padded(a, n):
        z = np.zeros(a.shape[:-1] + (n,), a.dtype)
        z[..., :a.shape[-1]] = a
        return z
    a = {}
    x = i["L0_attn_x"].reshape(T, C)
    a["x_tm"] = x.reshape(NT, P, C).transpose(1, 0, 2)
    a["x_cm"] = x.T
    a["w_qkv"], a["w_proj"], a["b_proj"] = i["L0_attn_w_qkv"], i["L0_attn_w_proj"], i["L0_attn_b_proj"]
    a["w_router"], a["b_router"] = i["L0_ffn_W_router"], i["L0_ffn_b_router"]
    a["moe_w1"] = i["L0_ffn_W1"].transpose(1, 0, 2)
    a["moe_b1"] = i["L0_ffn_b1"].reshape(NE * HE, P).T
    a["moe_w2"] = i["L0_ffn_W2"].reshape(NE, HE, P, C).transpose(2, 0, 1, 3)
    a["moe_b2"] = i["L0_ffn_b2"]
    a["cols1"] = np.stack([i["L1_attn_a"], i["L1_attn_b"], i["L1_attn_n1_w"], i["L1_attn_n2_w"]], axis=1)
    a["out_w"], a["out_b"] = i["L1_attn_out_w"].T, i["L1_attn_out_b"]
    a["w1_w"], a["w2_w"] = i["L1_attn_w1_w"].T, i["L1_attn_w2_w"].T
    a["w3_w"] = i["L1_attn_w3_w"].T.reshape(H1, P, C).transpose(1, 0, 2)
    a["w3_b"] = i["L1_attn_w3_b"]
    a["gu_b"] = np.stack([i["L1_attn_w1_b"].reshape(H1, P).T, i["L1_attn_w2_b"].reshape(H1, P).T], axis=1)
    a["wqkv"] = i["L1_ffn_wqkv"].transpose(1, 0, 2)
    a["wo"] = i["L1_ffn_wo"].reshape(L2, PAIRS, P, C).transpose(2, 0, 1, 3)
    a["ff1"] = padded(i["L1_ffn_w1"].transpose(1, 0, 2).reshape(C, L2, 2, hid), HF * P)
    a["ff2"] = padded(i["L1_ffn_w2"].transpose(0, 2, 1), HF * P).reshape(L2, C, HF, P).transpose(3, 0, 2, 1)
    a["ffb1"] = padded(i["L1_ffn_b1"].reshape(L2, 2, hid), HF * P).reshape(L2, 2, HF, P).transpose(3, 0, 1, 2)
    a["ffb2"] = i["L1_ffn_b2"]
    a["lgb"] = np.stack([i["L1_ffn_ln_g"].T, i["L1_ffn_ln_b"].T], axis=1)
    a["qks"] = np.stack([i["L1_ffn_q_scale"], i["L1_ffn_k_scale"]], axis=1)
    return a


def kernel(**inputs):
    import numpy as _np
    import concourse.bacc as _bacc
    from concourse import mybir as _mybir
    from concourse.bass_utils import run_bass_kernel_spmd as _run

    nc = _bacc.Bacc("TRN2", target_bir_lowering=False, num_devices=1)
    arrays, aps = {}, {}
    for name, a in layout({k: _np.asarray(v) for k, v in inputs.items()}).items():
        a = _np.ascontiguousarray(a)
        arrays[f"in_{name}"] = a
        aps[name] = nc.dram_tensor(f"in_{name}", a.shape, _mybir.dt.from_np(a.dtype), kind="ExternalInput").ap()
    out = nc.dram_tensor("out_tokens", [P, NT, C], F32, kind="ExternalOutput").ap()
    build(nc, aps, out)
    r = _run(nc, [arrays], core_ids=[0])
    return r.results[0]["out_tokens"].transpose(1, 0, 2).reshape(B, N, C)
```

```python
from contextlib import ExitStack

import numpy as np

import concourse.bass as bass
from concourse import mybir

ALU = mybir.AluOpType
ACT = mybir.ActivationFunctionType
AX = mybir.AxisListType
F32 = mybir.dt.float32
BF16 = mybir.dt.bfloat16
U32 = mybir.dt.uint32

P = 128
B, N, C = 4, 1024, 128
T = B * N
NT = T // P
NS = T // 512
TB = N // P

H0, D0, G0 = 16, 8, 8
HG = 4
NG = B * H0 // HG
TERMS = 9 * D0
ZROWS = 96
SROWS = ZROWS + 3
NBUF = 3

NE, FE = 8, 512
HE = FE // P

HID1 = 512
H1 = HID1 // P

L2, H2, DH, WINDOW = 2, 8, 64, 64
INNER = H2 * DH
PAIRS = H2 // 2
DIMF = 341
HF = -(-DIMF // P)
QK_SCALE = 8.0
MASKED = -1e30
LNS = 2 * NS

EPS = 1e-5




class Chain:

    def __init__(self, eng, sem, settled):
        self.settled = settled
        self.eng, self.sem, self.base, self.n, self.done = eng, sem, 0, 0, 0

    def loop(self, turn, per):
        self.done += self.n
        self.base, self.n, self.per = self.done + turn * per, 0, per

    def close(self, turns):
        assert self.n == self.per, (self.n, self.per)
        self.done += turns * self.per
        self.base, self.n = self.done, 0

    def link(self, ins, settle=False):
        self.n += 1
        ins.then_inc(self.sem, 1)
        self.eng.wait_ge(self.sem, self.base + self.n)
        if settle:
            self.settle()

    def settle(self):
        self.eng.nop().then_inc(self.settled, 1)


def ring_uses(second, first, outputs):
    uses = []
    if second:
        uses += [("next", 32 + i) for i in range(32)]
    rest = [("after", i) for i in range(32)] if first else []
    if second:
        uses += rest[:16] + [("max", 0)] + rest[16:]
    if outputs:
        uses += [("out", 0), ("out", 1)]
    return uses


def network_kernel(nc, d, out):
    ctx = ExitStack()
    with ctx:
        def sem(name):
            return ctx.enter_context(nc.semaphore(name))

        def sems(names):
            return [sem(name) for name in names.split()]

        def sb(name, shape, dt=F32, at=ctx):
            return at.enter_context(nc.sbuf_tensor(name, shape, dt))

        PS = ctx.enter_context(nc.psum_tensor("PS", [P, 8, 512], F32))

        parts_dram = nc.dram_tensor("parts_dram", [2, 3, B * P, N], BF16, kind="Internal").ap()
        max_dram = nc.dram_tensor("max_dram", [NBUF, 3, HG * N], BF16, kind="Internal").ap()

        x_tm = sb("x_tm", [P, NT, C])
        ident = sb("ident", [P, P])
        identb = sb("identb", [P, P], BF16)
        o_all = sb("o_all", [P, NG, 2, HG, HG * D0])
        neghalf = sb("neghalf", [P, 8])
        wq_bd = sb("wq_bd", [P, 3 * C])
        wp_bd = sb("wp_bd", [P, C])
        bp_row = sb("bp_row", [P, C])
        wr = sb("wr", [P, NE])
        br_row = sb("br_row", [P, NE])
        b2s = sb("b2s", [NE, C])
        iota8 = sb("iota8", [P, NE])
        cols1 = sb("cols1", [P, 4])
        a_tanh = sb("a_tanh", [P, 1])
        onward = sb("onward", [P, P])
        carry = sb("carry", [P, P])
        b1c = sb("b1c", [P, NE * HE])

        at = ExitStack()
        v_all = sb("v_all", [P, NG, TB, HG * D0], at=at)
        vaug = sb("vaug", [P, NBUF, TB, HG, 32], at=at)
        qst = sb("qst", [P, NBUF, HG, N], BF16, at=at)
        kst = sb("kst", [P, NBUF, HG, N], BF16, at=at)
        osb = sb("osb", [P, N], at=at)
        mx = sb("mx", [P, HG * TB, 2], at=at)
        mneg = sb("mneg", [P, 4, HG * TB], at=at)
        mparts = sb("mparts", [P, 3, HG * TB], BF16, at=at)
        mT = sb("mT", [ZROWS, P], BF16, at=at)
        orec = sb("orec", [P, 2, HG, HG, 1], at=at)
        pre = ExitStack()
        xcm = sb("xcm", [P, T], at=pre)
        qk32 = sb("qk32", [P, 2, 2, N], at=pre)
        parts = sb("parts", [P, 2, 2, 3, N], BF16, at=pre)
        res = sb("res", [P, N], at=pre)
        pre.close()
        probs = sb("probs", [P, 2, HG, N], at=at)
        at.close()

        rt = ExitStack()
        x_cm = sb("x_cm", [P, T], at=rt)
        w_all = sb("w_all", [P, NT, NE], at=rt)
        w1s = sb("w1s", [P, NE, FE], at=rt)
        w2s = sb("w2s", [P, NE, HE, C], at=rt)
        hid = sb("hid", [P, 2, HE, 512], at=rt)
        pj = ExitStack()
        ost = sb("ost", [P, 2, 4, C], at=pj)
        ocm = sb("ocm", [P, 2, 512], at=pj)
        y1 = sb("y1", [P, 2, 4, C], at=pj)
        xs = sb("xs", [P, 2, 4, C], at=pj)
        xc = sb("xc", [P, 2, 512], at=pj)
        st6 = sb("st6", [P, 2, 4, 6], at=pj)
        mv = sb("mv", [P, 2, 4, 2], at=pj)
        rstd = sb("rstd", [P, 2, 4], at=pj)
        lg = sb("lg", [P, 2, 4, NE], at=pj)
        v8 = sb("v8", [P, 2, 4, 8], at=pj)
        ix8 = sb("ix8", [P, 2, 4, 8], U32, at=pj)
        ixf = sb("ixf", [P, 2, 4, 2], at=pj)
        gap = sb("gap", [P, 2, 4], at=pj)
        e2 = sb("e2", [P, 2, 4], at=pj)
        wpair = sb("wpair", [P, 2, 3, 4], at=pj)
        hot = sb("hot", [P, 2, 2, 4, NE], at=pj)
        wts = sb("wts", [P, 2, 4, NE], at=pj)
        wT = sb("wT", [NE, 2, 512], at=pj)
        pj.close()
        rt.close()
        dd = ExitStack()
        x_n = sb("x_n", [P, T], at=dd)
        ow = sb("ow", [P, C], at=dd)
        ob_row = sb("ob_row", [P, C], at=dd)
        w3b_row = sb("w3b_row", [P, C], at=dd)
        wu = sb("wu", [P, HID1], at=dd)
        wg = sb("wg", [P, HID1], at=dd)
        w3 = sb("w3", [P, H1, C], at=dd)
        gu_b = sb("gu_b", [P, 2, H1], at=dd)
        yin = sb("yin", [P, 2, 4, C], at=dd)
        x2 = sb("x2", [P, 2, 4, C], at=dd)
        x3 = sb("x3", [P, 2, 4, C], at=dd)
        xr = sb("xr", [P, 2, 4, C], at=dd)
        st6d = sb("st6d", [P, 2, 4, 6], at=dd)
        mvd = sb("mvd", [P, 2, 4, 2], at=dd)
        sqd = sb("sqd", [P, 2, 4], at=dd)
        rsd = sb("rsd", [P, 2, 4], at=dd)
        u_cm = sb("u_cm", [P, N], at=dd)
        y_cm = sb("y_cm", [P, N], at=dd)
        sg = sb("sg", [P, 2, 512], at=dd)
        hm = sb("hm", [P, H1, 512], at=dd)
        dd.close()

        lo = ExitStack()
        x5 = sb("x5", [P, NT, C], at=lo)
        h_all = sb("h_all", [P, B, N + 1], at=lo)
        n_all = o_all[:].rearrange("p g a t c -> p (g a t c)")
        wl = sb("wl", [P, L2, 3 * INNER], at=lo)
        wo = sb("wo", [P, L2, PAIRS, C], at=lo)
        ff1 = sb("ff1", [P, L2, 2, HF * P], at=lo)
        ff2 = sb("ff2", [P, L2, HF, C], at=lo)
        ffb1 = sb("ffb1", [P, L2, 2, HF], at=lo)
        ffb2 = sb("ffb2", [P, L2, C], at=lo)
        lgb = sb("lgb", [P, 2, L2], at=lo)
        mask = sb("mask", [P, TB, 192], BF16, at=lo)
        rot = sb("rot", [P, 4, TB, DH], at=lo)
        rotl = sb("rotl", [P, 4, TB, DH], at=lo)
        qks = sb("qks", [P, L2, 2, DH], at=lo)
        yl = sb("yl", [P, 2, 4, C], at=lo)
        xl = sb("xl", [P, 2, 4, C], at=lo)
        st6l = sb("st6l", [P, 2, 4, 6], at=lo)
        mvl = sb("mvl", [P, 2, 4, 2], at=lo)
        rsl = sb("rsl", [P, 2, 4], at=lo)
        la = ExitStack()
        hs = sb("hs", [P, 2, P], at=la)
        sqb = sb("sqb", [P, 2, INNER], at=la)
        ssq = sb("ssq", [P, 2, 2, H2], at=la)
        rin = sb("rin", [P, 2, H2], at=la)
        rqk = sb("rqk", [P, 2, 2, H2], at=la)
        prod = sb("prod", [P, 2, 2, INNER], at=la)
        ksum = sb("ksum", [P, INNER], at=la)
        qkr = sb("qkr", [P, 2, INNER], at=la)
        vring = sb("vring", [P, 4, INNER], at=la)
        qz = sb("qz", [P, PAIRS, 2, P], at=la)
        kwin = sb("kwin", [P, 2, PAIRS, 256], at=la)
        mx2 = sb("mx2", [P, 2, H2], at=la)
        nb = sb("nb", [P, 2, H2], at=la)
        rsum = sb("rsum", [P, 2, H2], at=la)
        rrec = sb("rrec", [P, 2, H2], at=la)
        pbuf = sb("pbuf", [P, 2, H2, 256], at=la)
        pT = sb("pT", [P, 2, 2, 2, P], at=la)
        oT = sb("oT", [P, PAIRS, P], at=la)
        la.close()
        sgf = sb("sgf", [P, HF, 512], at=lo)
        hf = sb("hf", [P, HF, 512], at=lo)
        lo.close()


        (const_ready, blocks_zeroed, weights_loaded, x_loaded) = \
            sems("const_ready blocks_zeroed weights_loaded x_loaded")
        (q_done, k_done, v_done, q_evac, k_evac, v_evac, split) = \
            sems("q_done k_done v_done q_evac k_evac v_evac split")
        (rows_filled, vaug_filled, vaug_ready) = \
            sems("rows_filled vaug_filled vaug_ready")
        (st_ready, exp_done, av_done, o_evac, ring_ready, ring_used, maxsplit, max_stored, out_norm) = \
            sems("st_ready exp_done av_done o_evac ring_ready ring_used maxsplit max_stored out_norm")
        attn_done = sem("attn_done")
        (ost_ready, oT_done, ocm_ready, proj_done, sum_ready, var_ready, rstd_ready, x1_ready, x1T_done) = \
            sems("ost_ready oT_done ocm_ready proj_done sum_ready var_ready rstd_ready x1_ready x1T_done")
        (xc_ready, route_done, gap_ready, e2_ready, wts_ready, wT_done, wT_ready, b2_done, acc_ready) = \
            sems("xc_ready route_done gap_ready e2_ready wts_ready wT_done wT_ready b2_done acc_ready")
        (cm_ready, experts_loaded, out_stored) = \
            sems("cm_ready experts_loaded out_stored")
        (dve_chain, pool_chain, dve_settled, pool_settled) = \
            sems("dve_chain pool_chain dve_settled pool_settled")
        act_settled = sem("act_settled")
        (up_done, relu_done, down_done, moe_added) = \
            sems("up_done relu_done down_done moe_added")
        (mid_loaded, yin_ready, var2_ready, rstd2_ready, xr_ready, xrT_done, u_ready, scanned, ssm_done) = \
            sems("mid_loaded yin_ready var2_ready rstd2_ready xr_ready xrT_done u_ready scanned ssm_done")
        (x3_done, xrT2_done, xn_ready, z_ready, tanh_ready) = \
            sems("x3_done xrT2_done xn_ready z_ready tanh_ready")
        (g_done, u_done, silu_done, gate_done, mlp_done, z_added) = \
            sems("g_done u_done silu_done gate_done mlp_done z_added")
        (late_loaded, yl_ready, var3_ready, rstd3_ready, xl_ready, xlT_done, h_ready, kept) = \
            sems("late_loaded yl_ready var3_ready rstd3_ready xl_ready xlT_done h_ready kept")
        (late_filled, hs_ready, qp_done, kp_done, vp_done, sq_ready, ssq_ready, rqk_ready) = \
            sems("late_filled hs_ready qp_done kp_done vp_done sq_ready ssq_ready rqk_ready")
        (qpart_ready, kpart_ready, q_rot, k_rot, qT_done, kT_done, qz_ready, kwin_ready) = \
            sems("qpart_ready kpart_ready q_rot k_rot qT_done kT_done qz_ready kwin_ready")
        (v_kept, sc_done, max_ready, wexp_done, pn_ready, pT_done, pTa_ready, pTd_ready) = \
            sems("v_kept sc_done max_ready wexp_done pn_ready pT_done pTa_ready pTd_ready")
        (pv_done, oTs_ready, wo_done, xw_ready) = \
            sems("pv_done oTs_ready wo_done xw_ready")
        (moved_done, n_ready, fg_done, fa_done, gelu_done, fgate_done, ff_done, ff_added) = \
            sems("moved_done n_ready fg_done fa_done gelu_done fgate_done ff_done ff_added")
        stack_loaded = [sem(f"stack_loaded{i}") for i in range(NBUF)]
        xcm_loaded = [sem(f"xcm_loaded{b}") for b in range(B)]
        parts_stored = [[sem(f"parts_stored{b}_{w}") for w in "qk"] for b in range(B)]
        maxrow_loaded = [sem(f"maxrow_loaded{i}") for i in range(NBUF)]
        LOADS = 18 * 16
        PRE_USES = 64 + 1 + 32
        RING, VALUES = 5, 3
        BODY_USES = len(ring_uses(True, True, True))
        NFULL = NG - 4
        WEIGHTS = 16 * (2 * G0 + 7)

        def later(it, u, k):
            return it + (u + k) // NBUF, (u + k) % NBUF

        def ring_base(g):
            n = PRE_USES
            for i in range(g):
                n += len(ring_uses(i + 1 < NG, i + 2 < NG, True))
            return n

        def ring_bank(use):
            return RING + use % 3

        def score_bank(u, kt, i):
            return ((u * TB + kt) * (2 * HG) + i) % 3

        def attention_bodies(eng, body):
            def three(it):
                for u in range(NBUF):
                    used = PRE_USES + u * BODY_USES
                    body(it, u, used + it * (NBUF * BODY_USES), used % 3, True, True)
            with eng.Fori(0, NFULL // NBUF) as it:
                three(it)
            for g in range(NFULL, NG):
                body(g // NBUF, g % NBUF, ring_base(g), ring_base(g) % 3, g + 1 < NG, g + 2 < NG)

        def norm_stats(dve, ch, src, st, mvx, h, ready, square=None):
            for t in range(4):
                ins = dve.bn_stats(st[:, h, t, :], src[:, t, :])
            ch.link(ins, settle=True)
            for t in range(4):
                ins = dve.bn_aggr(mvx[:, h, t, :], st[:, h, t, :])
            if square is not None:
                ch.link(ins)
                ch.link(dve.tensor_tensor(square[:, h, :], mvx[:, h, :, 0], mvx[:, h, :, 0], ALU.mult))
                ins = dve.tensor_tensor(mvx[:, h, :, 1], mvx[:, h, :, 1], square[:, h, :], ALU.add)
            ins.then_inc(ready, 1)

        def rstds(pool, ch, pairs, base, ready, done, mvx, r):
            def pair(i):
                ch.loop(i, 2)
                for h in range(2):
                    pool.wait_ge(ready, base + i * 2 + h + 1)
                    ch.settle()
                    ch.link(pool.tensor_scalar(r[:, h, :], mvx[:, h, :, 1], EPS, None, ALU.add))
                    pool.tensor_tensor(r[:, h, :], r[:, h, :], neghalf[:, 0:4], ALU.pow).then_inc(done, 1)
            with pool.Fori(0, pairs) as i:
                pair(i)
            ch.close(pairs)

        def turn4(pe, bank, src, done):
            for t in range(4):
                mm = pe.transpose(PS[:, bank, t * P:(t + 1) * P], src(t), ident[:])
            mm.then_inc(done, 1)

        def four(bank):
            return PS[:, bank, :].rearrange("p (t c) -> p t c", t=4)

        def every4(row):
            return row.unsqueeze(1).broadcast_to([P, 4, C])

        STEPS, TURNS, PRODUCTS = 6, 6, 7
        STEP_AFTER = {0: 0, 1: 1, 3: 2, 4: 3, 6: 4, 7: 5}

        def wide_tiles(eng, tile, ch=None, per=0):
            def both(b, last):
                tile(b, 0, (b, 1))
                tile(b, 1, None if last else (b + 1, 0))
            with eng.Fori(0, B - 1) as b:
                if ch is not None:
                    ch.loop(b, 2 * per)
                both(b, False)
            if ch is not None:
                ch.close(B - 1)
            both(B - 1, True)

        NORMED = 3

        def tile_steps(eng, step, ch=None, per=0):
            for i in range(4):
                step(i, i, True, i >= 1, i >= 2)
            with eng.Fori(0, NT // 4 - 2) as it:
                if ch is not None:
                    ch.loop(it, 4 * per)
                for r in range(4):
                    step(it * 4 + (4 + r), r, True, True, True)
            if ch is not None:
                ch.close(NT // 4 - 2)
            for i in range(NT - 4, NT + 2):
                step(i, i % 4, i < NT, i <= NT, True)

        def settle(eng):
            eng.nop().then_inc(act_settled, 1)

        def wait(eng, what, value):
            if not isinstance(value, int) or value > 0:
                eng.wait_ge(what, value)

        block = ctx.enter_context(nc.Block())

        @block.sync
        def _(sp):
            for b in range(B):
                sp.dma_start(xcm[:, b * N:(b + 1) * N], d["x_cm"][:, b * N:(b + 1) * N]).then_inc(xcm_loaded[b], 16)
                if b == 0:
                    sp.wait_ge(blocks_zeroed, 2)
                    for g in range(G0):
                        c = C // G0
                        sp.dma_start(wq_bd[g * c:(g + 1) * c, 3 * g * c:3 * (g + 1) * c], d["w_qkv"][g])\
                          .then_inc(weights_loaded, 16)
                        sp.dma_start(wp_bd[g * c:(g + 1) * c, g * c:(g + 1) * c], d["w_proj"][g])\
                          .then_inc(weights_loaded, 16)
            sp.dma_start(x_tm[:], d["x_tm"]).then_inc(x_loaded, 16)
            sp.dma_start(bp_row[:], d["b_proj"].partition_broadcast(P)).then_inc(weights_loaded, 16)
            sp.dma_start(wr[:], d["w_router"]).then_inc(weights_loaded, 16)
            sp.dma_start(br_row[:], d["b_router"].partition_broadcast(P)).then_inc(weights_loaded, 16)
            sp.dma_start(b2s[:], d["moe_b2"]).then_inc(weights_loaded, 16)
            sp.dma_start(b1c[:], d["moe_b1"]).then_inc(weights_loaded, 16)
            sp.dma_start(cols1[:], d["cols1"]).then_inc(weights_loaded, 16)
            sp.dma_start(iota8[:], d["iota8"].partition_broadcast(P)).then_inc(weights_loaded, 16)
            for b in range(B):
                for w in range(2):
                    sp.wait_ge(split, 8 * b + 4 * w + 4)
                    sp.dma_start(parts_dram[w, :, b * P:(b + 1) * P, :].rearrange("s r t -> r s t"),
                                 parts[:, b % 2, w, :, :]).then_inc(parts_stored[b][w], 16)
            for stored in parts_stored:
                for one in stored:
                    sp.wait_ge(one, 16)
            sp.wait_ge(rows_filled, 3)

            def load_stack(g, u):
                for i in range(3):
                    for j in range(3):
                        r = (3 * i + j) * D0
                        for dst, w, part in ((qst, 0, i), (kst, 1, j)):
                            src = parts_dram[w, part, bass.ds(g * (HG * D0), HG * D0), :]\
                                .rearrange("(h d) t -> d h t", d=D0)
                            sp.dma_start(dst[r:r + D0, u, :, :], src).then_inc(stack_loaded[u], 16)

            def turn_max(it, u, used):
                sp.wait_ge(ring_used, used)
                sp.dma_start(max_dram[u].rearrange("s (r t) -> (s r) t", t=P), mT[:]).then_inc(max_stored, 16)
                sp.wait_ge(max_stored, 16 * (it * NBUF + u) + 16)
                sp.dma_start(qst[ZROWS:SROWS, u, :, :], max_dram[u].rearrange("s (h t) -> s h t", h=HG))\
                  .then_inc(maxrow_loaded[u], 16)

            load_stack(0, 0)
            load_stack(1, 1)
            turn_max(0, 0, 65)

            def body(it, u, used, phase, nxt, aft):
                if aft:
                    it2, u2 = later(it, u, 2)
                    sp.wait_ge(st_ready, (it * NBUF + u) * (2 * HG * TB) + 1)
                    load_stack(it2 * NBUF + u2, u2)
                if nxt:
                    it1, u1 = later(it, u, 1)
                    turn_max(it1, u1, used + 32 + 16 * aft + 1)
            attention_bodies(sp, body)

            sp.wait_ge(out_norm, 2 * NG + 1)
            for e in range(NE):
                sp.dma_start(w1s[:, e, :], d["moe_w1"][:, e, :]).then_inc(experts_loaded, 16)
                sp.dma_start(w2s[:, e, :, :], d["moe_w2"][:, e, :, :]).then_inc(experts_loaded, 16)
            sp.wait_ge(moe_added, NS * NE + 2)
            for dst, src in ((ow[:], d["out_w"]), (ob_row[:], d["out_b"].partition_broadcast(P)),
                             (w3b_row[:], d["w3_b"].partition_broadcast(P)), (wu[:], d["w1_w"]), (wg[:], d["w2_w"]),
                             (w3[:], d["w3_w"]), (gu_b[:], d["gu_b"])):
                sp.dma_start(dst, src).then_inc(mid_loaded, 16)
            sp.wait_ge(z_added, NS + 1)
            for dst, src in ((wl[:], d["wqkv"]), (wo[:], d["wo"]), (ff1[:], d["ff1"]), (ff2[:], d["ff2"]), (ffb1[:], d["ffb1"]),
                             (ffb2[:], d["ffb2"].partition_broadcast(P)), (lgb[:], d["lgb"]), (mask[:], d["mask"]),
                             (rot[:], d["rot"]), (qks[:], d["qks"].partition_broadcast(P))):
                sp.dma_start(dst, src).then_inc(late_loaded, 16)
            sp.wait_ge(kept, LNS + NS)
            sp.dma_start(out, x_tm[:]).then_inc(out_stored, 16)
            sp.wait_ge(out_stored, 16)

        @block.gpsimd
        def _(pool):
            ch = Chain(pool, pool_chain, pool_settled)
            pool.memset(wq_bd[:], 0.0).then_inc(blocks_zeroed, 1)
            pool.memset(wp_bd[:], 0.0).then_inc(blocks_zeroed, 1)
            for t in (ident, identb):
                ch.link(pool.memset(t[:], 0.0))
                pool.affine_select(out=t[:], in_=t[:], compare_op=ALU.not_equal, fill=1.0, base=0,
                                   pattern=[[-1, P]], channel_multiplier=1).then_inc(const_ready, 1)
            pool.memset(neghalf[:], -0.5).then_inc(const_ready, 1)
            for t, base in ((onward, 1), (carry, 1 - P)):
                ch.link(pool.memset(t[:], 0.0))
                pool.affine_select(out=t[:], in_=t[:], compare_op=ALU.not_equal, fill=1.0, base=base,
                                   pattern=[[-1, P]], channel_multiplier=1).then_inc(const_ready, 1)
            ch.link(pool.memset(vaug[:], 0.0))
            ch.link(pool.memset(vaug[:, :, :, :, D0:D0 + 1], 1.0))
            pool.nop().then_inc(vaug_filled, 1)
            ch.link(pool.memset(qst[64:ZROWS, :, :, :].bitcast(F32), 0.0))
            pool.nop().then_inc(rows_filled, 1)
            ch.link(pool.memset(kst[64:ZROWS, :, :, :].bitcast(F32), 0.0))
            pool.nop().then_inc(rows_filled, 1)
            pool.memset(kst[ZROWS:SROWS, :, :, :], 1.0).then_inc(rows_filled, 1)

            PERB = 2
            with pool.Fori(0, B) as b:
                ch.loop(b, PERB)
                for h in range(2):
                    pool.wait_ge(var_ready, b * 2 + h + 1)
                    ch.settle()
                    ch.link(pool.tensor_scalar(rstd[:, h, :], mv[:, h, :, 1], EPS, None, ALU.add))
                    pool.tensor_tensor(rstd[:, h, :], rstd[:, h, :], neghalf[:, 0:4], ALU.pow)\
                        .then_inc(rstd_ready, 1)
            ch.close(B)
            rstds(pool, ch, 3 * B, 0, var2_ready, rstd2_ready, mvd, rsd)
            rstds(pool, ch, B, 0, var3_ready, rstd3_ready, mvl, rsl)
            for t in (qz, kwin, pbuf, vring):
                ch.link(pool.memset(t[:], 0.0))
            pool.nop().then_inc(late_filled, 1)
            for l in range(L2):
                def step(i, r, proj, scores, output):
                    n, u = l * NT + i, r % 2
                    if proj:
                        pool.wait_ge(qpart_ready, n + 1)
                        wait(pool, qT_done, n)
                        pool.tensor_tensor(qkr[:, 0, :], prod[:, 0, 0, :], prod[:, 0, 1, :], ALU.add).then_inc(q_rot, 1)
                        pool.wait_ge(kpart_ready, n + 1)
                        ch.link(pool.tensor_tensor(ksum[:], prod[:, 1, 0, :], prod[:, 1, 1, :], ALU.add))
                        pool.wait_ge(ssq_ready, 2 * n + 1)
                        ch.settle()
                        ch.link(pool.tensor_scalar(rin[:, 1, :], ssq[:, u, 1, :], 1e-24, None, ALU.max))
                        ch.link(pool.tensor_tensor(rqk[:, u, 1, :], rin[:, 1, :],
                                                   neghalf[:, 0:1].broadcast_to([P, H2]), ALU.pow))
                        wait(pool, kT_done, n)
                        pool.tensor_tensor(qkr[:, 1, :].rearrange("p (h c) -> p h c", h=H2),
                                           ksum[:].rearrange("p (h c) -> p h c", h=H2),
                                           rqk[:, u, 1, :].unsqueeze(2).broadcast_to([P, H2, DH]), ALU.mult)\
                            .then_inc(k_rot, 1)
                        pool.wait_ge(ssq_ready, 2 * n + 2)
                        ch.settle()
                        ch.link(pool.tensor_scalar(rin[:, 0, :], ssq[:, u, 0, :], 1e-24, 1.0 / QK_SCALE ** 2,
                                                   ALU.max, ALU.mult))
                        wait(pool, wexp_done, (n - 1) * H2)
                        pool.tensor_tensor(rqk[:, u, 0, :], rin[:, 0, :],
                                           neghalf[:, 0:1].broadcast_to([P, H2]), ALU.pow).then_inc(rqk_ready, 1)
                tile_steps(pool, step, ch, 3 + 1)
                rstds(pool, ch, B, (l + 1) * NS, var3_ready, rstd3_ready, mvl, rsl)
            rstds(pool, ch, B, (L2 + 1) * NS, var3_ready, rstd3_ready, mvl, rsl)

        @block.scalar
        def _(act):
            for credit in (o_evac, h_ready):
                act.nop().then_inc(credit, 1)
            for b in range(B):
                p2 = b % 2
                act.wait_ge(q_done, b + 1)
                if b >= 2:
                    act.wait_ge(split, 8 * (b - 2) + 8)
                act.activation(qk32[:, p2, 0, :], PS[:, 0:2, :].rearrange("p a b -> p (a b)"), ACT.Copy,
                               scale=float(D0) ** -0.5).then_inc(q_evac, 1)
                act.wait_ge(k_done, b + 1)
                act.activation(qk32[:, p2, 1, :], PS[:, 2:4, :].rearrange("p a b -> p (a b)"), ACT.Copy)\
                   .then_inc(k_evac, 1)
                act.wait_ge(v_done, b + 1)
                for t in range(2):
                    act.activation(
                        v_all[:, b * HG:(b + 1) * HG, 4 * t:4 * t + 4, :].rearrange("p g t c -> p t g c"),
                        PS[:, 4 + t, :].rearrange("p (t g c) -> p t g c", t=4, g=HG), ACT.Copy)\
                       .then_inc(v_evac, 1)

            def exps(it, u, kt):
                g = it * NBUF + u
                for i in range(2 * HG):
                    act.wait_ge(st_ready, (g * TB + kt) * (2 * HG) + i + 1)
                    if i == 0 and not (kt < 2 and isinstance(g, int) and g == 0):
                        act.wait_ge(av_done, g * (2 * TB) + 2 * kt - 2 + 1)
                    act.activation(probs[:, kt % 2, i // 2, i % 2 * 512:i % 2 * 512 + 512],
                                   PS[:, score_bank(u, kt, i), :], ACT.Exp).then_inc(exp_done, 1)

            act.wait_ge(split, 8 * B)
            for stored in parts_stored:
                for one in stored:
                    act.wait_ge(one, 16)
            exps(0, 0, 0)

            def body(it, u, used, phase, nxt, aft):
                g = it * NBUF + u
                for kt in range(1, TB):
                    exps(it, u, kt)
                if nxt:
                    exps(*later(it, u, 1), 0)
                act.wait_ge(av_done, g * (2 * TB) + 2 * TB + 1)
                act.wait_ge(out_norm, g * 2 + 1)
                for t in range(2):
                    act.activation(osb[:, 512 * t:512 * t + 512], PS[:, VALUES + t, :], ACT.Copy)\
                       .then_inc(o_evac, 1)
            attention_bodies(act, body)

            def prepare(k, b, h):
                n = b * 2 + h
                if k == 0:
                    act.wait_ge(oT_done, n + 1)
                    act.activation(ocm[:, h, :], PS[:, TURNS, :], ACT.Copy).then_inc(ocm_ready, 1)
                if k == 2:
                    act.wait_ge(x1T_done, n + 1)
                    act.activation(xc[:, h, :], PS[:, TURNS, :], ACT.Copy).then_inc(xc_ready, 1)
                    act.activation(x_cm[:, bass.ds(b * N + h * 512, 512)], PS[:, TURNS, :], ACT.Copy)\
                       .then_inc(cm_ready, 1)
                if k == 3:
                    act.wait_ge(gap_ready, n + 1)
                    act.activation(e2[:, h, :], gap[:, h, :], ACT.Exp).then_inc(e2_ready, 1)
                if k == 4:
                    act.wait_ge(wT_done, n + 1)
                    act.activation(wT[:, h, :], PS[0:NE, TURNS, :], ACT.Copy).then_inc(wT_ready, 1)
            for k in range(STEPS):
                prepare(k, 0, 0)
            act.nop().then_inc(relu_done, HE)

            def experts(b, h, after):
                for e in range(NE):
                    m = (b * 2 + h) * NE + e
                    act.wait_ge(down_done, m + 1)
                    for t in range(HE):
                        act.wait_ge(up_done, m * HE + t + 1)
                        act.activation(hid[:, e % 2, t, :], PS[:, t, :], ACT.Relu,
                                       bias=b1c[:, e * HE + t:e * HE + t + 1]).then_inc(relu_done, 1)
                    if after is not None and e - 1 in STEP_AFTER:
                        prepare(STEP_AFTER[e - 1], *after)
                if after is not None:
                    prepare(STEP_AFTER[NE - 1], *after)
            wide_tiles(act, experts)
            act.wait_ge(moe_added, NS * NE + 2)
            act.activation(a_tanh[:], cols1[:, 0:1], ACT.Tanh).then_inc(tanh_ready, 1)
            with act.Fori(0, B) as b:
                for h in range(2):
                    act.wait_ge(z_ready, b * 2 + 1)
                    settle(act)
                    act.activation(yin[:, h, :, :], x_tm[:, bass.ds(b * TB + h * 4, 4), :], ACT.Copy)\
                       .then_inc(yin_ready, 1)
            with act.Fori(0, NS) as i:
                for t in range(H1):
                    act.wait_ge(g_done, i * H1 + t + 1)
                    act.wait_ge(gate_done, i * H1 + t + 1)
                    act.activation(sg[:, t % 2, :], PS[:, t % 2, :], ACT.Silu, bias=gu_b[:, 1, t:t + 1])\
                       .then_inc(silu_done, 1)
            act.wait_ge(z_added, NS + 1)
            def to_shifted(b, h, base):
                act.wait_ge(xlT_done, base + b * 2 + h + 1 + 1)
                settle(act)
                act.activation(h_all[0:64, b, h * 512:h * 512 + 512], PS[0:64, 4 * h, :], ACT.Copy)
                act.activation(h_all[64:P, b, h * 512 + 1:h * 512 + 513], PS[64:P, 4 * h, :], ACT.Copy)\
                   .then_inc(h_ready, 1)
            with act.Fori(0, B) as b:
                for h in range(2):
                    act.wait_ge(xlT_done, b * 2 + 1)
                    settle(act)
                    act.activation(yl[:, h, :, :], x_tm[:, bass.ds(b * TB + h * 4, 4), :], ACT.Copy)\
                       .then_inc(yl_ready, 1)
                for h in range(2):
                    to_shifted(b, h, 0)
            act.wait_ge(late_filled, 1)

            def keep_tile(i, u):
                at = (i % TB) * P
                act.activation(hs[:, u, :], h_all[:, i // TB, bass.ds(at, P)], ACT.Copy).then_inc(hs_ready, 1)

            for l in range(L2):
                act.wait_ge(h_ready, (l + 1) * NS + 1)
                def step(i, r, proj, scores, output):
                    n, u = l * NT + i, r % 2
                    if scores:
                        act.wait_ge(qT_done, n)
                        wait(act, sc_done, 2 * (n - 1))
                        for k in range(2):
                            rows = slice(64 * k, 64 * k + 64)
                            ins = act.activation(qz[rows, :, k, :],
                                                 PS[rows, 5, :].rearrange("p (c t) -> p c t", c=PAIRS), ACT.Copy)
                        ins.then_inc(qz_ready, 1)
                    if proj:
                        wait(act, ssq_ready, 2 * n)
                        for k, done in enumerate((qp_done, kp_done)):
                            act.wait_ge(done, n + 1)
                            act.activation(sqb[:, k, :], PS[:, k, :], ACT.Square).then_inc(sq_ready, 1)
                        act.wait_ge(vp_done, n + 1)
                        wait(act, pv_done, 4 * (n - 2))
                        act.activation(vring[:, r, :], PS[:, 2, :], ACT.Copy).then_inc(v_kept, 1)
                        if not (isinstance(i, int) and i == NT - 1):
                            keep_tile(i + 1, 1 - u)
                    if output:
                        for c in (0, 2):
                            act.wait_ge(pT_done, 4 * (n - 2) + c + 1)
                            wait(act, pv_done, 4 * (n - 2) + c - 1)
                            act.activation(pT[:, 0, :, :, :].rearrange("p a b c -> p (a b c)"), PS[:, 5, :], ACT.Copy)\
                               .then_inc(pTa_ready, 1)
                    for c in range(2):
                        if scores:
                            j = n - 1
                            act.wait_ge(max_ready, 2 * j + c + 1)
                            if c == 0:
                                wait(act, pT_done, 4 * (j - 1))
                            for h in range(4 * c, 4 * c + 4):
                                act.activation(pbuf[:, 1 - u, h, 64:256],
                                               PS[:, 3 + h % 4 // 2, (h % 2) * 192:(h % 2) * 192 + 192], ACT.Exp,
                                               bias=nb[:, 1 - u, h:h + 1], scale=rqk[:, 1 - u, 0, h:h + 1],
                                               accum_out=rsum[:, 1 - u, h:h + 1]).then_inc(wexp_done, 1)
                        if output and c == 0:
                            act.wait_ge(pv_done, 4 * (n - 2) + 4)
                            wait(act, wo_done, n - 2)
                            act.activation(oT[:].rearrange("p c t -> p (c t)"), PS[:, 7, :], ACT.Copy)\
                               .then_inc(oTs_ready, 1)
                keep_tile(0, 0)
                tile_steps(act, step)
                with act.Fori(0, NS) as i:
                    for t in range(HF):
                        k = l * NS * HF + i * HF + t
                        act.wait_ge(fg_done, k + 1)
                        act.wait_ge(fgate_done, k + 1)
                        act.activation(sgf[:, t, :], PS[:, t, :], ACT.Gelu,
                                       bias=ffb1[:, l, 1, t:t + 1]).then_inc(gelu_done, 1)
                act.wait_ge(ff_added, (l + 1) * NS + 1)
                fb = (l + 1) * NS
                if l + 1 < L2:
                    with act.Fori(0, B) as b:
                        for h in range(2):
                            act.wait_ge(xlT_done, fb + b * 2 + 1)
                            settle(act)
                            act.activation(yl[:, h, :, :], x_tm[:, bass.ds(b * TB + h * 4, 4), :], ACT.Copy)\
                               .then_inc(yl_ready, 1)
                        for h in range(2):
                            to_shifted(b, h, fb)

        @block.tensor
        def _(pe):
            for credit in (av_done, xlT_done, ff_done):
                pe.nop().then_inc(credit, 1)
            pe.wait_ge(weights_loaded, WEIGHTS)
            pe.wait_ge(const_ready, 2)
            for b in range(B):
                pe.wait_ge(xcm_loaded[b], 16)
                for w, (done, evac) in enumerate(((q_done, q_evac), (k_done, k_evac))):
                    if b:
                        pe.wait_ge(evac, b)
                    for t in range(2):
                        mm = pe.matmul(PS[:, 2 * w + t, :], wq_bd[:, w * C:(w + 1) * C],
                                       xcm[:, b * N + 512 * t:b * N + 512 * t + 512], start=True, stop=True)
                    mm.then_inc(done, 1)
                if b:
                    pe.wait_ge(v_evac, 2 * b)
                for t in range(TB):
                    mm = pe.matmul(PS[:, 4 + t // 4, (t % 4) * P:(t % 4 + 1) * P],
                                   xcm[:, b * N + t * P:b * N + (t + 1) * P], wq_bd[:, 2 * C:3 * C],
                                   start=True, stop=True)
                mm.then_inc(v_done, 1)

            pe.wait_ge(v_evac, 2 * B)
            ring = {"base": 0, "phase": 0, "n": 0}

            def ring_slot():
                if not (isinstance(ring["base"], int) and ring["base"] + ring["n"] < 3):
                    pe.wait_ge(ring_used, ring["base"] + ring["n"] - 2)
                ring["n"] += 1
                return ring_bank(ring["phase"] + ring["n"] - 1)

            def max_unit(it, u, i):
                h, qt, half = i // 16, i // 2 % TB, i % 2
                if i == 0:
                    pe.wait_ge(stack_loaded[u], it * LOADS + LOADS)
                bank = ring_slot()
                pe.matmul(PS[:, bank, :], qst[0:ZROWS, u, h, qt * P:(qt + 1) * P],
                          kst[0:ZROWS, u, h, half * 512:half * 512 + 512], start=True, stop=True)\
                  .then_inc(ring_ready, 1)

            def max_turn(it, u):
                pe.wait_ge(maxsplit, (it * NBUF + u) * 5 + 5)
                bank = ring_slot()
                pe.transpose(PS[:, bank, :].bitcast(BF16)[0:ZROWS, 0:P],
                             mparts[:].rearrange("p s r -> p (s r)"), identb[:]).then_inc(ring_ready, 1)

            def score_unit(it, u, kt, i):
                g, h, half = it * NBUF + u, i // 2, i % 2
                if kt == 0 and i == 0:
                    pe.wait_ge(maxrow_loaded[u], it * 16 + 16)
                if not (isinstance(g, int) and g == 0 and kt == 0 and i < 3):
                    pe.wait_ge(exp_done, (g * TB + kt) * (2 * HG) + i - 2)
                pe.matmul(PS[:, score_bank(u, kt, i), :], kst[0:SROWS, u, h, kt * P:(kt + 1) * P],
                          qst[0:SROWS, u, h, 512 * half:512 * half + 512], start=True, stop=True)\
                  .then_inc(st_ready, 1)

            def value_unit(it, u, kt, half):
                g = it * NBUF + u
                if half == 0:
                    pe.wait_ge(exp_done, (g * TB + kt + 1) * (2 * HG))
                    if kt == 0:
                        pe.wait_ge(vaug_ready, g + 1)
                        pe.wait_ge(o_evac, g * 2 + 1)
                for h in range(HG):
                    mm = pe.matmul(PS[32 * h:32 * h + 32, VALUES + half, :], vaug[:, u, kt, h, :],
                                   probs[:, kt % 2, h, 512 * half:512 * half + 512],
                                   start=(kt == 0), stop=(kt == TB - 1))
                mm.then_inc(av_done, 1)

            def out_turn(it, u, half):
                pe.wait_ge(o_evac, (it * NBUF + u) * 2 + half + 1 + 1)
                bank = ring_slot()
                for t in range(4):
                    mm = pe.transpose(PS[:, bank, t * P:(t + 1) * P],
                                      osb[:, 512 * half + t * P:512 * half + (t + 1) * P], ident[:])
                mm.then_inc(ring_ready, 1)

            for i in range(64):
                max_unit(0, 0, i)
            max_turn(0, 0)
            for i in range(32):
                max_unit(0, 1, i)
            for i in range(2 * HG):
                score_unit(0, 0, 0, i)

            def body(it, u, used, phase, nxt, aft):
                ring["base"], ring["phase"], ring["n"] = used, phase, 0
                for kt in range(1, TB + 1):
                    units = []
                    if kt <= 4 and nxt:
                        units = [(*later(it, u, 1), 32 + 8 * (kt - 1) + i) for i in range(8)]
                    if kt > 4 and aft:
                        units = [(*later(it, u, 2), 8 * (kt - 5) + i) for i in range(8)]
                    if kt == 7 and nxt:
                        max_turn(*later(it, u, 1))
                    for i in range(2 * HG):
                        for x in units[i:i + 1]:
                            max_unit(*x)
                        if kt < TB:
                            score_unit(it, u, kt, i)
                        elif nxt:
                            score_unit(*later(it, u, 1), 0, i)
                        if i % HG == HG - 1:
                            value_unit(it, u, kt - 1, i // HG)
                for half in range(2):
                    out_turn(it, u, half)
            attention_bodies(pe, body)

            def prepare(k, b, h):
                n = b * 2 + h
                if k == 0:
                    pe.wait_ge(ost_ready, n + 1)
                    turn4(pe, TURNS, lambda t: ost[:, h, t, :], oT_done)
                if k == 1:
                    pe.wait_ge(ocm_ready, n + 1)
                    wait(pe, acc_ready, n)
                    for t in range(4):
                        mm = pe.matmul(PS[:, PRODUCTS, t * P:(t + 1) * P], ocm[:, h, t * P:(t + 1) * P],
                                       wp_bd[:], start=True, stop=True)
                    mm.then_inc(proj_done, 1)
                if k == 2:
                    pe.wait_ge(x1_ready, n + 1)
                    turn4(pe, TURNS, lambda t: xs[:, h, t, :], x1T_done)
                if k == 3:
                    pe.wait_ge(xc_ready, n + 1)
                    for t in range(4):
                        mm = pe.matmul(PS[:, PRODUCTS, t * NE:(t + 1) * NE], xc[:, h, t * P:(t + 1) * P],
                                       wr[:], start=True, stop=True)
                    mm.then_inc(route_done, 1)
                if k == 4:
                    pe.wait_ge(wts_ready, n + 1)
                    pe.wait_ge(cm_ready, n + 1)
                    for t in range(4):
                        mm = pe.transpose(PS[0:NE, TURNS, t * P:(t + 1) * P], wts[:, h, t, :], ident[:])
                    mm.then_inc(wT_done, 1)
                if k == 5:
                    pe.wait_ge(wT_ready, n + 1)
                    for t in range(4):
                        mm = pe.matmul(PS[:, PRODUCTS, t * P:(t + 1) * P], wT[:, h, t * P:(t + 1) * P],
                                       b2s[:], start=True, stop=True)
                    mm.then_inc(b2_done, 1)
            pe.wait_ge(out_norm, 2 * NG + 1)
            for k in range(STEPS):
                prepare(k, 0, 0)
            pe.nop().then_inc(down_done, 2)
            pe.wait_ge(experts_loaded, 16 * 2 * NE)
            def experts(b, h, after):
                i = b * 2 + h

                def up(e):
                    for t in range(HE):
                        pe.wait_ge(relu_done, (i * NE + e) * HE + t + 1)
                        pe.matmul(PS[:, t, :], w1s[:, e, t * P:(t + 1) * P], x_cm[:, bass.ds(i * 512, 512)],
                                  start=True, stop=True).then_inc(up_done, 1)

                def down(e):
                    m = i * NE + e
                    pe.wait_ge(relu_done, m * HE + 2 * HE)
                    pe.wait_ge(moe_added, m + 1)
                    for t in range(4):
                        for k in range(HE):
                            mm = pe.matmul(PS[:, 4 + e % 2, t * P:(t + 1) * P], hid[:, e % 2, k, t * P:(t + 1) * P],
                                           w2s[:, e, k, :], start=(k == 0), stop=(k == HE - 1))
                    mm.then_inc(down_done, 1)
                up(0)
                for e in range(1, NE):
                    up(e)
                    down(e - 1)
                    if after is not None and e - 1 in STEP_AFTER:
                        prepare(STEP_AFTER[e - 1], *after)
                down(NE - 1)
                if after is not None:
                    prepare(STEP_AFTER[NE - 1], *after)
            wide_tiles(pe, experts)
            pe.wait_ge(mid_loaded, 16 * 7)
            with pe.Fori(0, B) as b:
                for h in range(2):
                    pe.wait_ge(xr_ready, b * 4 + h + 1)
                    turn4(pe, 4 * h, lambda t: xr[:, h, t, :], xrT_done)
                pe.wait_ge(scanned, b + 1)
                for h in range(2):
                    for t in range(4):
                        mm = pe.matmul(PS[:, 4 * h + 1, t * P:(t + 1) * P], y_cm[:, h * 512 + t * P:h * 512 + (t + 1) * P],
                                       ow[:], start=True, stop=True)
                    mm.then_inc(ssm_done, 1)
                for h in range(2):
                    pe.wait_ge(xr_ready, b * 4 + 2 + h + 1)
                    turn4(pe, 4 * h + 2, lambda t: xr[:, h, t, :], xrT2_done)
                pe.wait_ge(xn_ready, b * 2 + 2)
            pe.wait_ge(z_ready, NS + 1)
            pe.nop().then_inc(mlp_done, 1)
            with pe.Fori(0, NS) as i:
                for t in range(H1):
                    pe.wait_ge(gate_done, i * H1 + t + 1)
                    for w, done, bank in ((wg, g_done, 0), (wu, u_done, 2)):
                        pe.matmul(PS[:, bank + t % 2, :], w[:, t * P:(t + 1) * P], x_n[:, bass.ds(i * 512, 512)],
                                  start=True, stop=True).then_inc(done, 1)
                pe.wait_ge(gate_done, i * H1 + H1 + 2)
                wait(pe, z_added, i + 1)
                for t in range(4):
                    for k in range(H1):
                        mm = pe.matmul(PS[:, 4, t * P:(t + 1) * P], hm[:, k, t * P:(t + 1) * P], w3[:, k, :],
                                       start=(k == 0), stop=(k == H1 - 1))
                mm.then_inc(mlp_done, 1)
            pe.wait_ge(late_loaded, 16 * 10)
            def turned_inputs(src, ready, base):
                with pe.Fori(0, B) as b:
                    for h in range(2):
                        pe.wait_ge(ready, base + b * 2 + h + 1)
                        wait(pe, h_ready, base + b * 2 + 1)
                        turn4(pe, 4 * h, lambda t: src[:, h, t, :], xlT_done)
            turned_inputs(xl, xl_ready, 0)
            pe.wait_ge(h_ready, NS + 1)
            for l in range(L2):
                def step(i, r, proj, scores, output):
                    n, u = l * NT + i, r % 2
                    j, m, w = n - 1, n - 2, 1 - u
                    if scores:
                        pe.wait_ge(q_rot, j + 1)
                        wait(pe, pTa_ready, 2 * m)
                        turn4(pe, 5, lambda c: qkr[:, 0, c * P:(c + 1) * P], qT_done)
                        pe.wait_ge(k_rot, j + 1)
                        wait(pe, pTd_ready, 2 * m)
                        turn4(pe, 6, lambda c: qkr[:, 1, c * P:(c + 1) * P], kT_done)
                    if proj:
                        pe.wait_ge(hs_ready, n + 1)
                        for k, (done, free) in enumerate(((qp_done, qpart_ready), (kp_done, kpart_ready),
                                                          (vp_done, v_kept))):
                            wait(pe, free, n)
                            if k == 0:
                                wait(pe, sq_ready, 2 * n)
                            pe.matmul(PS[:, k, :], hs[:, u, :], wl[:, l, k * INNER:(k + 1) * INNER],
                                      start=True, stop=True).then_inc(done, 1)

                    def half_scores(c):
                        pe.wait_ge(qz_ready, j + 1)
                        pe.wait_ge(kwin_ready, j + 1)
                        wait(pe, wexp_done, H2 * j + 4 * c)
                        for h in range(4 * c, 4 * c + 4):
                            to = PS[:, 3 + h % 4 // 2, (h % 2) * 192:(h % 2) * 192 + 192]
                            pe.matmul(to, identb[:], mask[:, (i - 1) % TB, :], start=True, stop=False)
                            mm = pe.matmul(to, qz[:, h // 2, h % 2, :], kwin[:, w, h // 2, 64:256],
                                           start=False, stop=True)
                        mm.then_inc(sc_done, 1)

                    def turn_probs(c):
                        if c == 0:
                            pe.wait_ge(pn_ready, 2 * m + 1)
                            if scores:
                                pe.wait_ge(qz_ready, j + 1)
                        if c == 1 and scores:
                            pe.wait_ge(kwin_ready, j + 1)
                        if c == 2:
                            pe.wait_ge(pn_ready, 2 * m + 2)
                            pe.wait_ge(pTa_ready, 2 * m + 1)
                        if c == 3:
                            pe.wait_ge(pTd_ready, 2 * m + 1)
                        turn4(pe, 5 + c % 2, lambda k: pbuf[:, u, 2 * c + k // 2, (k % 2) * P:(k % 2 + 1) * P], pT_done)

                    def values(c):
                        if c == 0:
                            pe.wait_ge(v_kept, m + 1)
                            wait(pe, xw_ready, m)
                        pe.wait_ge(pTd_ready if c % 2 else pTa_ready, 2 * m + c // 2 + 1)
                        for chunk in range(2):
                            v = vring[:, (r + 1 + chunk) % 4, :]
                            for k in range(2):
                                h = 2 * c + k
                                mm = pe.matmul(PS[64 * k:64 * k + 64, 7, c * P:(c + 1) * P], v[:, h * DH:(h + 1) * DH],
                                               pT[:, c % 2, k, chunk, :], start=(chunk == 0), stop=(chunk == 1))
                        mm.then_inc(pv_done, 1)

                    if output:
                        turn_probs(0)
                        turn_probs(1)
                    if scores:
                        half_scores(0)
                    if output:
                        values(0)
                        turn_probs(2)
                        values(1)
                        turn_probs(3)
                        values(2)
                        values(3)
                    if scores:
                        half_scores(1)
                    if output:
                        pe.wait_ge(oTs_ready, m + 1)
                        for c in range(PAIRS):
                            mm = pe.matmul(PS[:, 7, 0:C], oT[:, c, :], wo[:, l, c, :], start=(c == 0),
                                           stop=(c == PAIRS - 1))
                        mm.then_inc(wo_done, 1)
                tile_steps(pe, step)
                pe.wait_ge(xw_ready, (l + 1) * NT)
                pe.wait_ge(const_ready, 5)

                def shifted(b, h):
                    n, tile0 = l * NS + b * 2 + h, b * TB + h * 4
                    wait(pe, n_ready, n)
                    at_x = bass.ds(tile0, 4)
                    pe.matmul(four(NORMED)[:, :, 0:64], ident[:], x_tm[:, at_x, 0:64], start=True, stop=True)
                    pe.matmul(four(NORMED)[:, :, 64:P], onward[:], x_tm[:, at_x, 64:P], start=True, stop=False)
                    first = 1 - h
                    pe.matmul(four(NORMED)[:, first:4, 64:P], carry[:], x_tm[:, bass.ds(tile0 - h, 4 - first), 64:P],
                              start=False, stop=True).then_inc(moved_done, 1)

                def turned(b, h):
                    pe.wait_ge(xl_ready, (l + 1) * NS + b * 2 + h + 1)
                    turn4(pe, NORMED, lambda t: xl[:, h, t, :], xrT_done)

                def forward(b, h, after):
                    i = b * 2 + h
                    pe.wait_ge(n_ready, l * NS + i + 1)
                    if after is not None:
                        shifted(*after)
                    for t in range(HF):
                        k = l * NS * HF + i * HF + t
                        pe.wait_ge(fgate_done, k + 1)
                        for g, done, bank in ((1, fg_done, t), (0, fa_done, 5 + t)):
                            pe.matmul(PS[:, bank, :], ff1[:, l, g, t * P:(t + 1) * P], n_all[:, bass.ds(i * 512, 512)],
                                      start=True, stop=True).then_inc(done, 1)
                    if after is not None:
                        turned(*after)
                    pe.wait_ge(fgate_done, l * NS * HF + i * HF + 2 * HF)
                    wait(pe, ff_added, l * NS + i + 1)
                    for t in range(4):
                        for k in range(HF):
                            mm = pe.matmul(PS[:, 4, t * P:(t + 1) * P], hf[:, k, t * P:(t + 1) * P], ff2[:, l, k, :],
                                           start=(k == 0), stop=(k == HF - 1))
                    mm.then_inc(ff_done, 1)
                shifted(0, 0)
                turned(0, 0)
                wide_tiles(pe, forward)
                if l + 1 < L2:
                    turned_inputs(yl, yl_ready, (l + 1) * NS)
                    pe.wait_ge(h_ready, (l + 2) * NS + 1)

        @block.vector
        def _(dve):
            for credit in (out_norm, z_ready, z_added, ff_added):
                dve.nop().then_inc(credit, 1)
            ch = Chain(dve, dve_chain, dve_settled)
            for b in range(B):
                for w, evac in enumerate((q_evac, k_evac)):
                    src, to, n = qk32[:, b % 2, w, :], parts[:, b % 2, w, :, :], 8 * b + 4 * w
                    dve.wait_ge(evac, b + 1)
                    if b >= 2:
                        dve.wait_ge(parts_stored[b - 2][w], 16)
                    dve.tensor_copy(to[:, 0, :], src).then_inc(split, 1)
                    dve.wait_ge(split, n + 1)
                    dve.tensor_tensor(res[:], src, to[:, 0, :], ALU.subtract).then_inc(split, 1)
                    dve.wait_ge(split, n + 2)
                    dve.tensor_copy(to[:, 1, :], res[:]).then_inc(split, 1)
                    dve.wait_ge(split, n + 3)
                    dve.tensor_tensor(to[:, 2, :], res[:], to[:, 1, :], ALU.subtract).then_inc(split, 1)

            def fill_v(g, u):
                src = v_all[:, g, :, :].rearrange("p t (h c) -> p t h c", h=HG)
                dve.tensor_scalar(vaug[:, u, :, :, 0:D0], src, 1.0, None, ALU.mult).then_inc(vaug_ready, 1)

            dve.wait_ge(vaug_filled, 1)
            dve.wait_ge(v_evac, 2 * B)
            fill_v(0, 0)
            fill_v(1, 1)

            def unit_max(i, use, bank):
                dve.wait_ge(ring_ready, use + 1)
                dve.tensor_reduce(mx[:, i // 2, i % 2:i % 2 + 1], PS[:, bank, :], AX.X, ALU.max)\
                   .then_inc(ring_used, 1)

            def split_max(it, u, used):
                n = (it * NBUF + u) * 5
                dve.wait_ge(ring_used, used)
                ch.link(dve.tensor_reduce(mneg[:, 0, :], mx[:], AX.X, ALU.max))
                dve.tensor_scalar(mneg[:, 1, :], mneg[:, 0, :], -1.0, None, ALU.mult).then_inc(maxsplit, 1)
                dve.wait_ge(maxsplit, n + 1)
                dve.tensor_copy(mparts[:, 0, :], mneg[:, 1, :]).then_inc(maxsplit, 1)
                dve.wait_ge(maxsplit, n + 2)
                dve.tensor_tensor(mneg[:, 2, :], mneg[:, 1, :], mparts[:, 0, :], ALU.subtract).then_inc(maxsplit, 1)
                dve.wait_ge(maxsplit, n + 3)
                dve.tensor_copy(mparts[:, 1, :], mneg[:, 2, :]).then_inc(maxsplit, 1)
                dve.wait_ge(maxsplit, n + 4)
                dve.tensor_tensor(mparts[:, 2, :], mneg[:, 2, :], mparts[:, 1, :], ALU.subtract).then_inc(maxsplit, 1)

            def keep_turned(it, u, use, bank):
                dve.wait_ge(ring_ready, use + 1)
                if not (isinstance(it, int) and it == 0 and u == 0):
                    dve.wait_ge(max_stored, 16 * (it * NBUF + u))
                dve.tensor_copy(mT[:], PS[:, bank, :].bitcast(BF16)[0:ZROWS, 0:P]).then_inc(ring_used, 1)

            for i in range(64):
                unit_max(i, i, ring_bank(i))
            split_max(0, 0, 64)
            keep_turned(0, 0, 64, ring_bank(64))
            for i in range(32):
                unit_max(i, 65 + i, ring_bank(65 + i))

            def body(it, u, used, phase, nxt, aft):
                g = it * NBUF + u
                if aft:
                    it2, u2 = later(it, u, 2)
                    dve.wait_ge(av_done, g * (2 * TB) + 1)
                    fill_v(it2 * NBUF + u2, u2)
                for n, (what, i) in enumerate(ring_uses(nxt, aft, True)):
                    bank = ring_bank(phase + n)
                    if what in ("next", "after"):
                        unit_max(i, used + n, bank)
                        if what == "next" and i == 63:
                            split_max(*later(it, u, 1), used + 32)
                    elif what == "max":
                        keep_turned(*later(it, u, 1), used + n, bank)
                    elif what == "out":
                        ps = PS[:, bank, :].rearrange("p (t h c) -> p t h c", t=4, h=HG)
                        dve.wait_ge(ring_ready, used + n + 1)
                        ch.link(dve.reciprocal(orec[:, i, :, :, :], ps[:, :, :, D0:D0 + 1]))
                        dve.tensor_tensor(o_all[:, g, i, :, :].rearrange("p t (h c) -> p t h c", h=HG),
                                          ps[:, :, :, 0:D0], orec[:, i, :, :, :].broadcast_to([P, 4, HG, D0]), ALU.mult)\
                           .then_inc(ring_used, 1)
                        dve.nop().then_inc(out_norm, 1)

            def body_chained(it, u, used, phase, nxt, aft):
                if not isinstance(it, int):
                    if u == 0:
                        ch.loop(it, NBUF * 3)
                elif u == NFULL % NBUF and it == NFULL // NBUF:
                    ch.close(NFULL // NBUF)
                body(it, u, used, phase, nxt, aft)
            attention_bodies(dve, body_chained)

            dve.wait_ge(x_loaded, 16)

            def prepare(k, b, h):
                n = b * 2 + h
                if k == 0:
                    src = o_all[:, bass.ds(b * HG, HG), h, :, :].rearrange("p g t c -> p t g c")
                    dve.tensor_scalar(ost[:, h, :, :].rearrange("p t (g c) -> p t g c", g=HG), src, 1.0, None,
                                      ALU.mult).then_inc(ost_ready, 1)
                if k == 1:
                    dve.wait_ge(proj_done, n + 1)
                    ch.link(dve.tensor_tensor(y1[:, h, :, :], four(PRODUCTS), x_tm[:, bass.ds(b * TB + h * 4, 4), :],
                                              ALU.add))
                    ch.link(dve.tensor_tensor(y1[:, h, :, :], y1[:, h, :, :], every4(bp_row[:]), ALU.add))
                    for t in range(4):
                        ins = dve.bn_stats(st6[:, h, t, :], y1[:, h, t, :])
                    ch.link(ins, settle=True)
                    for t in range(4):
                        ins = dve.bn_aggr(mv[:, h, t, :], st6[:, h, t, :])
                    ins.then_inc(var_ready, 1)
                    dve.wait_ge(rstd_ready, n + 1)
                    for t in range(4):
                        ins = dve.tensor_scalar(xs[:, h, t, :], y1[:, h, t, :], mv[:, h, t, 0:1],
                                                rstd[:, h, t:t + 1], ALU.subtract, ALU.mult)
                    ins.then_inc(x1_ready, 1)
                if k == 3:
                    dve.wait_ge(route_done, n + 1)
                    ch.link(dve.tensor_tensor(lg[:, h, :, :], PS[:, PRODUCTS, 0:4 * NE].rearrange("p (t e) -> p t e", t=4),
                                              br_row[:].unsqueeze(1).broadcast_to([P, 4, NE]), ALU.add), settle=True)
                    for t in range(4):
                        ins = dve.max(v8[:, h, t, :], lg[:, h, t, :])
                    ch.link(ins)
                    dve.tensor_tensor(gap[:, h, :], v8[:, h, :, 1], v8[:, h, :, 0], ALU.subtract).then_inc(gap_ready, 1)
                    for t in range(4):
                        ins = dve.max_index(ix8[:, h, t, :], v8[:, h, t, :], lg[:, h, t, :])
                    ch.link(ins)
                    ch.link(dve.tensor_copy(ixf[:, h, :, :], ix8[:, h, :, 0:2]))
                    dve.wait_ge(e2_ready, n + 1)
                    ch.link(dve.tensor_scalar(wpair[:, h, 2, :], e2[:, h, :], 1.0, None, ALU.add))
                    ch.link(dve.reciprocal(wpair[:, h, 0, :], wpair[:, h, 2, :]))
                    ch.link(dve.tensor_tensor(wpair[:, h, 1, :], wpair[:, h, 0, :], e2[:, h, :], ALU.mult))
                    for j in range(2):
                        ins = dve.tensor_tensor(hot[:, h, j, :, :], iota8[:].unsqueeze(1).broadcast_to([P, 4, NE]),
                                                ixf[:, h, :, j:j + 1].broadcast_to([P, 4, NE]), ALU.is_equal)
                    ch.link(ins)
                    for j in range(2):
                        ins = dve.tensor_tensor(hot[:, h, j, :, :], hot[:, h, j, :, :],
                                                wpair[:, h, j, :].unsqueeze(2).broadcast_to([P, 4, NE]), ALU.mult)
                    ch.link(ins)
                    ch.link(dve.tensor_tensor(wts[:, h, :, :], hot[:, h, 0, :, :], hot[:, h, 1, :, :], ALU.add))
                    dve.tensor_copy(w_all[:, bass.ds(b * TB + h * 4, 4), :], wts[:, h, :, :]).then_inc(wts_ready, 1)
                if k == 5:
                    dve.wait_ge(b2_done, n + 1)
                    dve.tensor_tensor(x_tm[:, bass.ds(b * TB + h * 4, 4), :], four(PRODUCTS), xs[:, h, :, :], ALU.add)\
                       .then_inc(acc_ready, 1)
            PREP_LINKS = 3 + 4 + 6
            for k in range(STEPS):
                prepare(k, 0, 0)
            dve.nop().then_inc(moe_added, 2)

            def experts(b, h, after):
                i = b * 2 + h
                dve.wait_ge(acc_ready, i + 1)
                if after is not None:
                    prepare(0, *after)
                for e in range(NE):
                    m = i * NE + e
                    dve.wait_ge(down_done, m + 3)
                    dve.wait_ge(moe_added, m + 2)
                    for t in range(4):
                        x = x_tm[:, i * 4 + t, :]
                        ins = dve.scalar_tensor_tensor(out=x, in0=PS[:, 4 + e % 2, t * P:(t + 1) * P],
                                                       scalar=w_all[:, i * 4 + t, e:e + 1], in1=x,
                                                       op0=ALU.mult, op1=ALU.add)
                    ins.then_inc(moe_added, 1)
                    if after is not None and e and e in STEP_AFTER:
                        prepare(STEP_AFTER[e], *after)
            wide_tiles(dve, experts, ch, PREP_LINKS)
            dve.wait_ge(mid_loaded, 16 * 7)
            dve.wait_ge(tanh_ready, 1)
            with dve.Fori(0, B) as b:
                ch.loop(b, 23)
                for h in range(2):
                    dve.wait_ge(yin_ready, b * 2 + h + 1)
                    norm_stats(dve, ch, yin[:, h, :, :], st6d, mvd, h, var2_ready)
                for h in range(2):
                    dve.wait_ge(rstd2_ready, b * 6 + h + 1)
                    for t in range(4):
                        ins = dve.tensor_scalar(x2[:, h, t, :], yin[:, h, t, :], mvd[:, h, t, 0:1],
                                                rsd[:, h, t:t + 1], ALU.subtract, ALU.mult)
                    ch.link(ins)
                    norm_stats(dve, ch, x2[:, h, :, :], st6d, mvd, h, var2_ready, sqd)
                for h in range(2):
                    dve.wait_ge(rstd2_ready, b * 6 + 2 + h + 1)
                    for t in range(4):
                        ins = dve.tensor_scalar(xr[:, h, t, :], x2[:, h, t, :], rsd[:, h, t:t + 1], None, ALU.mult)
                    ins.then_inc(xr_ready, 1)
                for h in range(2):
                    dve.wait_ge(xrT_done, b * 2 + h + 1)
                    ins = dve.tensor_scalar(u_cm[:, h * 512:h * 512 + 512], PS[:, 4 * h, :], cols1[:, 2:3], cols1[:, 1:2],
                                            ALU.mult, ALU.mult)
                ch.link(ins)
                dve.tensor_tensor_scan(y_cm[:], a_tanh[:].broadcast_to([P, N]), u_cm[:], 0.0, ALU.mult, ALU.add)\
                   .then_inc(scanned, 1)
                for h in range(2):
                    dve.wait_ge(ssm_done, b * 2 + h + 1)
                    ch.link(dve.tensor_tensor(x3[:, h, :, :], four(4 * h + 1), x2[:, h, :, :], ALU.add))
                    ch.link(dve.tensor_tensor(x3[:, h, :, :], x3[:, h, :, :], every4(ob_row[:]), ALU.add))
                    norm_stats(dve, ch, x3[:, h, :, :], st6d, mvd, h, var2_ready, sqd)
                for h in range(2):
                    dve.wait_ge(rstd2_ready, b * 6 + 4 + h + 1)
                    for t in range(4):
                        ins = dve.tensor_scalar(xr[:, h, t, :], x3[:, h, t, :], rsd[:, h, t:t + 1], None, ALU.mult)
                    ins.then_inc(xr_ready, 1)
                for h in range(2):
                    ch.link(dve.tensor_tensor(x2[:, h, :, :], x2[:, h, :, :], x3[:, h, :, :], ALU.add))
                    dve.tensor_tensor(x_tm[:, bass.ds(b * TB + h * 4, 4), :], x2[:, h, :, :], every4(w3b_row[:]), ALU.add)\
                       .then_inc(z_ready, 1)
                for h in range(2):
                    dve.wait_ge(xrT2_done, b * 2 + h + 1)
                    dve.tensor_scalar(x_n[:, bass.ds(b * N + h * 512, 512)], PS[:, 4 * h + 2, :], cols1[:, 3:4], None,
                                      ALU.mult).then_inc(xn_ready, 1)
                dve.wait_ge(z_ready, b * 2 + 2 + 1)
            ch.close(B)
            dve.nop().then_inc(gate_done, 2)
            with dve.Fori(0, NS) as i:
                for t in range(H1):
                    dve.wait_ge(u_done, i * H1 + t + 1)
                    dve.wait_ge(silu_done, i * H1 + t + 1)
                    dve.wait_ge(mlp_done, i + 1)
                    dve.scalar_tensor_tensor(out=hm[:, t, :], in0=PS[:, 2 + t % 2, :], scalar=gu_b[:, 0, t:t + 1],
                                             in1=sg[:, t % 2, :], op0=ALU.add, op1=ALU.mult).then_inc(gate_done, 1)
                dve.wait_ge(mlp_done, i + 2)
                x = x_tm[:, bass.ds(i * 4, 4), :]
                dve.tensor_tensor(x, four(4), x, ALU.add).then_inc(z_added, 1)
            dve.wait_ge(z_added, NS + 1)
            ch.link(dve.memset(h_all[64:P, :, 0:1], 0.0))
            with dve.Fori(0, B) as b:
                ch.loop(b, 2)
                for h in range(2):
                    dve.wait_ge(yl_ready, b * 2 + h + 1)
                    norm_stats(dve, ch, yl[:, h, :, :], st6l, mvl, h, var3_ready)
                for h in range(2):
                    dve.wait_ge(rstd3_ready, b * 2 + h + 1)
                    for t in range(4):
                        ins = dve.tensor_scalar(xl[:, h, t, :], yl[:, h, t, :], mvl[:, h, t, 0:1],
                                                rsl[:, h, t:t + 1], ALU.subtract, ALU.mult)
                    ins.then_inc(xl_ready, 1)
                dve.wait_ge(xl_ready, b * 2 + 2)
                for h in range(2):
                    for to in (x5, x_tm):
                        dve.tensor_scalar(to[:, bass.ds(b * TB + h * 4, 4), :], xl[:, h, :, :], 1.0, None, ALU.mult)\
                           .then_inc(kept, 1)
                dve.wait_ge(kept, b * 4 + 4)
            ch.close(B)
            dve.wait_ge(late_loaded, 16 * 10)
            dve.wait_ge(late_filled, 1)
            for l in range(L2):
                for k in range(2):
                    qs = qks[:, l, k, :]
                    ins = dve.tensor_tensor(rotl[:, 2 * k, :, :], rot[:, 2 * k, :, :],
                                            qs.unsqueeze(1).broadcast_to([P, TB, DH]), ALU.mult)
                    for a, b2 in ((0, 32), (32, 0)):
                        ins = dve.tensor_tensor(rotl[:, 2 * k + 1, :, a:a + 32], rot[:, 2 * k + 1, :, a:a + 32],
                                                qs[:, b2:b2 + 32].unsqueeze(1).broadcast_to([P, TB, 32]), ALU.mult)
                ch.link(ins)

                def step(i, r, proj, scores, output):
                    n, u = l * NT + i, r % 2
                    j, m, w = n - 1, n - 2, 1 - u

                    def parts(k, ready, rotated):
                        dve.wait_ge(sq_ready, 2 * n + k + 1)
                        wait(dve, rotated, n)
                        src = PS[:, k, :].rearrange("p (h c) -> p h c", h=H2)
                        a, b2 = (prod[:, k, x, :].rearrange("p (h c) -> p h c", h=H2) for x in range(2))
                        dve.tensor_tensor(a, src, rotl[:, 2 * k, i % TB, :].unsqueeze(1).broadcast_to([P, H2, DH]),
                                          ALU.mult)
                        for to, of in ((0, 32), (32, 0)):
                            ins = dve.tensor_tensor(b2[:, :, to:to + 32], src[:, :, of:of + 32],
                                                    rotl[:, 2 * k + 1, i % TB, to:to + 32].unsqueeze(1)
                                                    .broadcast_to([P, H2, 32]), ALU.mult)
                        ins.then_inc(ready, 1)

                    def squares(k):
                        dve.tensor_reduce(ssq[:, u, k, :], sqb[:, k, :].rearrange("p (h c) -> p h c", h=H2),
                                          AX.X, ALU.add).then_inc(ssq_ready, 1)

                    def turned_probs(c):
                        dve.wait_ge(pT_done, 4 * m + c + 1)
                        wait(dve, pv_done, 4 * m + c - 1)
                        dve.tensor_copy(pT[:, 1, :, :, :].rearrange("p a b c -> p (a b c)"), PS[:, 6, :])\
                           .then_inc(pTd_ready, 1)

                    def half_max(c):
                        hh = slice(4 * c, 4 * c + 4)
                        dve.wait_ge(sc_done, 2 * j + c + 1)
                        dve.wait_ge(rqk_ready, j + 1)
                        ch.link(dve.tensor_reduce(mx2[:, w, hh], PS[:, 3:5, 0:384].rearrange("p b (h k) -> p b h k", h=2),
                                                  AX.X, ALU.max))
                        dve.scalar_tensor_tensor(out=nb[:, w, hh], in0=mx2[:, w, hh], scalar=-1.0,
                                                 in1=rqk[:, w, 0, hh], op0=ALU.mult, op1=ALU.mult)\
                           .then_inc(max_ready, 1)

                    def half_norm(c, tile, side):
                        hh = slice(4 * c, 4 * c + 4)
                        dve.wait_ge(wexp_done, H2 * tile + 4 * c + 4)
                        ch.link(dve.reciprocal(rrec[:, side, hh], rsum[:, side, hh]))
                        p = pbuf[:, side, hh, 64:256]
                        dve.tensor_tensor(p, p, rrec[:, side, hh].unsqueeze(2).broadcast_to([P, 4, 192]), ALU.mult)\
                           .then_inc(pn_ready, 1)

                    if scores:
                        dve.wait_ge(kT_done, j + 1)
                        wait(dve, sc_done, 2 * j)
                        src = PS[:, 6, :].rearrange("p (c t) -> p c t", c=PAIRS)
                        dve.tensor_copy(kwin[:, w, :, 128:256], src)
                        dve.tensor_copy(kwin[:, u, :, 64:128], src[:, :, 64:128]).then_inc(kwin_ready, 1)
                    if output:
                        half_norm(1, m, u)
                    if proj:
                        parts(0, qpart_ready, q_rot)
                    if output:
                        turned_probs(1)
                    if proj:
                        parts(1, kpart_ready, k_rot)
                    if scores:
                        half_max(0)
                    if proj:
                        squares(1)
                    if output:
                        turned_probs(3)
                    if proj:
                        squares(0)
                    if scores:
                        half_norm(0, j, w)
                        half_max(1)
                    if output:
                        dve.wait_ge(wo_done, m + 1)
                        x = x_tm[:, i - 2, :]
                        dve.tensor_tensor(x, PS[:, 7, 0:C], x, ALU.add).then_inc(xw_ready, 1)
                tile_steps(dve, step, ch, 4)
                dve.wait_ge(xw_ready, (l + 1) * NT)
                vb = (l + 1) * NS

                def normed_stats(b, h):
                    dve.wait_ge(moved_done, l * NS + b * 2 + h + 1)
                    norm_stats(dve, ch, four(NORMED), st6l, mvl, h, var3_ready)

                def normed(b, h):
                    dve.wait_ge(rstd3_ready, vb + b * 2 + h + 1)
                    for t in range(4):
                        ins = dve.tensor_scalar(xl[:, h, t, :], four(NORMED)[:, t, :], mvl[:, h, t, 0:1],
                                                rsl[:, h, t:t + 1], ALU.subtract, ALU.mult)
                    ins.then_inc(xl_ready, 1)

                def normed_turned(b, h):
                    dve.wait_ge(xrT_done, NS + l * NS + b * 2 + h + 1)
                    dve.tensor_scalar(n_all[:, bass.ds(b * N + h * 512, 512)], PS[:, NORMED, :],
                                      lgb[:, 0, l:l + 1], lgb[:, 1, l:l + 1], ALU.mult, ALU.add).then_inc(n_ready, 1)
                if l == 0:
                    dve.nop().then_inc(fgate_done, HF)

                def forward(b, h, after):
                    i = b * 2 + h
                    if after is not None:
                        normed_stats(*after)
                    for t in range(HF):
                        k = l * NS * HF + i * HF + t
                        dve.wait_ge(fa_done, k + 1)
                        dve.wait_ge(gelu_done, k + 1)
                        wait(dve, ff_done, l * NS + i + 1)
                        dve.scalar_tensor_tensor(out=hf[:, t, :], in0=PS[:, 5 + t, :], scalar=ffb1[:, l, 0, t:t + 1],
                                                 in1=sgf[:, t, :], op0=ALU.add, op1=ALU.mult).then_inc(fgate_done, 1)
                        if t == 0 and after is not None:
                            normed(*after)
                    if after is not None:
                        normed_turned(*after)
                    dve.wait_ge(ff_done, l * NS + i + 1 + 1)
                    x = x_tm[:, bass.ds(i * 4, 4), :]
                    ch.link(dve.tensor_tensor(x, four(4), x, ALU.add))
                    dve.tensor_tensor(x, x, every4(ffb2[:, l, :]), ALU.add).then_inc(ff_added, 1)
                normed_stats(0, 0)
                normed(0, 0)
                normed_turned(0, 0)
                wide_tiles(dve, forward, ch, 1 + 1)
            dve.wait_ge(ff_added, L2 * NS + 1)
            with dve.Fori(0, B) as b:
                ch.loop(b, 2 + 2)
                for h in range(2):
                    at_x = bass.ds(b * TB + h * 4, 4)
                    ch.link(dve.tensor_tensor(yl[:, h, :, :], x_tm[:, at_x, :], x5[:, at_x, :], ALU.add))
                    norm_stats(dve, ch, yl[:, h, :, :], st6l, mvl, h, var3_ready)
                for h in range(2):
                    dve.wait_ge(rstd3_ready, (L2 + 1) * NS + b * 2 + h + 1)
                    for t in range(4):
                        ins = dve.tensor_scalar(x_tm[:, b * TB + h * 4 + t, :], yl[:, h, t, :], mvl[:, h, t, 0:1],
                                                rsl[:, h, t:t + 1], ALU.subtract, ALU.mult)
                    ins.then_inc(kept, 1)
                dve.wait_ge(kept, LNS + b * 2 + 2)
            ch.close(B)


def shape_constants():
    q = np.arange(P)[:, None]
    k = np.arange(192)[None, :]
    inside = (k >= q) & (k <= q + WINDOW)
    mask = np.zeros((P, TB, 192), np.float32)
    mask[:] = np.where(inside, 0.0, MASKED)[:, None, :]
    mask[:, 0, :] = np.where(inside & (k >= WINDOW), 0.0, MASKED)
    f = np.float32
    half = np.arange(0, DH, 2, dtype=f)
    inv = (f(1.0) / np.power(f(10000.0), half / f(DH))).astype(f)
    t = np.arange(N, dtype=f)
    ang = t[:, None] * inv[None, :]
    base = (half + f(0.4 * DH)) / f(1.4 * DH)
    power = (t - f(N // 2)) / f(WINDOW // 2)
    scale = np.power(base[None, :], power[:, None]).astype(f)
    cos, sin = np.cos(ang), np.sin(ang)
    rows = [np.concatenate([cos * scale] * 2, 1), np.concatenate([-sin * scale, sin * scale], 1),
            np.concatenate([cos / scale] * 2, 1), np.concatenate([-sin / scale, sin / scale], 1)]
    rot = np.stack(rows).reshape(4, TB, P, DH).transpose(2, 0, 1, 3)
    return mask, np.ascontiguousarray(rot.astype(f)), np.arange(NE, dtype=f)


def build(nc, aps, out):
    d = dict(aps)
    mask, rot, iota = shape_constants()
    d["mask"] = nc.inline_tensor((mask.view(np.uint32) >> 16).astype(np.uint16), name="window_mask")[:].bitcast(BF16)
    d["rot"] = nc.inline_tensor(rot, name="rotation")[:]
    d["iota8"] = nc.inline_tensor(iota, name="expert_numbers")[:]
    network_kernel(nc, d, out)


def layout(i):
    hid = DIMF

    def padded(a, n):
        z = np.zeros(a.shape[:-1] + (n,), a.dtype)
        z[..., :a.shape[-1]] = a
        return z
    a = {}
    x = i["L0_attn_x"].reshape(T, C)
    a["x_tm"] = x.reshape(NT, P, C).transpose(1, 0, 2)
    a["x_cm"] = x.T
    a["w_qkv"], a["w_proj"], a["b_proj"] = i["L0_attn_w_qkv"], i["L0_attn_w_proj"], i["L0_attn_b_proj"]
    a["w_router"], a["b_router"] = i["L0_ffn_W_router"], i["L0_ffn_b_router"]
    a["moe_w1"] = i["L0_ffn_W1"].transpose(1, 0, 2)
    a["moe_b1"] = i["L0_ffn_b1"].reshape(NE * HE, P).T
    a["moe_w2"] = i["L0_ffn_W2"].reshape(NE, HE, P, C).transpose(2, 0, 1, 3)
    a["moe_b2"] = i["L0_ffn_b2"]
    a["cols1"] = np.stack([i["L1_attn_a"], i["L1_attn_b"], i["L1_attn_n1_w"], i["L1_attn_n2_w"]], axis=1)
    a["out_w"], a["out_b"] = i["L1_attn_out_w"].T, i["L1_attn_out_b"]
    a["w1_w"], a["w2_w"] = i["L1_attn_w1_w"].T, i["L1_attn_w2_w"].T
    a["w3_w"] = i["L1_attn_w3_w"].T.reshape(H1, P, C).transpose(1, 0, 2)
    a["w3_b"] = i["L1_attn_w3_b"]
    a["gu_b"] = np.stack([i["L1_attn_w1_b"].reshape(H1, P).T, i["L1_attn_w2_b"].reshape(H1, P).T], axis=1)
    a["wqkv"] = i["L1_ffn_wqkv"].transpose(1, 0, 2)
    a["wo"] = i["L1_ffn_wo"].reshape(L2, PAIRS, P, C).transpose(2, 0, 1, 3)
    a["ff1"] = padded(i["L1_ffn_w1"].transpose(1, 0, 2).reshape(C, L2, 2, hid), HF * P)
    a["ff2"] = padded(i["L1_ffn_w2"].transpose(0, 2, 1), HF * P).reshape(L2, C, HF, P).transpose(3, 0, 2, 1)
    a["ffb1"] = padded(i["L1_ffn_b1"].reshape(L2, 2, hid), HF * P).reshape(L2, 2, HF, P).transpose(3, 0, 1, 2)
    a["ffb2"] = i["L1_ffn_b2"]
    a["lgb"] = np.stack([i["L1_ffn_ln_g"].T, i["L1_ffn_ln_b"].T], axis=1)
    a["qks"] = np.stack([i["L1_ffn_q_scale"], i["L1_ffn_k_scale"]], axis=1)
    return a


def kernel(**inputs):
    import numpy as _np
    import concourse.bacc as _bacc
    from concourse import mybir as _mybir
    from concourse.bass_utils import run_bass_kernel_spmd as _run

    nc = _bacc.Bacc("TRN2", target_bir_lowering=False, num_devices=1)
    arrays, aps = {}, {}
    for name, a in layout({k: _np.asarray(v) for k, v in inputs.items()}).items():
        a = _np.ascontiguousarray(a)
        arrays[f"in_{name}"] = a
        aps[name] = nc.dram_tensor(f"in_{name}", a.shape, _mybir.dt.from_np(a.dtype), kind="ExternalInput").ap()
    out = nc.dram_tensor("out_tokens", [P, NT, C], F32, kind="ExternalOutput").ap()
    build(nc, aps, out)
    r = _run(nc, [arrays], core_ids=[0])
    return r.results[0]["out_tokens"].transpose(1, 0, 2).reshape(B, N, C)
```

```python
from contextlib import ExitStack

import numpy as np

import concourse.bass as bass
from concourse import mybir

ALU = mybir.AluOpType
ACT = mybir.ActivationFunctionType
AX = mybir.AxisListType
F32 = mybir.dt.float32
BF16 = mybir.dt.bfloat16
U32 = mybir.dt.uint32

P = 128
B, N, C = 4, 1024, 128
T = B * N
NT = T // P
NS = T // 512
TB = N // P

H0, D0, G0 = 16, 8, 8
HG = 4
NG = B * H0 // HG
TERMS = 9 * D0
ZROWS = 96
SROWS = ZROWS + 3
NBUF = 3

NE, FE = 8, 512
HE = FE // P

HID1 = 512
H1 = HID1 // P

L2, H2, DH, WINDOW = 2, 8, 64, 64
INNER = H2 * DH
PAIRS = H2 // 2
DIMF = 341
HF = -(-DIMF // P)
QK_SCALE = 8.0
MASKED = -1e30
LNS = 2 * NS

EPS = 1e-5


class Chain:

    def __init__(self, eng, sem, settled):
        self.settled = settled
        self.eng, self.sem, self.base, self.n, self.done = eng, sem, 0, 0, 0

    def loop(self, turn, per):
        self.done += self.n
        self.base, self.n, self.per = self.done + turn * per, 0, per

    def close(self, turns):
        assert self.n == self.per, (self.n, self.per)
        self.done += turns * self.per
        self.base, self.n = self.done, 0

    def link(self, ins, settle=False):
        self.n += 1
        ins.then_inc(self.sem, 1)
        self.eng.wait_ge(self.sem, self.base + self.n)
        if settle:
            self.settle()

    def settle(self):
        self.eng.nop().then_inc(self.settled, 1)


def ring_uses(second, first, outputs):
    uses = []
    if second:
        uses += [("next", 32 + i) for i in range(32)]
    rest = [("after", i) for i in range(32)] if first else []
    if second:
        uses += rest[:16] + [("max", 0)] + rest[16:]
    if outputs:
        uses += [("out", 0), ("out", 1)]
    return uses


def network_kernel(nc, d, out):
    ctx = ExitStack()
    with ctx:
        def sem(name):
            return ctx.enter_context(nc.semaphore(name))

        def sems(names):
            return [sem(name) for name in names.split()]

        def sb(name, shape, dt=F32, at=ctx):
            return at.enter_context(nc.sbuf_tensor(name, shape, dt))

        PS = ctx.enter_context(nc.psum_tensor("PS", [P, 8, 512], F32))

        parts_dram = nc.dram_tensor("parts_dram", [2, 3, B * P, N], BF16, kind="Internal").ap()
        max_dram = nc.dram_tensor("max_dram", [NBUF, 3, HG * N], BF16, kind="Internal").ap()

        x_tm = sb("x_tm", [P, NT, C])
        ident = sb("ident", [P, P])
        identb = sb("identb", [P, P], BF16)
        o_all = sb("o_all", [P, NG, 2, HG, HG * D0])
        neghalf = sb("neghalf", [P, 8])
        wq_bd = sb("wq_bd", [P, 3 * C])
        wp_bd = sb("wp_bd", [P, C])
        bp_row = sb("bp_row", [P, C])
        wr = sb("wr", [P, NE])
        br_row = sb("br_row", [P, NE])
        b2s = sb("b2s", [NE, C])
        iota8 = sb("iota8", [P, NE])
        cols1 = sb("cols1", [P, 4])
        a_tanh = sb("a_tanh", [P, 1])
        onward = sb("onward", [P, P])
        carry = sb("carry", [P, P])
        b1c = sb("b1c", [P, NE * HE])

        at = ExitStack()
        v_all = sb("v_all", [P, NG, TB, HG * D0], at=at)
        vaug = sb("vaug", [P, NBUF, TB, HG, 32], at=at)
        qst = sb("qst", [P, NBUF, HG, N], BF16, at=at)
        kst = sb("kst", [P, NBUF, HG, N], BF16, at=at)
        osb = sb("osb", [P, N], at=at)
        mx = sb("mx", [P, HG * TB, 2], at=at)
        mneg = sb("mneg", [P, 4, HG * TB], at=at)
        mparts = sb("mparts", [P, 3, HG * TB], BF16, at=at)
        mT = sb("mT", [ZROWS, P], BF16, at=at)
        orec = sb("orec", [P, 2, HG, HG, 1], at=at)
        pre = ExitStack()
        xcm = sb("xcm", [P, T], at=pre)
        qk32 = sb("qk32", [P, 2, 2, N], at=pre)
        parts = sb("parts", [P, 2, 2, 3, N], BF16, at=pre)
        res = sb("res", [P, 2, N], at=pre)
        pre.close()
        probs = sb("probs", [P, 2, HG, N], at=at)
        at.close()

        rt = ExitStack()
        x_cm = sb("x_cm", [P, T], at=rt)
        w_all = sb("w_all", [P, NT, NE], at=rt)
        w1s = sb("w1s", [P, NE, FE], at=rt)
        w2s = sb("w2s", [P, NE, HE, C], at=rt)
        hid = sb("hid", [P, 2, HE, 512], at=rt)
        x_n = o_all[:].rearrange("p g a t c -> p (g a t c)")
        ow = sb("ow", [P, C], at=rt)
        ob_row = sb("ob_row", [P, C], at=rt)
        w3b_row = sb("w3b_row", [P, C], at=rt)
        wu = sb("wu", [P, HID1], at=rt)
        wg = sb("wg", [P, HID1], at=rt)
        w3 = sb("w3", [P, H1, C], at=rt)
        gu_b = sb("gu_b", [P, 2, H1], at=rt)
        yin = sb("yin", [P, 2, 4, C], at=rt)
        x2 = sb("x2", [P, 2, 4, C], at=rt)
        x3 = sb("x3", [P, 2, 4, C], at=rt)
        xr = sb("xr", [P, 2, 4, C], at=rt)
        st6d = sb("st6d", [P, 2, 4, 6], at=rt)
        mvd = sb("mvd", [P, 2, 4, 2], at=rt)
        sqd = sb("sqd", [P, 2, 4], at=rt)
        rsd = sb("rsd", [P, 2, 4], at=rt)
        u_cm = sb("u_cm", [P, N], at=rt)
        y_cm = sb("y_cm", [P, N], at=rt)
        sg = sb("sg", [P, 2, 512], at=rt)
        hm = sb("hm", [P, H1, 512], at=rt)
        pj = ExitStack()
        ost = sb("ost", [P, 2, 4, C], at=pj)
        ocm = sb("ocm", [P, 2, 512], at=pj)
        y1 = sb("y1", [P, 2, 4, C], at=pj)
        xs = sb("xs", [P, 2, 4, C], at=pj)
        xc = sb("xc", [P, 2, 512], at=pj)
        st6 = sb("st6", [P, 2, 4, 6], at=pj)
        mv = sb("mv", [P, 2, 4, 2], at=pj)
        rstd = sb("rstd", [P, 2, 4], at=pj)
        lg = sb("lg", [P, 2, 4, NE], at=pj)
        v8 = sb("v8", [P, 2, 4, 8], at=pj)
        ix8 = sb("ix8", [P, 2, 4, 8], U32, at=pj)
        ixf = sb("ixf", [P, 2, 4, 2], at=pj)
        gap = sb("gap", [P, 2, 4], at=pj)
        e2 = sb("e2", [P, 2, 4], at=pj)
        wpair = sb("wpair", [P, 2, 3, 4], at=pj)
        hot = sb("hot", [P, 2, 2, 4, NE], at=pj)
        wts = sb("wts", [P, 2, 4, NE], at=pj)
        wT = sb("wT", [NE, 2, 512], at=pj)
        pj.close()
        rt.close()
        lo = ExitStack()
        x5 = sb("x5", [P, NT, C], at=lo)
        h_all = sb("h_all", [P, B, N + 1], at=lo)
        n_all = o_all[:].rearrange("p g a t c -> p (g a t c)")
        wl = sb("wl", [P, L2, 3 * INNER], at=lo)
        wo = sb("wo", [P, L2, PAIRS, C], at=lo)
        ff1 = sb("ff1", [P, L2, 2, HF * P], at=lo)
        ff2 = sb("ff2", [P, L2, HF, C], at=lo)
        ffb1 = sb("ffb1", [P, L2, 2, HF], at=lo)
        ffb2 = sb("ffb2", [P, L2, C], at=lo)
        lgb = sb("lgb", [P, 2, L2], at=lo)
        mask = sb("mask", [P, TB, 192], BF16, at=lo)
        rot = sb("rot", [P, 4, TB, DH], at=lo)
        rotl = sb("rotl", [P, 4, TB, DH], at=lo)
        qks = sb("qks", [P, L2, 2, DH], at=lo)
        yl = sb("yl", [P, 2, 4, C], at=lo)
        xl = sb("xl", [P, 2, 4, C], at=lo)
        st6l = sb("st6l", [P, 2, 4, 6], at=lo)
        mvl = sb("mvl", [P, 2, 4, 2], at=lo)
        rsl = sb("rsl", [P, 2, 4], at=lo)
        la = ExitStack()
        hs = sb("hs", [P, 2, P], at=la)
        sqb = sb("sqb", [P, 2, INNER], at=la)
        ssq = sb("ssq", [P, 2, 2, H2], at=la)
        rin = sb("rin", [P, 2, H2], at=la)
        rqk = sb("rqk", [P, 2, 2, H2], at=la)
        prod = sb("prod", [P, 2, 2, INNER], at=la)
        ksum = sb("ksum", [P, INNER], at=la)
        qkr = sb("qkr", [P, 2, INNER], at=la)
        vring = sb("vring", [P, 4, INNER], at=la)
        qz = sb("qz", [P, PAIRS, 2, P], at=la)
        kwin = sb("kwin", [P, 2, PAIRS, 256], at=la)
        mx2 = sb("mx2", [P, 2, H2], at=la)
        nb = sb("nb", [P, 2, H2], at=la)
        rsum = sb("rsum", [P, 2, H2], at=la)
        rrec = sb("rrec", [P, 2, H2], at=la)
        pbuf = sb("pbuf", [P, 2, H2, 256], at=la)
        pT = sb("pT", [P, 2, 2, 2, P], at=la)
        oT = sb("oT", [P, PAIRS, P], at=la)
        la.close()
        sgf = sb("sgf", [P, HF, 512], at=lo)
        hf = sb("hf", [P, HF, 512], at=lo)
        lo.close()


        (const_ready, blocks_zeroed, weights_loaded, x_loaded) = \
            sems("const_ready blocks_zeroed weights_loaded x_loaded")
        (wq_loaded, q_done, k_done, v_done, q_evac, k_evac, v_evac, split, split_late) = \
            sems("wq_loaded q_done k_done v_done q_evac k_evac v_evac split split_late")
        (rows_filled, vaug_filled, vaug_ready) = \
            sems("rows_filled vaug_filled vaug_ready")
        (st_ready, exp_done, av_done, o_evac, ring_ready, ring_used, maxsplit, max_stored, out_norm) = \
            sems("st_ready exp_done av_done o_evac ring_ready ring_used maxsplit max_stored out_norm")
        (ost_ready, oT_done, ocm_ready, proj_done, var_ready, rstd_ready, x1_ready, x1T_done) = \
            sems("ost_ready oT_done ocm_ready proj_done var_ready rstd_ready x1_ready x1T_done")
        (xc_ready, route_done, gap_ready, e2_ready, wts_ready, wT_done, wT_ready, b2_done, acc_ready) = \
            sems("xc_ready route_done gap_ready e2_ready wts_ready wT_done wT_ready b2_done acc_ready")
        (cm_ready, experts_loaded, out_stored) = \
            sems("cm_ready experts_loaded out_stored")
        (dve_chain, pool_chain, dve_settled, pool_settled) = \
            sems("dve_chain pool_chain dve_settled pool_settled")
        act_settled = sem("act_settled")
        (up_done, relu_done, down_done, moe_added) = \
            sems("up_done relu_done down_done moe_added")
        (mid_loaded, yin_ready, var2_ready, rstd2_ready, xr_ready, xrT_done, scanned, ssm_done) = \
            sems("mid_loaded yin_ready var2_ready rstd2_ready xr_ready xrT_done scanned ssm_done")
        (xrT2_done, xn_ready, z_ready, tanh_ready) = \
            sems("xrT2_done xn_ready z_ready tanh_ready")
        (g_done, u_done, silu_done, gate_done, mlp_done, z_added) = \
            sems("g_done u_done silu_done gate_done mlp_done z_added")
        (late_loaded, yl_ready, var3_ready, rstd3_ready, xl_ready, xlT_done, h_ready, kept) = \
            sems("late_loaded yl_ready var3_ready rstd3_ready xl_ready xlT_done h_ready kept")
        (late_filled, hs_ready, qp_done, kp_done, vp_done, sq_ready, ssq_ready, rqk_ready) = \
            sems("late_filled hs_ready qp_done kp_done vp_done sq_ready ssq_ready rqk_ready")
        (qpart_ready, kpart_ready, q_rot, k_rot, qT_done, kT_done, qz_ready, kwin_ready) = \
            sems("qpart_ready kpart_ready q_rot k_rot qT_done kT_done qz_ready kwin_ready")
        (v_kept, sc_done, max_ready, wexp_done, pn_ready, pT_done, pTa_ready, pTd_ready) = \
            sems("v_kept sc_done max_ready wexp_done pn_ready pT_done pTa_ready pTd_ready")
        (pv_done, oTs_ready, wo_done, xw_ready) = \
            sems("pv_done oTs_ready wo_done xw_ready")
        (moved_done, n_ready, fg_done, fa_done, gelu_done, fgate_done, ff_done, ff_added) = \
            sems("moved_done n_ready fg_done fa_done gelu_done fgate_done ff_done ff_added")
        stack_loaded = [sem(f"stack_loaded{i}") for i in range(NBUF)]
        xcm_loaded = [sem(f"xcm_loaded{b}") for b in range(B)]
        parts_stored = [[sem(f"parts_stored{b}_{w}") for w in "qk"] for b in range(B)]
        maxrow_loaded = [sem(f"maxrow_loaded{i}") for i in range(NBUF)]
        LOADS = 18 * 16
        PRE_USES = 64 + 1 + 32
        RING, VALUES = 5, 3
        BODY_USES = len(ring_uses(True, True, True))
        NFULL = NG - 4
        WEIGHTS = 16 * (G0 + 7)
        CG = C // G0

        def store_parts(eng, b, w):
            eng.dma_start(parts_dram[w, :, b * P:(b + 1) * P, :].rearrange("s r t -> r s t"),
                          parts[:, b % 2, w, :, :]).then_inc(parts_stored[b][w], 16)

        def split_parts(eng, b, w, rest, done, n):
            src, to = qk32[:, b % 2, w, :], parts[:, b % 2, w, :, :]
            eng.wait_ge(k_evac if w else q_evac, b + 1)
            if b >= 2:
                eng.wait_ge(parts_stored[b - 2][w], 16)
            eng.tensor_copy(to[:, 0, :], src).then_inc(done, 1)
            eng.wait_ge(done, n + 1)
            eng.tensor_tensor(rest, src, to[:, 0, :], ALU.subtract).then_inc(done, 1)
            eng.wait_ge(done, n + 2)
            eng.tensor_copy(to[:, 1, :], rest).then_inc(done, 1)
            eng.wait_ge(done, n + 3)
            eng.tensor_tensor(to[:, 2, :], rest, to[:, 1, :], ALU.subtract).then_inc(done, 1)

        def later(it, u, k):
            return it + (u + k) // NBUF, (u + k) % NBUF

        def ring_base(g):
            n = PRE_USES
            for i in range(g):
                n += len(ring_uses(i + 1 < NG, i + 2 < NG, True))
            return n

        def ring_bank(use):
            return RING + use % 3

        def score_bank(u, kt, i):
            return ((u * TB + kt) * (2 * HG) + i) % 3

        def attention_bodies(eng, body):
            def three(it):
                for u in range(NBUF):
                    used = PRE_USES + u * BODY_USES
                    body(it, u, used + it * (NBUF * BODY_USES), used % 3, True, True)
            with eng.Fori(0, NFULL // NBUF) as it:
                three(it)
            for g in range(NFULL, NG):
                body(g // NBUF, g % NBUF, ring_base(g), ring_base(g) % 3, g + 1 < NG, g + 2 < NG)

        def norm_stats(dve, ch, src, st, mvx, h, ready, square=None):
            for t in range(4):
                ins = dve.bn_stats(st[:, h, t, :], src[:, t, :])
            ch.link(ins, settle=True)
            for t in range(4):
                ins = dve.bn_aggr(mvx[:, h, t, :], st[:, h, t, :])
            if square is not None:
                ch.link(ins)
                ch.link(dve.tensor_tensor(square[:, h, :], mvx[:, h, :, 0], mvx[:, h, :, 0], ALU.mult))
                ins = dve.tensor_tensor(mvx[:, h, :, 1], mvx[:, h, :, 1], square[:, h, :], ALU.add)
            ins.then_inc(ready, 1)

        def rstds(pool, ch, pairs, base, ready, done, mvx, r):
            def pair(i):
                ch.loop(i, 2)
                for h in range(2):
                    pool.wait_ge(ready, base + i * 2 + h + 1)
                    ch.settle()
                    ch.link(pool.tensor_scalar(r[:, h, :], mvx[:, h, :, 1], EPS, None, ALU.add))
                    pool.tensor_tensor(r[:, h, :], r[:, h, :], neghalf[:, 0:4], ALU.pow).then_inc(done, 1)
            with pool.Fori(0, pairs) as i:
                pair(i)
            ch.close(pairs)

        def turn4(pe, bank, src, done):
            for t in range(4):
                mm = pe.transpose(PS[:, bank, t * P:(t + 1) * P], src(t), ident[:])
            mm.then_inc(done, 1)

        def four(bank):
            return PS[:, bank, :].rearrange("p (t c) -> p t c", t=4)

        def every4(row):
            return row.unsqueeze(1).broadcast_to([P, 4, C])

        STEPS, TURNS, PRODUCTS = 6, 6, 7
        STEP_AFTER = {0: 0, 1: 1, 3: 2, 4: 3, 6: 4, 7: 5}

        def expert_tiles(eng, tile, ch=None, per=0):
            def both(b, before, last):
                tile(b, 0, (b, 1), before)
                tile(b, 1, None if last else (b + 1, 0), before)
            both(0, None, False)
            with eng.Fori(0, B - 2) as it:
                if ch is not None:
                    ch.loop(it, per)
                both(it + 1, it, False)
            if ch is not None:
                ch.close(B - 2)
            both(B - 1, B - 2, True)

        def wide_tiles(eng, tile, ch=None, per=0):
            def both(b, last):
                tile(b, 0, (b, 1))
                tile(b, 1, None if last else (b + 1, 0))
            with eng.Fori(0, B - 1) as b:
                if ch is not None:
                    ch.loop(b, 2 * per)
                both(b, False)
            if ch is not None:
                ch.close(B - 1)
            both(B - 1, True)

        NORMED = 3

        def tile_steps(eng, step, ch=None, per=0):
            for i in range(4):
                step(i, i, True, i >= 1, i >= 2)
            with eng.Fori(0, NT // 4 - 2) as it:
                if ch is not None:
                    ch.loop(it, 4 * per)
                for r in range(4):
                    step(it * 4 + (4 + r), r, True, True, True)
            if ch is not None:
                ch.close(NT // 4 - 2)
            for i in range(NT - 4, NT + 2):
                step(i, i % 4, i < NT, i <= NT, True)

        def settle(eng):
            eng.nop().then_inc(act_settled, 1)

        def wait(eng, what, value):
            if not isinstance(value, int) or value > 0:
                eng.wait_ge(what, value)

        block = ctx.enter_context(nc.Block())

        @block.sync
        def _(sp):
            for b in range(B):
                sp.dma_start(xcm[:, b * N:(b + 1) * N], d["x_cm"][:, b * N:(b + 1) * N]).then_inc(xcm_loaded[b], 16)
                if b == 0:
                    sp.wait_ge(blocks_zeroed, 2)
                    for g in range(G0):
                        sp.dma_start(wq_bd[g * CG:(g + 1) * CG, 3 * g * CG:3 * (g + 1) * CG], d["w_qkv"][g])\
                          .then_inc(wq_loaded, 16)
            for w in range(2):
                sp.wait_ge(split, 4 * w + 4)
                store_parts(sp, 0, w)
            for one in parts_stored[0]:
                sp.wait_ge(one, 16)
            sp.wait_ge(rows_filled, 3)

            def load_stack(g, u):
                for i in range(3):
                    for j in range(3):
                        r = (3 * i + j) * D0
                        for dst, w, part in ((qst, 0, i), (kst, 1, j)):
                            src = parts_dram[w, part, bass.ds(g * (HG * D0), HG * D0), :]\
                                .rearrange("(h d) t -> d h t", d=D0)
                            sp.dma_start(dst[r:r + D0, u, :, :], src).then_inc(stack_loaded[u], 16)

            def turn_max(it, u, used):
                sp.wait_ge(ring_used, used)
                sp.dma_start(max_dram[u].rearrange("s (r t) -> (s r) t", t=P), mT[:]).then_inc(max_stored, 16)
                sp.wait_ge(max_stored, 16 * (it * NBUF + u) + 16)
                sp.dma_start(qst[ZROWS:SROWS, u, :, :], max_dram[u].rearrange("s (h t) -> s h t", h=HG))\
                  .then_inc(maxrow_loaded[u], 16)

            load_stack(0, 0)
            load_stack(1, 1)
            for g in range(G0):
                sp.dma_start(wp_bd[g * CG:(g + 1) * CG, g * CG:(g + 1) * CG], d["w_proj"][g])\
                  .then_inc(weights_loaded, 16)
            for dst, src in ((bp_row[:], d["b_proj"].partition_broadcast(P)), (wr[:], d["w_router"]),
                             (br_row[:], d["b_router"].partition_broadcast(P)), (b2s[:], d["moe_b2"]),
                             (b1c[:], d["moe_b1"]), (cols1[:], d["cols1"]),
                             (iota8[:], d["iota8"].partition_broadcast(P))):
                sp.dma_start(dst, src).then_inc(weights_loaded, 16)
            sp.dma_start(x_tm[:], d["x_tm"]).then_inc(x_loaded, 16)
            turn_max(0, 0, 65)
            for stored in parts_stored[1:]:
                for one in stored:
                    sp.wait_ge(one, 16)

            def body(it, u, used, phase, nxt, aft):
                if aft:
                    it2, u2 = later(it, u, 2)
                    sp.wait_ge(st_ready, (it * NBUF + u) * (2 * HG * TB) + 1)
                    load_stack(it2 * NBUF + u2, u2)
                if nxt:
                    it1, u1 = later(it, u, 1)
                    turn_max(it1, u1, used + 32 + 16 * aft + 1)
            attention_bodies(sp, body)

            sp.wait_ge(out_norm, 2 * NG + 1)
            for e in range(NE):
                sp.dma_start(w1s[:, e, :], d["moe_w1"][:, e, :]).then_inc(experts_loaded, 16)
                sp.dma_start(w2s[:, e, :, :], d["moe_w2"][:, e, :, :]).then_inc(experts_loaded, 16)
            for dst, src in ((ow[:], d["out_w"]), (ob_row[:], d["out_b"].partition_broadcast(P)),
                             (w3b_row[:], d["w3_b"].partition_broadcast(P)), (wu[:], d["w1_w"]), (wg[:], d["w2_w"]),
                             (w3[:], d["w3_w"]), (gu_b[:], d["gu_b"])):
                sp.dma_start(dst, src).then_inc(mid_loaded, 16)
            sp.wait_ge(z_added, NS + 1)
            for dst, src in ((wl[:], d["wqkv"]), (wo[:], d["wo"]), (ff1[:], d["ff1"]), (ff2[:], d["ff2"]), (ffb1[:], d["ffb1"]),
                             (ffb2[:], d["ffb2"].partition_broadcast(P)), (lgb[:], d["lgb"]), (mask[:], d["mask"]),
                             (rot[:], d["rot"]), (qks[:], d["qks"].partition_broadcast(P))):
                sp.dma_start(dst, src).then_inc(late_loaded, 16)
            for b in range(B):
                sp.wait_ge(kept, LNS + 2 * b + 2)
                sp.dma_start(out[:, b * TB:(b + 1) * TB, :], x_tm[:, b * TB:(b + 1) * TB, :]).then_inc(out_stored, 16)
            sp.wait_ge(out_stored, 16 * B)

        @block.gpsimd
        def _(pool):
            ch = Chain(pool, pool_chain, pool_settled)
            pool.memset(wq_bd[:], 0.0).then_inc(blocks_zeroed, 1)
            pool.memset(wp_bd[:], 0.0).then_inc(blocks_zeroed, 1)
            for t in (ident, identb):
                ch.link(pool.memset(t[:], 0.0))
                pool.affine_select(out=t[:], in_=t[:], compare_op=ALU.not_equal, fill=1.0, base=0,
                                   pattern=[[-1, P]], channel_multiplier=1).then_inc(const_ready, 1)
            pool.memset(neghalf[:], -0.5).then_inc(const_ready, 1)
            for t, base in ((onward, 1), (carry, 1 - P)):
                ch.link(pool.memset(t[:], 0.0))
                pool.affine_select(out=t[:], in_=t[:], compare_op=ALU.not_equal, fill=1.0, base=base,
                                   pattern=[[-1, P]], channel_multiplier=1).then_inc(const_ready, 1)
            ch.link(pool.memset(vaug[:], 0.0))
            ch.link(pool.memset(vaug[:, :, :, :, D0:D0 + 1], 1.0))
            pool.nop().then_inc(vaug_filled, 1)
            ch.link(pool.memset(qst[64:ZROWS, :, :, :].bitcast(F32), 0.0))
            pool.nop().then_inc(rows_filled, 1)
            ch.link(pool.memset(kst[64:ZROWS, :, :, :].bitcast(F32), 0.0))
            pool.nop().then_inc(rows_filled, 1)
            ch.link(pool.memset(kst[ZROWS:SROWS, :, :, :], 1.0))
            pool.nop().then_inc(rows_filled, 1)
            for b in range(1, B):
                for w in range(2):
                    split_parts(pool, b, w, res[:, 1, :], split_late, 8 * (b - 1) + 4 * w)

            def rstd_of(ready, done, count, mvx, r, h):
                pool.wait_ge(ready, count)
                ch.settle()
                ch.link(pool.tensor_scalar(r[:, h, :], mvx[:, h, :, 1], EPS, None, ALU.add))
                pool.tensor_tensor(r[:, h, :], r[:, h, :], neghalf[:, 0:4], ALU.pow).then_inc(done, 1)

            def ssm_rstds(b, norms):
                for k in norms:
                    for h in range(2):
                        rstd_of(var2_ready, rstd2_ready, b * 6 + 2 * k + h + 1, mvd, rsd, h)

            def beside_experts(b, h, after, before):
                if before is not None and h == 0:
                    ssm_rstds(before, (0, 1))
                if after is not None:
                    rstd_of(var_ready, rstd_ready, after[0] * 2 + after[1] + 1, mv, rstd, after[1])
                if before is not None and h == 0:
                    ssm_rstds(before, (2,))
            rstd_of(var_ready, rstd_ready, 1, mv, rstd, 0)
            expert_tiles(pool, beside_experts, ch, 2 + 6)
            ssm_rstds(B - 1, (0, 1, 2))
            rstds(pool, ch, B, 0, var3_ready, rstd3_ready, mvl, rsl)
            for t in (qz, kwin, pbuf, vring):
                ch.link(pool.memset(t[:], 0.0))
            pool.nop().then_inc(late_filled, 1)
            for l in range(L2):
                def step(i, r, proj, scores, output):
                    n, u = l * NT + i, r % 2
                    if proj:
                        pool.wait_ge(qpart_ready, n + 1)
                        wait(pool, qT_done, n)
                        pool.tensor_tensor(qkr[:, 0, :], prod[:, 0, 0, :], prod[:, 0, 1, :], ALU.add).then_inc(q_rot, 1)
                        pool.wait_ge(kpart_ready, n + 1)
                        ch.link(pool.tensor_tensor(ksum[:], prod[:, 1, 0, :], prod[:, 1, 1, :], ALU.add))
                        pool.wait_ge(ssq_ready, 2 * n + 1)
                        ch.settle()
                        ch.link(pool.tensor_scalar(rin[:, 1, :], ssq[:, u, 1, :], 1e-24, None, ALU.max))
                        ch.link(pool.tensor_tensor(rqk[:, u, 1, :], rin[:, 1, :],
                                                   neghalf[:, 0:1].broadcast_to([P, H2]), ALU.pow))
                        wait(pool, kT_done, n)
                        pool.tensor_tensor(qkr[:, 1, :].rearrange("p (h c) -> p h c", h=H2),
                                           ksum[:].rearrange("p (h c) -> p h c", h=H2),
                                           rqk[:, u, 1, :].unsqueeze(2).broadcast_to([P, H2, DH]), ALU.mult)\
                            .then_inc(k_rot, 1)
                        pool.wait_ge(ssq_ready, 2 * n + 2)
                        ch.settle()
                        ch.link(pool.tensor_scalar(rin[:, 0, :], ssq[:, u, 0, :], 1e-24, 1.0 / QK_SCALE ** 2,
                                                   ALU.max, ALU.mult))
                        wait(pool, wexp_done, (n - 1) * H2)
                        pool.tensor_tensor(rqk[:, u, 0, :], rin[:, 0, :],
                                           neghalf[:, 0:1].broadcast_to([P, H2]), ALU.pow).then_inc(rqk_ready, 1)
                tile_steps(pool, step, ch, 3 + 1)
                rstds(pool, ch, B, (l + 1) * NS, var3_ready, rstd3_ready, mvl, rsl)
            rstds(pool, ch, B, (L2 + 1) * NS, var3_ready, rstd3_ready, mvl, rsl)

        @block.scalar
        def _(act):
            for credit in (o_evac, h_ready):
                act.nop().then_inc(credit, 1)
            def qk_out(b):
                p2 = b % 2
                act.wait_ge(q_done, b + 1)
                if b >= 2:
                    act.wait_ge(split if b == 2 else split_late, 8)
                act.activation(qk32[:, p2, 0, :], PS[:, 0:2, :].rearrange("p a b -> p (a b)"), ACT.Copy,
                               scale=float(D0) ** -0.5).then_inc(q_evac, 1)
                act.wait_ge(k_done, b + 1)
                act.activation(qk32[:, p2, 1, :], PS[:, 2:4, :].rearrange("p a b -> p (a b)"), ACT.Copy)\
                   .then_inc(k_evac, 1)

            def v_out(b):
                act.wait_ge(v_done, b + 1)
                for t in range(2):
                    act.activation(
                        v_all[:, b * HG:(b + 1) * HG, 4 * t:4 * t + 4, :].rearrange("p g t c -> p t g c"),
                        PS[:, 4 + t, :].rearrange("p (t g c) -> p t g c", t=4, g=HG), ACT.Copy)\
                       .then_inc(v_evac, 1)
            for b in range(B - 1):
                qk_out(b)
                v_out(b)
            v_out(B - 1)
            for b in range(1, B):
                for w in range(2):
                    act.wait_ge(split_late, 8 * (b - 1) + 4 * w + 4)
                    store_parts(act, b, w)
                if b == 1:
                    qk_out(B - 1)

            def exps(it, u, kt):
                g = it * NBUF + u
                for i in range(2 * HG):
                    act.wait_ge(st_ready, (g * TB + kt) * (2 * HG) + i + 1)
                    if i == 0 and not (kt < 2 and isinstance(g, int) and g == 0):
                        act.wait_ge(av_done, g * (2 * TB) + 2 * kt - 2 + 1)
                    act.activation(probs[:, kt % 2, i // 2, i % 2 * 512:i % 2 * 512 + 512],
                                   PS[:, score_bank(u, kt, i), :], ACT.Exp).then_inc(exp_done, 1)

            act.wait_ge(split, 8)
            for stored in parts_stored:
                for one in stored:
                    act.wait_ge(one, 16)
            exps(0, 0, 0)

            def body(it, u, used, phase, nxt, aft):
                g = it * NBUF + u
                for kt in range(1, TB):
                    exps(it, u, kt)
                if nxt:
                    exps(*later(it, u, 1), 0)
                act.wait_ge(av_done, g * (2 * TB) + 2 * TB + 1)
                act.wait_ge(out_norm, g * 2 + 1)
                for t in range(2):
                    act.activation(osb[:, 512 * t:512 * t + 512], PS[:, VALUES + t, :], ACT.Copy)\
                       .then_inc(o_evac, 1)
            attention_bodies(act, body)

            def prepare(k, b, h):
                n = b * 2 + h
                if k == 0:
                    act.wait_ge(oT_done, n + 1)
                    act.activation(ocm[:, h, :], PS[:, TURNS, :], ACT.Copy).then_inc(ocm_ready, 1)
                if k == 2:
                    act.wait_ge(x1T_done, n + 1)
                    act.activation(xc[:, h, :], PS[:, TURNS, :], ACT.Copy).then_inc(xc_ready, 1)
                    act.activation(x_cm[:, bass.ds(b * N + h * 512, 512)], PS[:, TURNS, :], ACT.Copy)\
                       .then_inc(cm_ready, 1)
                if k == 3:
                    act.wait_ge(gap_ready, n + 1)
                    act.activation(e2[:, h, :], gap[:, h, :], ACT.Exp).then_inc(e2_ready, 1)
                if k == 4:
                    act.wait_ge(wT_done, n + 1)
                    act.activation(wT[:, h, :], PS[0:NE, TURNS, :], ACT.Copy).then_inc(wT_ready, 1)
            for k in range(STEPS):
                prepare(k, 0, 0)
            act.nop().then_inc(relu_done, HE)
            act.wait_ge(weights_loaded, WEIGHTS)
            act.activation(a_tanh[:], cols1[:, 0:1], ACT.Tanh).then_inc(tanh_ready, 1)

            def ssm_input(b):
                act.wait_ge(moe_added, (b + 1) * (2 * NE) + 2)
                for h in range(2):
                    act.wait_ge(z_ready, b * 2 + 1)
                    settle(act)
                    act.activation(yin[:, h, :, :], x_tm[:, bass.ds(b * TB + h * 4, 4), :], ACT.Copy)\
                       .then_inc(yin_ready, 1)

            def experts(b, h, after, before):
                for e in range(NE):
                    m = (b * 2 + h) * NE + e
                    act.wait_ge(down_done, m + 1)
                    for t in range(HE):
                        act.wait_ge(up_done, m * HE + t + 1)
                        act.activation(hid[:, e % 2, t, :], PS[:, t, :], ACT.Relu,
                                       bias=b1c[:, e * HE + t:e * HE + t + 1]).then_inc(relu_done, 1)
                    if e == 0 and h == 0 and before is not None:
                        ssm_input(before)
                    if after is not None and e - 1 in STEP_AFTER:
                        prepare(STEP_AFTER[e - 1], *after)
                if after is not None:
                    prepare(STEP_AFTER[NE - 1], *after)
            expert_tiles(act, experts)
            ssm_input(B - 1)
            with act.Fori(0, NS) as i:
                for t in range(H1):
                    act.wait_ge(g_done, i * H1 + t + 1)
                    act.wait_ge(gate_done, i * H1 + t + 1)
                    act.activation(sg[:, t % 2, :], PS[:, t % 2, :], ACT.Silu, bias=gu_b[:, 1, t:t + 1])\
                       .then_inc(silu_done, 1)
            act.wait_ge(z_added, NS + 1)
            def to_shifted(b, h, base):
                act.wait_ge(xlT_done, base + b * 2 + h + 1 + 1)
                settle(act)
                act.activation(h_all[0:64, b, h * 512:h * 512 + 512], PS[0:64, 4 * h, :], ACT.Copy)
                act.activation(h_all[64:P, b, h * 512 + 1:h * 512 + 513], PS[64:P, 4 * h, :], ACT.Copy)\
                   .then_inc(h_ready, 1)
            with act.Fori(0, B) as b:
                for h in range(2):
                    to_shifted(b, h, 0)
            act.wait_ge(late_filled, 1)

            def keep_tile(i, u):
                at = (i % TB) * P
                act.activation(hs[:, u, :], h_all[:, i // TB, bass.ds(at, P)], ACT.Copy).then_inc(hs_ready, 1)

            for l in range(L2):
                act.wait_ge(h_ready, (l + 1) * NS + 1)
                def step(i, r, proj, scores, output):
                    n, u = l * NT + i, r % 2
                    if scores:
                        act.wait_ge(qT_done, n)
                        wait(act, sc_done, 2 * (n - 1))
                        for k in range(2):
                            rows = slice(64 * k, 64 * k + 64)
                            ins = act.activation(qz[rows, :, k, :],
                                                 PS[rows, 5, :].rearrange("p (c t) -> p c t", c=PAIRS), ACT.Copy)
                        ins.then_inc(qz_ready, 1)
                    if proj:
                        wait(act, ssq_ready, 2 * n)
                        for k, done in enumerate((qp_done, kp_done)):
                            act.wait_ge(done, n + 1)
                            act.activation(sqb[:, k, :], PS[:, k, :], ACT.Square).then_inc(sq_ready, 1)
                        act.wait_ge(vp_done, n + 1)
                        wait(act, pv_done, 4 * (n - 2))
                        act.activation(vring[:, r, :], PS[:, 2, :], ACT.Copy).then_inc(v_kept, 1)
                        if not (isinstance(i, int) and i == NT - 1):
                            keep_tile(i + 1, 1 - u)
                    if output:
                        for c in (0, 2):
                            act.wait_ge(pT_done, 4 * (n - 2) + c + 1)
                            wait(act, pv_done, 4 * (n - 2) + c - 1)
                            act.activation(pT[:, 0, :, :, :].rearrange("p a b c -> p (a b c)"), PS[:, 5, :], ACT.Copy)\
                               .then_inc(pTa_ready, 1)
                    for c in range(2):
                        if scores:
                            j = n - 1
                            act.wait_ge(max_ready, 2 * j + c + 1)
                            if c == 0:
                                wait(act, pT_done, 4 * (j - 1))
                            for h in range(4 * c, 4 * c + 4):
                                act.activation(pbuf[:, 1 - u, h, 64:256],
                                               PS[:, 3 + h % 4 // 2, (h % 2) * 192:(h % 2) * 192 + 192], ACT.Exp,
                                               bias=nb[:, 1 - u, h:h + 1], scale=rqk[:, 1 - u, 0, h:h + 1],
                                               accum_out=rsum[:, 1 - u, h:h + 1]).then_inc(wexp_done, 1)
                        if output and c == 0:
                            act.wait_ge(pv_done, 4 * (n - 2) + 4)
                            wait(act, wo_done, n - 2)
                            act.activation(oT[:].rearrange("p c t -> p (c t)"), PS[:, 7, :], ACT.Copy)\
                               .then_inc(oTs_ready, 1)
                keep_tile(0, 0)
                tile_steps(act, step)
                with act.Fori(0, NS) as i:
                    for t in range(HF):
                        k = l * NS * HF + i * HF + t
                        act.wait_ge(fg_done, k + 1)
                        act.wait_ge(fgate_done, k + 1)
                        act.activation(sgf[:, t, :], PS[:, t, :], ACT.Gelu,
                                       bias=ffb1[:, l, 1, t:t + 1]).then_inc(gelu_done, 1)
                act.wait_ge(ff_added, (l + 1) * NS + 1)
                fb = (l + 1) * NS
                if l + 1 < L2:
                    with act.Fori(0, B) as b:
                        for h in range(2):
                            act.wait_ge(xlT_done, fb + b * 2 + 1)
                            settle(act)
                            act.activation(yl[:, h, :, :], x_tm[:, bass.ds(b * TB + h * 4, 4), :], ACT.Copy)\
                               .then_inc(yl_ready, 1)
                        for h in range(2):
                            to_shifted(b, h, fb)

        @block.tensor
        def _(pe):
            for credit in (av_done, xlT_done, ff_done):
                pe.nop().then_inc(credit, 1)
            pe.wait_ge(wq_loaded, 16 * G0)
            pe.wait_ge(const_ready, 2)
            for b in range(B):
                pe.wait_ge(xcm_loaded[b], 16)
                for w, (done, evac) in enumerate(((q_done, q_evac), (k_done, k_evac))):
                    if b:
                        pe.wait_ge(evac, b)
                    for t in range(2):
                        mm = pe.matmul(PS[:, 2 * w + t, :], wq_bd[:, w * C:(w + 1) * C],
                                       xcm[:, b * N + 512 * t:b * N + 512 * t + 512], start=True, stop=True)
                    mm.then_inc(done, 1)
                if b:
                    pe.wait_ge(v_evac, 2 * b)
                for t in range(TB):
                    mm = pe.matmul(PS[:, 4 + t // 4, (t % 4) * P:(t % 4 + 1) * P],
                                   xcm[:, b * N + t * P:b * N + (t + 1) * P], wq_bd[:, 2 * C:3 * C],
                                   start=True, stop=True)
                mm.then_inc(v_done, 1)

            pe.wait_ge(v_evac, 2 * B)
            ring = {"base": 0, "phase": 0, "n": 0}

            def ring_slot():
                if not (isinstance(ring["base"], int) and ring["base"] + ring["n"] < 3):
                    pe.wait_ge(ring_used, ring["base"] + ring["n"] - 2)
                ring["n"] += 1
                return ring_bank(ring["phase"] + ring["n"] - 1)

            def max_unit(it, u, i):
                h, qt, half = i // 16, i // 2 % TB, i % 2
                if i == 0:
                    pe.wait_ge(stack_loaded[u], it * LOADS + LOADS)
                bank = ring_slot()
                pe.matmul(PS[:, bank, :], qst[0:ZROWS, u, h, qt * P:(qt + 1) * P],
                          kst[0:ZROWS, u, h, half * 512:half * 512 + 512], start=True, stop=True)\
                  .then_inc(ring_ready, 1)

            def max_turn(it, u):
                pe.wait_ge(maxsplit, (it * NBUF + u) * 5 + 5)
                bank = ring_slot()
                pe.transpose(PS[:, bank, :].bitcast(BF16)[0:ZROWS, 0:P],
                             mparts[:].rearrange("p s r -> p (s r)"), identb[:]).then_inc(ring_ready, 1)

            def score_unit(it, u, kt, i):
                g, h, half = it * NBUF + u, i // 2, i % 2
                if kt == 0 and i == 0:
                    pe.wait_ge(maxrow_loaded[u], it * 16 + 16)
                if not (isinstance(g, int) and g == 0 and kt == 0 and i < 3):
                    pe.wait_ge(exp_done, (g * TB + kt) * (2 * HG) + i - 2)
                pe.matmul(PS[:, score_bank(u, kt, i), :], kst[0:SROWS, u, h, kt * P:(kt + 1) * P],
                          qst[0:SROWS, u, h, 512 * half:512 * half + 512], start=True, stop=True)\
                  .then_inc(st_ready, 1)

            def value_unit(it, u, kt, half):
                g = it * NBUF + u
                if half == 0:
                    pe.wait_ge(exp_done, (g * TB + kt + 1) * (2 * HG))
                    if kt == 0:
                        pe.wait_ge(vaug_ready, g + 1)
                        pe.wait_ge(o_evac, g * 2 + 1)
                for h in range(HG):
                    mm = pe.matmul(PS[32 * h:32 * h + 32, VALUES + half, :], vaug[:, u, kt, h, :],
                                   probs[:, kt % 2, h, 512 * half:512 * half + 512],
                                   start=(kt == 0), stop=(kt == TB - 1))
                mm.then_inc(av_done, 1)

            def out_turn(it, u, half):
                pe.wait_ge(o_evac, (it * NBUF + u) * 2 + half + 1 + 1)
                bank = ring_slot()
                for t in range(4):
                    mm = pe.transpose(PS[:, bank, t * P:(t + 1) * P],
                                      osb[:, 512 * half + t * P:512 * half + (t + 1) * P], ident[:])
                mm.then_inc(ring_ready, 1)

            for i in range(64):
                max_unit(0, 0, i)
            max_turn(0, 0)
            for i in range(32):
                max_unit(0, 1, i)
            pe.wait_ge(q_evac, B)
            pe.wait_ge(k_evac, B)
            for i in range(2 * HG):
                score_unit(0, 0, 0, i)

            def body(it, u, used, phase, nxt, aft):
                ring["base"], ring["phase"], ring["n"] = used, phase, 0
                for kt in range(1, TB + 1):
                    units = []
                    if kt <= 4 and nxt:
                        units = [(*later(it, u, 1), 32 + 8 * (kt - 1) + i) for i in range(8)]
                    if kt > 4 and aft:
                        units = [(*later(it, u, 2), 8 * (kt - 5) + i) for i in range(8)]
                    if kt == 7 and nxt:
                        max_turn(*later(it, u, 1))
                    for i in range(2 * HG):
                        for x in units[i:i + 1]:
                            max_unit(*x)
                        if kt < TB:
                            score_unit(it, u, kt, i)
                        elif nxt:
                            score_unit(*later(it, u, 1), 0, i)
                        if i % HG == HG - 1:
                            value_unit(it, u, kt - 1, i // HG)
                for half in range(2):
                    out_turn(it, u, half)
            attention_bodies(pe, body)

            def prepare(k, b, h):
                n = b * 2 + h
                if k == 0:
                    pe.wait_ge(ost_ready, n + 1)
                    turn4(pe, TURNS, lambda t: ost[:, h, t, :], oT_done)
                if k == 1:
                    pe.wait_ge(ocm_ready, n + 1)
                    wait(pe, acc_ready, n)
                    for t in range(4):
                        mm = pe.matmul(PS[:, PRODUCTS, t * P:(t + 1) * P], ocm[:, h, t * P:(t + 1) * P],
                                       wp_bd[:], start=True, stop=True)
                    mm.then_inc(proj_done, 1)
                if k == 2:
                    pe.wait_ge(x1_ready, n + 1)
                    turn4(pe, TURNS, lambda t: xs[:, h, t, :], x1T_done)
                if k == 3:
                    pe.wait_ge(xc_ready, n + 1)
                    for t in range(4):
                        mm = pe.matmul(PS[:, PRODUCTS, t * NE:(t + 1) * NE], xc[:, h, t * P:(t + 1) * P],
                                       wr[:], start=True, stop=True)
                    mm.then_inc(route_done, 1)
                if k == 4:
                    pe.wait_ge(wts_ready, n + 1)
                    pe.wait_ge(cm_ready, n + 1)
                    for t in range(4):
                        mm = pe.transpose(PS[0:NE, TURNS, t * P:(t + 1) * P], wts[:, h, t, :], ident[:])
                    mm.then_inc(wT_done, 1)
                if k == 5:
                    pe.wait_ge(wT_ready, n + 1)
                    for t in range(4):
                        mm = pe.matmul(PS[:, PRODUCTS, t * P:(t + 1) * P], wT[:, h, t * P:(t + 1) * P],
                                       b2s[:], start=True, stop=True)
                    mm.then_inc(b2_done, 1)
            pe.wait_ge(weights_loaded, WEIGHTS)
            pe.wait_ge(out_norm, 2 * NG + 1)
            for k in range(STEPS):
                prepare(k, 0, 0)
            pe.nop().then_inc(down_done, 2)
            pe.wait_ge(experts_loaded, 16 * 2 * NE)
            pe.wait_ge(mid_loaded, 16 * 7)

            def ssm(k, b):
                for h in range(2):
                    bank = TURNS + h
                    if k == 0:
                        pe.wait_ge(xr_ready, b * 4 + h + 1)
                        turn4(pe, bank, lambda t: xr[:, h, t, :], xrT_done)
                    if k == 1:
                        pe.wait_ge(scanned, b + 1)
                        for t in range(4):
                            mm = pe.matmul(PS[:, bank, t * P:(t + 1) * P],
                                           y_cm[:, h * 512 + t * P:h * 512 + (t + 1) * P], ow[:], start=True, stop=True)
                        mm.then_inc(ssm_done, 1)
                    if k == 2:
                        pe.wait_ge(xr_ready, b * 4 + 2 + h + 1)
                        turn4(pe, bank, lambda t: xr[:, h, t, :], xrT2_done)

            def experts(b, h, after, before):
                i = b * 2 + h

                def between(slot):
                    n = None if after is None else after[0] * 2 + after[1]
                    if before is not None and slot == 2:
                        pe.wait_ge(acc_ready, i + 1)
                        if n is not None:
                            pe.wait_ge(var_ready, n + 1)
                        ssm(0 if h == 0 else 2, before)
                    if before is not None and slot == 5 and h == 0:
                        pe.wait_ge(cm_ready, n + 1)
                        pe.wait_ge(gap_ready, n + 1)
                        ssm(1, before)
                    if after is not None and slot in STEP_AFTER:
                        if before is not None and slot == 3:
                            if h == 0:
                                pe.wait_ge(scanned, before + 1)
                            else:
                                pe.wait_ge(xn_ready, before * 2 + 2)
                        if before is not None and slot == 6 and h == 0:
                            pe.wait_ge(var2_ready, before * 6 + 6)
                        prepare(STEP_AFTER[slot], *after)

                def up(e):
                    for t in range(HE):
                        pe.wait_ge(relu_done, (i * NE + e) * HE + t + 1)
                        pe.matmul(PS[:, t, :], w1s[:, e, t * P:(t + 1) * P], x_cm[:, bass.ds(i * 512, 512)],
                                  start=True, stop=True).then_inc(up_done, 1)

                def down(e):
                    m = i * NE + e
                    pe.wait_ge(relu_done, m * HE + 2 * HE)
                    pe.wait_ge(moe_added, m + 1)
                    for t in range(4):
                        for k in range(HE):
                            mm = pe.matmul(PS[:, 4 + e % 2, t * P:(t + 1) * P], hid[:, e % 2, k, t * P:(t + 1) * P],
                                           w2s[:, e, k, :], start=(k == 0), stop=(k == HE - 1))
                    mm.then_inc(down_done, 1)
                up(0)
                for e in range(1, NE):
                    up(e)
                    down(e - 1)
                    between(e - 1)
                down(NE - 1)
                between(NE - 1)
            expert_tiles(pe, experts)
            for k in range(3):
                ssm(k, B - 1)
            pe.wait_ge(xn_ready, NS)
            pe.wait_ge(z_ready, NS + 1)
            pe.nop().then_inc(mlp_done, 1)

            def gates_up(i, t):
                pe.wait_ge(gate_done, i * H1 + t + 1)
                for w, done, bank in ((wg, g_done, 0), (wu, u_done, 2)):
                    pe.matmul(PS[:, bank + t % 2, :], w[:, t * P:(t + 1) * P], x_n[:, bass.ds(i * 512, 512)],
                              start=True, stop=True).then_inc(done, 1)

            def mlp(b, h, after):
                i = b * 2 + h
                for t in range(1, H1):
                    gates_up(i, t)
                if after is not None:
                    gates_up(after[0] * 2 + after[1], 0)
                pe.wait_ge(gate_done, i * H1 + H1 + 2)
                wait(pe, z_added, i + 1)
                for t in range(4):
                    for k in range(H1):
                        mm = pe.matmul(PS[:, 4, t * P:(t + 1) * P], hm[:, k, t * P:(t + 1) * P], w3[:, k, :],
                                       start=(k == 0), stop=(k == H1 - 1))
                mm.then_inc(mlp_done, 1)
            gates_up(0, 0)
            wide_tiles(pe, mlp)
            def turned_inputs(src, ready, count, base):
                with pe.Fori(0, B) as b:
                    for h in range(2):
                        pe.wait_ge(ready, count + b * 2 + h + 1)
                        wait(pe, h_ready, base + b * 2 + 1)
                        turn4(pe, 4 * h, lambda t: src[:, h, t, :], xlT_done)
            turned_inputs(xl, xl_ready, 0, 0)
            pe.wait_ge(h_ready, NS + 1)
            pe.wait_ge(late_loaded, 16 * 10)
            for l in range(L2):
                def step(i, r, proj, scores, output):
                    n, u = l * NT + i, r % 2
                    j, m, w = n - 1, n - 2, 1 - u
                    if scores:
                        pe.wait_ge(q_rot, j + 1)
                        wait(pe, pTa_ready, 2 * m)
                        turn4(pe, 5, lambda c: qkr[:, 0, c * P:(c + 1) * P], qT_done)
                        pe.wait_ge(k_rot, j + 1)
                        wait(pe, pTd_ready, 2 * m)
                        turn4(pe, 6, lambda c: qkr[:, 1, c * P:(c + 1) * P], kT_done)
                    if proj:
                        pe.wait_ge(hs_ready, n + 1)
                        for k, (done, free) in enumerate(((qp_done, qpart_ready), (kp_done, kpart_ready),
                                                          (vp_done, v_kept))):
                            wait(pe, free, n)
                            if k == 0:
                                wait(pe, sq_ready, 2 * n)
                            pe.matmul(PS[:, k, :], hs[:, u, :], wl[:, l, k * INNER:(k + 1) * INNER],
                                      start=True, stop=True).then_inc(done, 1)

                    def half_scores(c):
                        pe.wait_ge(qz_ready, j + 1)
                        pe.wait_ge(kwin_ready, j + 1)
                        wait(pe, wexp_done, H2 * j + 4 * c)
                        for h in range(4 * c, 4 * c + 4):
                            to = PS[:, 3 + h % 4 // 2, (h % 2) * 192:(h % 2) * 192 + 192]
                            pe.matmul(to, identb[:], mask[:, (i - 1) % TB, :], start=True, stop=False)
                            mm = pe.matmul(to, qz[:, h // 2, h % 2, :], kwin[:, w, h // 2, 64:256],
                                           start=False, stop=True)
                        mm.then_inc(sc_done, 1)

                    def turn_probs(c):
                        if c == 0:
                            pe.wait_ge(pn_ready, 2 * m + 1)
                            if scores:
                                pe.wait_ge(qz_ready, j + 1)
                        if c == 1 and scores:
                            pe.wait_ge(kwin_ready, j + 1)
                        if c == 2:
                            pe.wait_ge(pn_ready, 2 * m + 2)
                            pe.wait_ge(pTa_ready, 2 * m + 1)
                        if c == 3:
                            pe.wait_ge(pTd_ready, 2 * m + 1)
                        turn4(pe, 5 + c % 2, lambda k: pbuf[:, u, 2 * c + k // 2, (k % 2) * P:(k % 2 + 1) * P], pT_done)

                    def values(c):
                        if c == 0:
                            pe.wait_ge(v_kept, m + 1)
                            wait(pe, xw_ready, m)
                        pe.wait_ge(pTd_ready if c % 2 else pTa_ready, 2 * m + c // 2 + 1)
                        for chunk in range(2):
                            v = vring[:, (r + 1 + chunk) % 4, :]
                            for k in range(2):
                                h = 2 * c + k
                                mm = pe.matmul(PS[64 * k:64 * k + 64, 7, c * P:(c + 1) * P], v[:, h * DH:(h + 1) * DH],
                                               pT[:, c % 2, k, chunk, :], start=(chunk == 0), stop=(chunk == 1))
                        mm.then_inc(pv_done, 1)

                    if output:
                        turn_probs(0)
                        turn_probs(1)
                    if scores:
                        half_scores(0)
                    if output:
                        values(0)
                        turn_probs(2)
                        values(1)
                        turn_probs(3)
                        values(2)
                        values(3)
                    if scores:
                        half_scores(1)
                    if output:
                        pe.wait_ge(oTs_ready, m + 1)
                        for c in range(PAIRS):
                            mm = pe.matmul(PS[:, 7, 0:C], oT[:, c, :], wo[:, l, c, :], start=(c == 0),
                                           stop=(c == PAIRS - 1))
                        mm.then_inc(wo_done, 1)
                tile_steps(pe, step)
                pe.wait_ge(xw_ready, (l + 1) * NT)
                pe.wait_ge(const_ready, 5)

                def shifted(b, h):
                    n, tile0 = l * NS + b * 2 + h, b * TB + h * 4
                    wait(pe, n_ready, n)
                    at_x = bass.ds(tile0, 4)
                    pe.matmul(four(NORMED)[:, :, 0:64], ident[:], x_tm[:, at_x, 0:64], start=True, stop=True)
                    pe.matmul(four(NORMED)[:, :, 64:P], onward[:], x_tm[:, at_x, 64:P], start=True, stop=False)
                    first = 1 - h
                    pe.matmul(four(NORMED)[:, first:4, 64:P], carry[:], x_tm[:, bass.ds(tile0 - h, 4 - first), 64:P],
                              start=False, stop=True).then_inc(moved_done, 1)

                def turned(b, h):
                    pe.wait_ge(xl_ready, (l + 1) * NS + b * 2 + h + 1)
                    turn4(pe, NORMED, lambda t: xl[:, h, t, :], xrT_done)

                def forward(b, h, after):
                    i = b * 2 + h
                    pe.wait_ge(n_ready, l * NS + i + 1)
                    if after is not None:
                        shifted(*after)
                    for t in range(HF):
                        k = l * NS * HF + i * HF + t
                        pe.wait_ge(fgate_done, k + 1)
                        for g, done, bank in ((1, fg_done, t), (0, fa_done, 5 + t)):
                            pe.matmul(PS[:, bank, :], ff1[:, l, g, t * P:(t + 1) * P], n_all[:, bass.ds(i * 512, 512)],
                                      start=True, stop=True).then_inc(done, 1)
                    if after is not None:
                        turned(*after)
                    pe.wait_ge(fgate_done, l * NS * HF + i * HF + 2 * HF)
                    wait(pe, ff_added, l * NS + i + 1)
                    for t in range(4):
                        for k in range(HF):
                            mm = pe.matmul(PS[:, 4, t * P:(t + 1) * P], hf[:, k, t * P:(t + 1) * P], ff2[:, l, k, :],
                                           start=(k == 0), stop=(k == HF - 1))
                    mm.then_inc(ff_done, 1)
                shifted(0, 0)
                turned(0, 0)
                wide_tiles(pe, forward)
                if l + 1 < L2:
                    turned_inputs(yl, yl_ready, l * NS, (l + 1) * NS)
                    pe.wait_ge(h_ready, (l + 2) * NS + 1)

        @block.vector
        def _(dve):
            for credit in (out_norm, z_ready, z_added, ff_added):
                dve.nop().then_inc(credit, 1)
            ch = Chain(dve, dve_chain, dve_settled)
            for w in range(2):
                split_parts(dve, 0, w, res[:, 0, :], split, 4 * w)

            def fill_v(g, u):
                src = v_all[:, g, :, :].rearrange("p t (h c) -> p t h c", h=HG)
                dve.tensor_scalar(vaug[:, u, :, :, 0:D0], src, 1.0, None, ALU.mult).then_inc(vaug_ready, 1)

            dve.wait_ge(vaug_filled, 1)
            dve.wait_ge(v_evac, 2)
            fill_v(0, 0)
            fill_v(1, 1)

            def unit_max(i, use, bank):
                dve.wait_ge(ring_ready, use + 1)
                dve.tensor_reduce(mx[:, i // 2, i % 2:i % 2 + 1], PS[:, bank, :], AX.X, ALU.max)\
                   .then_inc(ring_used, 1)

            def split_max(it, u, used):
                n = (it * NBUF + u) * 5
                dve.wait_ge(ring_used, used)
                ch.link(dve.tensor_reduce(mneg[:, 0, :], mx[:], AX.X, ALU.max))
                dve.tensor_scalar(mneg[:, 1, :], mneg[:, 0, :], -1.0, None, ALU.mult).then_inc(maxsplit, 1)
                dve.wait_ge(maxsplit, n + 1)
                dve.tensor_copy(mparts[:, 0, :], mneg[:, 1, :]).then_inc(maxsplit, 1)
                dve.wait_ge(maxsplit, n + 2)
                dve.tensor_tensor(mneg[:, 2, :], mneg[:, 1, :], mparts[:, 0, :], ALU.subtract).then_inc(maxsplit, 1)
                dve.wait_ge(maxsplit, n + 3)
                dve.tensor_copy(mparts[:, 1, :], mneg[:, 2, :]).then_inc(maxsplit, 1)
                dve.wait_ge(maxsplit, n + 4)
                dve.tensor_tensor(mparts[:, 2, :], mneg[:, 2, :], mparts[:, 1, :], ALU.subtract).then_inc(maxsplit, 1)

            def keep_turned(it, u, use, bank):
                dve.wait_ge(ring_ready, use + 1)
                if not (isinstance(it, int) and it == 0 and u == 0):
                    dve.wait_ge(max_stored, 16 * (it * NBUF + u))
                dve.tensor_copy(mT[:], PS[:, bank, :].bitcast(BF16)[0:ZROWS, 0:P]).then_inc(ring_used, 1)

            for i in range(64):
                unit_max(i, i, ring_bank(i))
            split_max(0, 0, 64)
            keep_turned(0, 0, 64, ring_bank(64))
            for i in range(32):
                unit_max(i, 65 + i, ring_bank(65 + i))

            dve.wait_ge(v_evac, 2 * B)

            def body(it, u, used, phase, nxt, aft):
                g = it * NBUF + u
                if aft:
                    it2, u2 = later(it, u, 2)
                    dve.wait_ge(av_done, g * (2 * TB) + 1)
                    fill_v(it2 * NBUF + u2, u2)
                for n, (what, i) in enumerate(ring_uses(nxt, aft, True)):
                    bank = ring_bank(phase + n)
                    if what in ("next", "after"):
                        unit_max(i, used + n, bank)
                        if what == "next" and i == 63:
                            split_max(*later(it, u, 1), used + 32)
                    elif what == "max":
                        keep_turned(*later(it, u, 1), used + n, bank)
                    elif what == "out":
                        ps = PS[:, bank, :].rearrange("p (t h c) -> p t h c", t=4, h=HG)
                        dve.wait_ge(ring_ready, used + n + 1)
                        ch.link(dve.reciprocal(orec[:, i, :, :, :], ps[:, :, :, D0:D0 + 1]))
                        dve.tensor_tensor(o_all[:, g, i, :, :].rearrange("p t (h c) -> p t h c", h=HG),
                                          ps[:, :, :, 0:D0], orec[:, i, :, :, :].broadcast_to([P, 4, HG, D0]), ALU.mult)\
                           .then_inc(ring_used, 1)
                        dve.nop().then_inc(out_norm, 1)

            def body_chained(it, u, used, phase, nxt, aft):
                if not isinstance(it, int):
                    if u == 0:
                        ch.loop(it, NBUF * 3)
                elif u == NFULL % NBUF and it == NFULL // NBUF:
                    ch.close(NFULL // NBUF)
                body(it, u, used, phase, nxt, aft)
            attention_bodies(dve, body_chained)

            dve.wait_ge(x_loaded, 16)

            def prepare(k, b, h):
                n = b * 2 + h
                if k == 0:
                    src = o_all[:, bass.ds(b * HG, HG), h, :, :].rearrange("p g t c -> p t g c")
                    dve.tensor_scalar(ost[:, h, :, :].rearrange("p t (g c) -> p t g c", g=HG), src, 1.0, None,
                                      ALU.mult).then_inc(ost_ready, 1)
                if k == 1:
                    dve.wait_ge(proj_done, n + 1)
                    ch.link(dve.tensor_tensor(y1[:, h, :, :], four(PRODUCTS), x_tm[:, bass.ds(b * TB + h * 4, 4), :],
                                              ALU.add))
                    ch.link(dve.tensor_tensor(y1[:, h, :, :], y1[:, h, :, :], every4(bp_row[:]), ALU.add))
                    for t in range(4):
                        ins = dve.bn_stats(st6[:, h, t, :], y1[:, h, t, :])
                    ch.link(ins, settle=True)
                    for t in range(4):
                        ins = dve.bn_aggr(mv[:, h, t, :], st6[:, h, t, :])
                    ins.then_inc(var_ready, 1)
                    dve.wait_ge(rstd_ready, n + 1)
                    for t in range(4):
                        ins = dve.tensor_scalar(xs[:, h, t, :], y1[:, h, t, :], mv[:, h, t, 0:1],
                                                rstd[:, h, t:t + 1], ALU.subtract, ALU.mult)
                    ins.then_inc(x1_ready, 1)
                if k == 3:
                    dve.wait_ge(route_done, n + 1)
                    ch.link(dve.tensor_tensor(lg[:, h, :, :], PS[:, PRODUCTS, 0:4 * NE].rearrange("p (t e) -> p t e", t=4),
                                              br_row[:].unsqueeze(1).broadcast_to([P, 4, NE]), ALU.add), settle=True)
                    for t in range(4):
                        ins = dve.max(v8[:, h, t, :], lg[:, h, t, :])
                    ch.link(ins)
                    dve.tensor_tensor(gap[:, h, :], v8[:, h, :, 1], v8[:, h, :, 0], ALU.subtract).then_inc(gap_ready, 1)
                    for t in range(4):
                        ins = dve.max_index(ix8[:, h, t, :], v8[:, h, t, :], lg[:, h, t, :])
                    ch.link(ins)
                    ch.link(dve.tensor_copy(ixf[:, h, :, :], ix8[:, h, :, 0:2]))
                    dve.wait_ge(e2_ready, n + 1)
                    ch.link(dve.tensor_scalar(wpair[:, h, 2, :], e2[:, h, :], 1.0, None, ALU.add))
                    ch.link(dve.reciprocal(wpair[:, h, 0, :], wpair[:, h, 2, :]))
                    ch.link(dve.tensor_tensor(wpair[:, h, 1, :], wpair[:, h, 0, :], e2[:, h, :], ALU.mult))
                    for j in range(2):
                        ins = dve.tensor_tensor(hot[:, h, j, :, :], iota8[:].unsqueeze(1).broadcast_to([P, 4, NE]),
                                                ixf[:, h, :, j:j + 1].broadcast_to([P, 4, NE]), ALU.is_equal)
                    ch.link(ins)
                    for j in range(2):
                        ins = dve.tensor_tensor(hot[:, h, j, :, :], hot[:, h, j, :, :],
                                                wpair[:, h, j, :].unsqueeze(2).broadcast_to([P, 4, NE]), ALU.mult)
                    ch.link(ins)
                    ch.link(dve.tensor_tensor(wts[:, h, :, :], hot[:, h, 0, :, :], hot[:, h, 1, :, :], ALU.add))
                    dve.tensor_copy(w_all[:, bass.ds(b * TB + h * 4, 4), :], wts[:, h, :, :]).then_inc(wts_ready, 1)
                if k == 5:
                    dve.wait_ge(b2_done, n + 1)
                    dve.tensor_tensor(x_tm[:, bass.ds(b * TB + h * 4, 4), :], four(PRODUCTS), xs[:, h, :, :], ALU.add)\
                       .then_inc(acc_ready, 1)
            PREP_LINKS = 3 + 4 + 6
            for k in range(STEPS):
                prepare(k, 0, 0)
            dve.nop().then_inc(moe_added, 2)
            dve.wait_ge(mid_loaded, 16 * 7)
            dve.wait_ge(tanh_ready, 1)
            SSM_LINKS = 23

            def ssm(k, b):
                if k == 0:
                    dve.wait_ge(z_ready, b * 2 + 1)
                    for h in range(2):
                        dve.wait_ge(yin_ready, b * 2 + h + 1)
                        norm_stats(dve, ch, yin[:, h, :, :], st6d, mvd, h, var2_ready)
                    for h in range(2):
                        dve.wait_ge(rstd2_ready, b * 6 + h + 1)
                        for t in range(4):
                            ins = dve.tensor_scalar(x2[:, h, t, :], yin[:, h, t, :], mvd[:, h, t, 0:1],
                                                    rsd[:, h, t:t + 1], ALU.subtract, ALU.mult)
                        ch.link(ins)
                        norm_stats(dve, ch, x2[:, h, :, :], st6d, mvd, h, var2_ready, sqd)
                    for h in range(2):
                        dve.wait_ge(rstd2_ready, b * 6 + 2 + h + 1)
                        for t in range(4):
                            ins = dve.tensor_scalar(xr[:, h, t, :], x2[:, h, t, :], rsd[:, h, t:t + 1], None, ALU.mult)
                        ins.then_inc(xr_ready, 1)
                if k == 1:
                    for h in range(2):
                        dve.wait_ge(xrT_done, b * 2 + h + 1)
                        ins = dve.tensor_scalar(u_cm[:, h * 512:h * 512 + 512], PS[:, TURNS + h, :], cols1[:, 2:3], cols1[:, 1:2],
                                                ALU.mult, ALU.mult)
                    ch.link(ins)
                    dve.tensor_tensor_scan(y_cm[:], a_tanh[:].broadcast_to([P, N]), u_cm[:], 0.0, ALU.mult, ALU.add)\
                       .then_inc(scanned, 1)
                if k == 2:
                    for h in range(2):
                        dve.wait_ge(ssm_done, b * 2 + h + 1)
                        ch.link(dve.tensor_tensor(x3[:, h, :, :], four(TURNS + h), x2[:, h, :, :], ALU.add))
                        ch.link(dve.tensor_tensor(x3[:, h, :, :], x3[:, h, :, :], every4(ob_row[:]), ALU.add))
                        norm_stats(dve, ch, x3[:, h, :, :], st6d, mvd, h, var2_ready, sqd)
                    for h in range(2):
                        dve.wait_ge(rstd2_ready, b * 6 + 4 + h + 1)
                        for t in range(4):
                            ins = dve.tensor_scalar(xr[:, h, t, :], x3[:, h, t, :], rsd[:, h, t:t + 1], None, ALU.mult)
                        ins.then_inc(xr_ready, 1)
                    for h in range(2):
                        ch.link(dve.tensor_tensor(x2[:, h, :, :], x2[:, h, :, :], x3[:, h, :, :], ALU.add))
                        dve.tensor_tensor(x_tm[:, bass.ds(b * TB + h * 4, 4), :], x2[:, h, :, :], every4(w3b_row[:]), ALU.add)\
                           .then_inc(z_ready, 1)
                if k == 3:
                    for h in range(2):
                        dve.wait_ge(xrT2_done, b * 2 + h + 1)
                        dve.tensor_scalar(x_n[:, bass.ds(b * N + h * 512, 512)], PS[:, TURNS + h, :], cols1[:, 3:4], None,
                                          ALU.mult).then_inc(xn_ready, 1)

            def experts(b, h, after, before):
                i = b * 2 + h
                dve.wait_ge(acc_ready, i + 1)
                if after is not None:
                    prepare(0, *after)
                if before is not None and h == 0:
                    ssm(0, before)
                for e in range(NE):
                    m = i * NE + e
                    dve.wait_ge(down_done, m + 3)
                    dve.wait_ge(moe_added, m + 2)
                    for t in range(4):
                        x = x_tm[:, i * 4 + t, :]
                        ins = dve.scalar_tensor_tensor(out=x, in0=PS[:, 4 + e % 2, t * P:(t + 1) * P],
                                                       scalar=w_all[:, i * 4 + t, e:e + 1], in1=x,
                                                       op0=ALU.mult, op1=ALU.add)
                    ins.then_inc(moe_added, 1)
                    if before is not None and e in (2, 5):
                        if h == 0:
                            ssm(1 if e == 2 else 2, before)
                        elif e == 2:
                            ssm(3, before)
                    if after is not None and e and e in STEP_AFTER:
                        prepare(STEP_AFTER[e], *after)
            expert_tiles(dve, experts, ch, 2 * PREP_LINKS + SSM_LINKS)
            for k in range(4):
                ssm(k, B - 1)
            dve.nop().then_inc(gate_done, 2)
            with dve.Fori(0, NS) as i:
                for t in range(H1):
                    dve.wait_ge(u_done, i * H1 + t + 1)
                    dve.wait_ge(silu_done, i * H1 + t + 1)
                    dve.wait_ge(mlp_done, i + 1)
                    dve.scalar_tensor_tensor(out=hm[:, t, :], in0=PS[:, 2 + t % 2, :], scalar=gu_b[:, 0, t:t + 1],
                                             in1=sg[:, t % 2, :], op0=ALU.add, op1=ALU.mult).then_inc(gate_done, 1)
                dve.wait_ge(mlp_done, i + 2)
                x = x_tm[:, bass.ds(i * 4, 4), :]
                dve.tensor_tensor(x, four(4), x, ALU.add).then_inc(z_added, 1)
            dve.wait_ge(z_added, NS + 1)
            ch.link(dve.memset(h_all[64:P, :, 0:1], 0.0))

            def input_stats(b, h):
                norm_stats(dve, ch, x_tm[:, bass.ds(b * TB + h * 4, 4), :], st6l, mvl, h, var3_ready)

            def input_norm(b, h, after):
                n, at_x = b * 2 + h, bass.ds(b * TB + h * 4, 4)
                if after is not None:
                    input_stats(*after)
                dve.wait_ge(rstd3_ready, n + 1)
                dve.wait_ge(xlT_done, n + 1)
                for t in range(4):
                    ins = dve.tensor_scalar(xl[:, h, t, :], x_tm[:, b * TB + h * 4 + t, :], mvl[:, h, t, 0:1],
                                            rsl[:, h, t:t + 1], ALU.subtract, ALU.mult)
                ins.then_inc(xl_ready, 1)
                dve.wait_ge(xl_ready, n + 1)
                for to in (x5, x_tm):
                    dve.tensor_scalar(to[:, at_x, :], xl[:, h, :, :], 1.0, None, ALU.mult).then_inc(kept, 1)
                dve.wait_ge(kept, 2 * n + 2)
            input_stats(0, 0)
            wide_tiles(dve, input_norm, ch, 1)
            dve.wait_ge(late_loaded, 16 * 10)
            dve.wait_ge(late_filled, 1)
            for l in range(L2):
                for k in range(2):
                    qs = qks[:, l, k, :]
                    ins = dve.tensor_tensor(rotl[:, 2 * k, :, :], rot[:, 2 * k, :, :],
                                            qs.unsqueeze(1).broadcast_to([P, TB, DH]), ALU.mult)
                    for a, b2 in ((0, 32), (32, 0)):
                        ins = dve.tensor_tensor(rotl[:, 2 * k + 1, :, a:a + 32], rot[:, 2 * k + 1, :, a:a + 32],
                                                qs[:, b2:b2 + 32].unsqueeze(1).broadcast_to([P, TB, 32]), ALU.mult)
                ch.link(ins)

                def step(i, r, proj, scores, output):
                    n, u = l * NT + i, r % 2
                    j, m, w = n - 1, n - 2, 1 - u

                    def parts(k, ready, rotated):
                        dve.wait_ge(sq_ready, 2 * n + k + 1)
                        wait(dve, rotated, n)
                        src = PS[:, k, :].rearrange("p (h c) -> p h c", h=H2)
                        a, b2 = (prod[:, k, x, :].rearrange("p (h c) -> p h c", h=H2) for x in range(2))
                        dve.tensor_tensor(a, src, rotl[:, 2 * k, i % TB, :].unsqueeze(1).broadcast_to([P, H2, DH]),
                                          ALU.mult)
                        for to, of in ((0, 32), (32, 0)):
                            ins = dve.tensor_tensor(b2[:, :, to:to + 32], src[:, :, of:of + 32],
                                                    rotl[:, 2 * k + 1, i % TB, to:to + 32].unsqueeze(1)
                                                    .broadcast_to([P, H2, 32]), ALU.mult)
                        ins.then_inc(ready, 1)

                    def squares(k):
                        dve.tensor_reduce(ssq[:, u, k, :], sqb[:, k, :].rearrange("p (h c) -> p h c", h=H2),
                                          AX.X, ALU.add).then_inc(ssq_ready, 1)

                    def turned_probs(c):
                        dve.wait_ge(pT_done, 4 * m + c + 1)
                        wait(dve, pv_done, 4 * m + c - 1)
                        dve.tensor_copy(pT[:, 1, :, :, :].rearrange("p a b c -> p (a b c)"), PS[:, 6, :])\
                           .then_inc(pTd_ready, 1)

                    def half_max(c):
                        hh = slice(4 * c, 4 * c + 4)
                        dve.wait_ge(sc_done, 2 * j + c + 1)
                        dve.wait_ge(rqk_ready, j + 1)
                        ch.link(dve.tensor_reduce(mx2[:, w, hh], PS[:, 3:5, 0:384].rearrange("p b (h k) -> p b h k", h=2),
                                                  AX.X, ALU.max))
                        dve.scalar_tensor_tensor(out=nb[:, w, hh], in0=mx2[:, w, hh], scalar=-1.0,
                                                 in1=rqk[:, w, 0, hh], op0=ALU.mult, op1=ALU.mult)\
                           .then_inc(max_ready, 1)

                    def half_norm(c, tile, side):
                        hh = slice(4 * c, 4 * c + 4)
                        dve.wait_ge(wexp_done, H2 * tile + 4 * c + 4)
                        ch.link(dve.reciprocal(rrec[:, side, hh], rsum[:, side, hh]))
                        p = pbuf[:, side, hh, 64:256]
                        dve.tensor_tensor(p, p, rrec[:, side, hh].unsqueeze(2).broadcast_to([P, 4, 192]), ALU.mult)\
                           .then_inc(pn_ready, 1)

                    if scores:
                        dve.wait_ge(kT_done, j + 1)
                        wait(dve, sc_done, 2 * j)
                        src = PS[:, 6, :].rearrange("p (c t) -> p c t", c=PAIRS)
                        dve.tensor_copy(kwin[:, w, :, 128:256], src)
                        dve.tensor_copy(kwin[:, u, :, 64:128], src[:, :, 64:128]).then_inc(kwin_ready, 1)
                    if output:
                        half_norm(1, m, u)
                    if proj:
                        parts(0, qpart_ready, q_rot)
                    if output:
                        turned_probs(1)
                    if proj:
                        parts(1, kpart_ready, k_rot)
                    if scores:
                        half_max(0)
                    if proj:
                        squares(1)
                    if output:
                        turned_probs(3)
                    if proj:
                        squares(0)
                    if scores:
                        half_norm(0, j, w)
                        half_max(1)
                    if output:
                        dve.wait_ge(wo_done, m + 1)
                        x = x_tm[:, i - 2, :]
                        dve.tensor_tensor(x, PS[:, 7, 0:C], x, ALU.add).then_inc(xw_ready, 1)
                tile_steps(dve, step, ch, 4)
                dve.wait_ge(xw_ready, (l + 1) * NT)
                vb = (l + 1) * NS

                def normed_stats(b, h):
                    dve.wait_ge(moved_done, l * NS + b * 2 + h + 1)
                    norm_stats(dve, ch, four(NORMED), st6l, mvl, h, var3_ready)

                def normed(b, h):
                    dve.wait_ge(rstd3_ready, vb + b * 2 + h + 1)
                    for t in range(4):
                        ins = dve.tensor_scalar(xl[:, h, t, :], four(NORMED)[:, t, :], mvl[:, h, t, 0:1],
                                                rsl[:, h, t:t + 1], ALU.subtract, ALU.mult)
                    ins.then_inc(xl_ready, 1)

                def normed_turned(b, h):
                    dve.wait_ge(xrT_done, NS + l * NS + b * 2 + h + 1)
                    dve.tensor_scalar(n_all[:, bass.ds(b * N + h * 512, 512)], PS[:, NORMED, :],
                                      lgb[:, 0, l:l + 1], lgb[:, 1, l:l + 1], ALU.mult, ALU.add).then_inc(n_ready, 1)
                if l == 0:
                    dve.nop().then_inc(fgate_done, HF)

                def forward(b, h, after):
                    i = b * 2 + h
                    if after is not None:
                        normed_stats(*after)
                    for t in range(HF):
                        k = l * NS * HF + i * HF + t
                        dve.wait_ge(fa_done, k + 1)
                        dve.wait_ge(gelu_done, k + 1)
                        wait(dve, ff_done, l * NS + i + 1)
                        dve.scalar_tensor_tensor(out=hf[:, t, :], in0=PS[:, 5 + t, :], scalar=ffb1[:, l, 0, t:t + 1],
                                                 in1=sgf[:, t, :], op0=ALU.add, op1=ALU.mult).then_inc(fgate_done, 1)
                        if t == 0 and after is not None:
                            normed(*after)
                    if after is not None:
                        normed_turned(*after)
                    dve.wait_ge(ff_done, l * NS + i + 1 + 1)
                    x = x_tm[:, bass.ds(i * 4, 4), :]
                    ch.link(dve.tensor_tensor(x, four(4), x, ALU.add))
                    dve.tensor_tensor(x, x, every4(ffb2[:, l, :]), ALU.add).then_inc(ff_added, 1)
                normed_stats(0, 0)
                normed(0, 0)
                normed_turned(0, 0)
                wide_tiles(dve, forward, ch, 1 + 1)
            dve.wait_ge(ff_added, L2 * NS + 1)

            def last_stats(b, h):
                at_x = bass.ds(b * TB + h * 4, 4)
                ch.link(dve.tensor_tensor(yl[:, h, :, :], x_tm[:, at_x, :], x5[:, at_x, :], ALU.add))
                norm_stats(dve, ch, yl[:, h, :, :], st6l, mvl, h, var3_ready)

            def last_norm(b, h, after):
                if after is not None:
                    dve.wait_ge(kept, LNS + b * 2 + h)
                    last_stats(*after)
                dve.wait_ge(rstd3_ready, (L2 + 1) * NS + b * 2 + h + 1)
                for t in range(4):
                    ins = dve.tensor_scalar(x_tm[:, b * TB + h * 4 + t, :], yl[:, h, t, :], mvl[:, h, t, 0:1],
                                            rsl[:, h, t:t + 1], ALU.subtract, ALU.mult)
                ins.then_inc(kept, 1)
            last_stats(0, 0)
            wide_tiles(dve, last_norm, ch, 2)


def shape_constants():
    q = np.arange(P)[:, None]
    k = np.arange(192)[None, :]
    inside = (k >= q) & (k <= q + WINDOW)
    mask = np.zeros((P, TB, 192), np.float32)
    mask[:] = np.where(inside, 0.0, MASKED)[:, None, :]
    mask[:, 0, :] = np.where(inside & (k >= WINDOW), 0.0, MASKED)
    f = np.float32
    half = np.arange(0, DH, 2, dtype=f)
    inv = (f(1.0) / np.power(f(10000.0), half / f(DH))).astype(f)
    t = np.arange(N, dtype=f)
    ang = t[:, None] * inv[None, :]
    base = (half + f(0.4 * DH)) / f(1.4 * DH)
    power = (t - f(N // 2)) / f(WINDOW // 2)
    scale = np.power(base[None, :], power[:, None]).astype(f)
    cos, sin = np.cos(ang), np.sin(ang)
    rows = [np.concatenate([cos * scale] * 2, 1), np.concatenate([-sin * scale, sin * scale], 1),
            np.concatenate([cos / scale] * 2, 1), np.concatenate([-sin / scale, sin / scale], 1)]
    rot = np.stack(rows).reshape(4, TB, P, DH).transpose(2, 0, 1, 3)
    return mask, np.ascontiguousarray(rot.astype(f)), np.arange(NE, dtype=f)


def build(nc, aps, out):
    d = dict(aps)
    mask, rot, iota = shape_constants()
    d["mask"] = nc.inline_tensor((mask.view(np.uint32) >> 16).astype(np.uint16), name="window_mask")[:].bitcast(BF16)
    d["rot"] = nc.inline_tensor(rot, name="rotation")[:]
    d["iota8"] = nc.inline_tensor(iota, name="expert_numbers")[:]
    network_kernel(nc, d, out)


def layout(i):
    hid = DIMF

    def padded(a, n):
        z = np.zeros(a.shape[:-1] + (n,), a.dtype)
        z[..., :a.shape[-1]] = a
        return z
    a = {}
    x = i["L0_attn_x"].reshape(T, C)
    a["x_tm"] = x.reshape(NT, P, C).transpose(1, 0, 2)
    a["x_cm"] = x.T
    a["w_qkv"], a["w_proj"], a["b_proj"] = i["L0_attn_w_qkv"], i["L0_attn_w_proj"], i["L0_attn_b_proj"]
    a["w_router"], a["b_router"] = i["L0_ffn_W_router"], i["L0_ffn_b_router"]
    a["moe_w1"] = i["L0_ffn_W1"].transpose(1, 0, 2)
    a["moe_b1"] = i["L0_ffn_b1"].reshape(NE * HE, P).T
    a["moe_w2"] = i["L0_ffn_W2"].reshape(NE, HE, P, C).transpose(2, 0, 1, 3)
    a["moe_b2"] = i["L0_ffn_b2"]
    a["cols1"] = np.stack([i["L1_attn_a"], i["L1_attn_b"], i["L1_attn_n1_w"], i["L1_attn_n2_w"]], axis=1)
    a["out_w"], a["out_b"] = i["L1_attn_out_w"].T, i["L1_attn_out_b"]
    a["w1_w"], a["w2_w"] = i["L1_attn_w1_w"].T, i["L1_attn_w2_w"].T
    a["w3_w"] = i["L1_attn_w3_w"].T.reshape(H1, P, C).transpose(1, 0, 2)
    a["w3_b"] = i["L1_attn_w3_b"]
    a["gu_b"] = np.stack([i["L1_attn_w1_b"].reshape(H1, P).T, i["L1_attn_w2_b"].reshape(H1, P).T], axis=1)
    a["wqkv"] = i["L1_ffn_wqkv"].transpose(1, 0, 2)
    a["wo"] = i["L1_ffn_wo"].reshape(L2, PAIRS, P, C).transpose(2, 0, 1, 3)
    a["ff1"] = padded(i["L1_ffn_w1"].transpose(1, 0, 2).reshape(C, L2, 2, hid), HF * P)
    a["ff2"] = padded(i["L1_ffn_w2"].transpose(0, 2, 1), HF * P).reshape(L2, C, HF, P).transpose(3, 0, 2, 1)
    a["ffb1"] = padded(i["L1_ffn_b1"].reshape(L2, 2, hid), HF * P).reshape(L2, 2, HF, P).transpose(3, 0, 1, 2)
    a["ffb2"] = i["L1_ffn_b2"]
    a["lgb"] = np.stack([i["L1_ffn_ln_g"].T, i["L1_ffn_ln_b"].T], axis=1)
    a["qks"] = np.stack([i["L1_ffn_q_scale"], i["L1_ffn_k_scale"]], axis=1)
    return a


def kernel(**inputs):
    import numpy as _np
    import concourse.bacc as _bacc
    from concourse import mybir as _mybir
    from concourse.bass_utils import run_bass_kernel_spmd as _run

    nc = _bacc.Bacc("TRN2", target_bir_lowering=False, num_devices=1)
    arrays, aps = {}, {}
    for name, a in layout({k: _np.asarray(v) for k, v in inputs.items()}).items():
        a = _np.ascontiguousarray(a)
        arrays[f"in_{name}"] = a
        aps[name] = nc.dram_tensor(f"in_{name}", a.shape, _mybir.dt.from_np(a.dtype), kind="ExternalInput").ap()
    out = nc.dram_tensor("out_tokens", [P, NT, C], F32, kind="ExternalOutput").ap()
    build(nc, aps, out)
    r = _run(nc, [arrays], core_ids=[0])
    return r.results[0]["out_tokens"].transpose(1, 0, 2).reshape(B, N, C)
```
